# Optimizing a Trainium2 kernel written in Bass

```python
import numpy as np
import jax
import jax.numpy as jnp

def _softmax(x, axis=-1):
    return jax.nn.softmax(x, axis=axis)

def _gelu(x):
    return jax.nn.gelu(x, approximate=True)

def _silu(x):
    return jax.nn.silu(x)

def _sigmoid(x):
    return jax.nn.sigmoid(x)

def _layernorm(x, axis=-1, eps=1e-05):
    m = jnp.mean(x, axis=axis, keepdims=True)
    v = jnp.var(x, axis=axis, keepdims=True)
    return (x - m) / jnp.sqrt(v + eps)

def _scatter_add(tgt, idx, src, axis=0):
    return tgt.at[idx].add(src)

def _segment_sum(src, seg, n):
    return jax.ops.segment_sum(src, seg, n)
kernel_name = 'mk_gnn_resnorm_d2_gnn_r32_39159b'

def setup_inputs(seed: int=0):
    np.random.seed(seed)
    _w = jnp.asarray

    def _rec_inputs():
        import jax
        import jax.numpy as jnp
        _gk = jax.random.key(seed)
        x = -0.000202 + 1 * jax.random.normal(jax.random.fold_in(_gk, 1), (50000, 128), jnp.float32)
        src = jax.random.randint(jax.random.fold_in(_gk, 2), (25000,), 0, 50000, jnp.int32)
        dst = jnp.minimum((50000 * jax.random.uniform(jax.random.fold_in(_gk, 3), (25000,)) ** 2.0).astype(jnp.int32), 49999)
        _o = jnp.argsort(dst, stable=True)
        src = src[_o]
        dst = dst[_o]
        edge_weight = jax.random.uniform(jax.random.fold_in(_gk, 12), (25000,), jnp.float32, 0.0, 0.999998)
        return (x, src, dst, edge_weight)
    x, src, dst, edge_weight = _rec_inputs()

    def _L0_gnn_setup():
        import jax, jax.numpy as jnp
        import numpy as np
        N_NODES = 50000
        N_EDGES = 25000
        NODE_DIM = 128
        HIDDEN = 128
        N_LAYERS = 2
        EPS = 1e-05

        def _layer_norm(h, gamma, beta):
            mu = jnp.mean(h, axis=-1, keepdims=True)
            var = jnp.mean(jnp.square(h - mu), axis=-1, keepdims=True)
            return (h - mu) * jax.lax.rsqrt(var + EPS) * gamma + beta
        key = jax.random.key(seed)
        ks = jax.random.split(key, 12)
        s = 0.05
        x = jax.random.normal(ks[0], (N_NODES, NODE_DIM), jnp.float32)
        edge_index = jax.random.randint(ks[1], (2, N_EDGES), 0, N_NODES, dtype=jnp.int64)
        W_enc = jax.random.normal(ks[2], (HIDDEN, NODE_DIM), jnp.float32) * s
        b_enc = jnp.zeros((HIDDEN,), jnp.float32)
        Wm1 = jax.random.normal(ks[3], (N_LAYERS, HIDDEN, 2 * HIDDEN), jnp.float32) * s
        bm1 = jnp.zeros((N_LAYERS, HIDDEN), jnp.float32)
        Wm2 = jax.random.normal(ks[4], (N_LAYERS, HIDDEN, HIDDEN), jnp.float32) * s
        bm2 = jnp.zeros((N_LAYERS, HIDDEN), jnp.float32)
        Wu = jax.random.normal(ks[5], (N_LAYERS, HIDDEN, 2 * HIDDEN), jnp.float32) * s
        bu = jnp.zeros((N_LAYERS, HIDDEN), jnp.float32)
        gamma = jnp.ones((N_LAYERS, HIDDEN), jnp.float32)
        beta = jnp.zeros((N_LAYERS, HIDDEN), jnp.float32)
        W_out = jax.random.normal(ks[6], (HIDDEN, HIDDEN), jnp.float32) * s
        b_out = jnp.zeros((HIDDEN,), jnp.float32)
        return {'x': x, 'edge_index': edge_index, 'W_enc': W_enc, 'b_enc': b_enc, 'Wm1': Wm1, 'bm1': bm1, 'Wm2': Wm2, 'bm2': bm2, 'Wu': Wu, 'bu': bu, 'gamma': gamma, 'beta': beta, 'W_out': W_out, 'b_out': b_out}
    _L0_gnn_all = _L0_gnn_setup()
    _L0_gnn_in = {k: v for k, v in _L0_gnn_all.items() if k in ('W_enc', 'b_enc', 'Wm1', 'bm1', 'Wm2', 'bm2', 'Wu', 'bu', 'gamma', 'beta', 'W_out', 'b_out')}
    del _L0_gnn_all

    def _L1_gnn_setup():
        import jax, jax.numpy as jnp
        import numpy as np
        N = 3125
        E = 31250
        F_IN = 128
        F_OUT = 64
        NHOP = 2

        def _xavier(k, shape, gain=1.414):
            fan_in, fan_out = shape
            std = gain * np.sqrt(2.0 / (fan_in + fan_out))
            return (jax.random.normal(k, shape) * std).astype(jnp.float32)

        def _spmm(row, col, val, v, n):
            return jax.ops.segment_sum(val[:, None] * v[col], row, num_segments=n)

        def _adaptive_enc(y, fc, bf):
            g = jax.nn.sigmoid(y @ fc + bf)
            return jnp.where(y < 0, 0.0, y) + g * jnp.where(y > 0, 0.0, y)
        key = jax.random.key(seed)
        ks = jax.random.split(key, 8)
        x = jax.random.normal(ks[0], (N, F_IN), jnp.float32)
        edge_index = jax.random.randint(ks[1], (2, E), 0, N)
        edge_attr = jax.random.uniform(ks[2], (E,), jnp.float32)
        W0 = _xavier(ks[3], (F_IN, F_OUT))
        W1 = _xavier(ks[4], (F_IN, F_OUT))
        b0 = jnp.zeros((F_OUT,), jnp.float32)
        b1 = jnp.zeros((F_OUT,), jnp.float32)
        fc0 = _xavier(ks[5], (F_OUT, 1))
        fc1 = _xavier(ks[6], (F_OUT, 1))
        bf0 = jnp.zeros((1,), jnp.float32)
        bf1 = jnp.zeros((1,), jnp.float32)
        return dict(x=x, edge_index=edge_index, edge_attr=edge_attr, W0=W0, b0=b0, W1=W1, b1=b1, fc0=fc0, bf0=bf0, fc1=fc1, bf1=bf1)
    _L1_gnn_all = _L1_gnn_setup()
    _L1_gnn_in = {k: v for k, v in _L1_gnn_all.items() if k in ('W0', 'b0', 'W1', 'b1', 'fc0', 'bf0', 'fc1', 'bf1')}
    del _L1_gnn_all
    return {'x': x, 'src': src, 'dst': dst, 'edge_weight': edge_weight, 'L0_gnn_W_enc': _L0_gnn_in['W_enc'], 'L0_gnn_b_enc': _L0_gnn_in['b_enc'], 'L0_gnn_Wm1': _L0_gnn_in['Wm1'], 'L0_gnn_bm1': _L0_gnn_in['bm1'], 'L0_gnn_Wm2': _L0_gnn_in['Wm2'], 'L0_gnn_bm2': _L0_gnn_in['bm2'], 'L0_gnn_Wu': _L0_gnn_in['Wu'], 'L0_gnn_bu': _L0_gnn_in['bu'], 'L0_gnn_gamma': _L0_gnn_in['gamma'], 'L0_gnn_beta': _L0_gnn_in['beta'], 'L0_gnn_W_out': _L0_gnn_in['W_out'], 'L0_gnn_b_out': _L0_gnn_in['b_out'], 'L1_gnn_W0': _L1_gnn_in['W0'], 'L1_gnn_b0': _L1_gnn_in['b0'], 'L1_gnn_W1': _L1_gnn_in['W1'], 'L1_gnn_b1': _L1_gnn_in['b1'], 'L1_gnn_fc0': _L1_gnn_in['fc0'], 'L1_gnn_bf0': _L1_gnn_in['bf0'], 'L1_gnn_fc1': _L1_gnn_in['fc1'], 'L1_gnn_bf1': _L1_gnn_in['bf1']}

def reference(x, src, dst, edge_weight, L0_gnn_W_enc, L0_gnn_b_enc, L0_gnn_Wm1, L0_gnn_bm1, L0_gnn_Wm2, L0_gnn_bm2, L0_gnn_Wu, L0_gnn_bu, L0_gnn_gamma, L0_gnn_beta, L0_gnn_W_out, L0_gnn_b_out, L1_gnn_W0, L1_gnn_b0, L1_gnn_W1, L1_gnn_b1, L1_gnn_fc0, L1_gnn_bf0, L1_gnn_fc1, L1_gnn_bf1):
    import jax
    import jax.numpy as jnp

    def _L0_gnn_ref(x, edge_index, W_enc, b_enc, Wm1, bm1, Wm2, bm2, Wu, bu, gamma, beta, W_out, b_out):
        import jax, jax.numpy as jnp
        import numpy as np
        N_NODES = 50000
        N_EDGES = 25000
        NODE_DIM = 128
        HIDDEN = 128
        N_LAYERS = 2
        EPS = 1e-05

        def _layer_norm(h, gamma, beta):
            mu = jnp.mean(h, axis=-1, keepdims=True)
            var = jnp.mean(jnp.square(h - mu), axis=-1, keepdims=True)
            return (h - mu) * jax.lax.rsqrt(var + EPS) * gamma + beta
        row, col = (edge_index[0], edge_index[1])
        h = x @ W_enc.T + b_enc
        for l in range(N_LAYERS):
            m = jnp.concatenate([h[row], h[col]], axis=-1)
            m = jax.nn.relu(m @ Wm1[l].T + bm1[l])
            m = m @ Wm2[l].T + bm2[l]
            agg = jax.ops.segment_sum(m, col, num_segments=N_NODES)
            upd = jnp.concatenate([h, agg], axis=-1) @ Wu[l].T + bu[l]
            h = _layer_norm(h + upd, gamma[l], beta[l])
        return h @ W_out.T + b_out

    def _L1_gnn_ref(x, edge_index, edge_attr, W0, b0, W1, b1, fc0, bf0, fc1, bf1):
        import jax, jax.numpy as jnp
        import numpy as np
        N = 3125
        E = 31250
        F_IN = 128
        F_OUT = 64
        NHOP = 2

        def _xavier(k, shape, gain=1.414):
            fan_in, fan_out = shape
            std = gain * np.sqrt(2.0 / (fan_in + fan_out))
            return (jax.random.normal(k, shape) * std).astype(jnp.float32)

        def _spmm(row, col, val, v, n):
            return jax.ops.segment_sum(val[:, None] * v[col], row, num_segments=n)

        def _adaptive_enc(y, fc, bf):
            g = jax.nn.sigmoid(y @ fc + bf)
            return jnp.where(y < 0, 0.0, y) + g * jnp.where(y > 0, 0.0, y)
        n = x.shape[0]
        row, col = (edge_index[0], edge_index[1])
        ones = jnp.ones((n, 1), x.dtype)
        params = [(W0, b0, fc0, bf0), (W1, b1, fc1, bf1)]
        outs = []
        for hop in range(NHOP):
            W, b, fc, bf = params[hop]
            h = x @ W
            agg, deg = (h, ones)
            for _ in range(hop + 1):
                agg = _spmm(row, col, edge_attr, agg, n)
                deg = _spmm(row, col, edge_attr, deg, n)
            safe_deg = jnp.where(deg > 0, deg, 1.0)
            y = jnp.where(deg > 0, agg / safe_deg, 0.0)
            y = y + b
            outs.append(_adaptive_enc(y, fc, bf))
        return jnp.concatenate(outs, axis=1)
    edge_index = jnp.stack([src, dst])
    x = _layernorm(x + _L0_gnn_ref(x, edge_index, L0_gnn_W_enc, L0_gnn_b_enc, L0_gnn_Wm1, L0_gnn_bm1, L0_gnn_Wm2, L0_gnn_bm2, L0_gnn_Wu, L0_gnn_bu, L0_gnn_gamma, L0_gnn_beta, L0_gnn_W_out, L0_gnn_b_out), axis=-1)
    x = _layernorm(x + _L1_gnn_ref(x, edge_index, edge_weight, L1_gnn_W0, L1_gnn_b0, L1_gnn_W1, L1_gnn_b1, L1_gnn_fc0, L1_gnn_bf0, L1_gnn_fc1, L1_gnn_bf1), axis=-1)
    return x

_drawn_inputs = setup_inputs


def setup_inputs(seed=0):
    import zlib

    import numpy as np

    out = dict(_drawn_inputs(seed))
    spreads = {'L0_gnn_b_enc': (0.0, 0.1),
     'L0_gnn_bm1': (0.0, 0.37),
     'L0_gnn_bm2': (0.0, 0.1),
     'L0_gnn_bu': (0.0, 0.1),
     'L0_gnn_gamma': (1.0, 0.2),
     'L0_gnn_beta': (0.0, 0.1),
     'L0_gnn_b_out': (0.0, 0.1),
     'L1_gnn_b0': (0.0, 0.1),
     'L1_gnn_b1': (0.0, 0.1)}
    factors = {}
    for name, (base, spread) in spreads.items():
        noise = np.random.default_rng([zlib.crc32(name.encode()), seed]).standard_normal(out[name].shape)
        drawn = base * np.exp(spread * noise) if base else spread * noise
        out[name] = jnp.asarray(drawn.astype(out[name].dtype))
    for name, factor in factors.items():
        out[name] = (out[name] * factor).astype(out[name].dtype)
    return out
```

```python
from contextlib import ExitStack

import concourse.bass as bass
from concourse import mybir

F32 = mybir.dt.float32
BF16 = mybir.dt.bfloat16
I32 = mybir.dt.int32
ALU = mybir.AluOpType
ACT = mybir.ActivationFunctionType
AX = mybir.AxisListType



P = 128
D = 128
W = D + 1
EPS = 1e-5
BATCH = 7
SKIP = 1 << 17
DIGIT = 256
QUAD = 4
CHUNK = 8


def graph_kernel(nc, x, src, dst, edge_weight, W_enc, b_enc, Wm1, bm1, Wm2, bm2, Wu, bu, gamma, beta,
                 W_out, b_out, W0, b0, W1, b1, fc0, bf0, fc1, bf1, out):
    N = x.shape[0]
    E = src.shape[0]
    T = -(-E // (P * 2 * BATCH)) * 2 * BATCH
    IT = T // (2 * BATCH)
    FULL = E // T
    REST = E - FULL * T
    HEAD = N + 1
    TAIL = HEAD + P
    ZROWS = 33
    TR = -(-(TAIL + P) // (P * ZROWS)) * P * ZROWS
    ROWS = CHUNK * P
    CHUNKS = -(-N // ROWS)
    LAST = N - ROWS
    PAIRS = (CHUNKS - 1) // 2
    assert CHUNKS == 2 * PAIRS + 1 and T < DIGIT and N < DIGIT * DIGIT

    with ExitStack() as ctx:
        def sb(name, shape, dt=F32):
            return ctx.enter_context(nc.sbuf_tensor(name, shape, dt))

        def sem(name):
            return ctx.enter_context(nc.semaphore(name))

        def dram(name, shape):
            return nc.dram_tensor(name, shape, F32, kind="Internal").ap()

        msg_sum = dram("msg_sum", [TR, W])
        hop1 = dram("hop1", [TR, W])
        hop2 = dram("hop2", [TR, W])
        n1_table = dram("n1_table", [N, D])
        x1_table = dram("x1_table", [N, D])
        by_low = dram("by_low", [P * T, 4])
        by_src = dram("by_src", [P * T, 4])

        ident = sb("ident", [P, P])
        ones = sb("ones", [P, P])
        before = sb("before", [P, P])
        upto = sb("upto", [P, P])
        ident_b = sb("ident_b", [P, P], BF16)
        ones_b = sb("ones_b", [P, P], BF16)
        before_b = sb("before_b", [P, P], BF16)
        notbefore_b = sb("notbefore_b", [P, P], BF16)
        digits_i = sb("digits_i", [P, DIGIT], I32)
        digits_b = sb("digits_b", [P, DIGIT], BF16)
        part_i = sb("part_i", [P, 1], I32)
        head_row = sb("head_row", [P, 1])
        tail_row = sb("tail_row", [P, 1])
        eps = sb("eps", [P, 1])
        zeros = sb("zeros", [P, ZROWS * W])

        nat = sb("nat", [P, 12, D])
        wT = sb("wT", [P, 9, D])
        gates = sb("gates", [P, 2, 64])
        cols = sb("cols", [P, 7])
        rows = sb("rows", [P, 7, D])
        bfs = sb("bfs", [P, 2])
        resid = sb("resid", [P, 2, D])
        scaleL = sb("scaleL", [P, 2, D])
        colsB = sb("colsB", [P, 5, D])
        ww = sb("ww", [P, 16, D])
        bias5 = sb("bias5", [5, 2, QUAD, D])

        raw = sb("raw", [P, 2, T], I32)
        raw_w = sb("raw_w", [P, T])
        edges = sb("edges", [P, T, 4])
        keyf = sb("keyf", [P, T])
        digit_i = sb("digit_i", [P, T], I32)
        digit_f = sb("digit_f", [P, T])
        tmp1 = sb("tmp1", [P, T])
        tmp2 = sb("tmp2", [P, T])

        class EdgeSet:
            def __init__(self, name):
                self.same = sb(f"{name}_same", [P, T])
                self.gat = sb(f"{name}_gat", [P, 2, T], I32)
                self.sca = sb(f"{name}_sca", [P, T], I32)
                self.hk = sb(f"{name}_hk", [P, 2])
                self.eq = sb(f"{name}_eq", [P, 4, P])
                self.widx = sb(f"{name}_widx", [P, 2], I32)

        by_dst_set = EdgeSet("dst")
        by_src_set = EdgeSet("src")
        wcol = sb("wcol", [P, T])
        merge_f = sb("merge_f", [P, 4, P])
        merge_d = sb("merge_d", [P, 2, P])
        merge_w = sb("merge_w", [P, 2])

        hot = sb("hot", [P, 2, BATCH, DIGIT], BF16)
        scan = sb("scan", [P, 3, DIGIT])
        base_i = sb("base_i", [P, 2, DIGIT], I32)
        base_f = sb("base_f", [P, 2, DIGIT])
        base_b = sb("base_b", [P, 2, DIGIT], BF16)
        junk = sb("junk", [P, DIGIT])
        rank = sb("rank", [P, 2, BATCH])
        rank_i = sb("rank_i", [P, 3, BATCH], I32)
        rank_f = sb("rank_f", [P, 2, BATCH])
        pos = sb("pos", [P, 2, BATCH], I32)
        load4 = sb("load4", [P, 2, BATCH, 4])

        st_gat = sb("st_gat", [P, 2, 2, BATCH], I32)
        st_sca = sb("st_sca", [P, 2, BATCH], I32)
        got = sb("got", [P, 2, 2, BATCH, W])
        gT = sb("gT", [P, 2, BATCH, P])
        pre = sb("pre", [P, BATCH, D])
        msg = sb("msg", [P, BATCH, W])
        run = sb("run", [P, 2, BATCH, W])
        part = sb("part", [P, 2, W])
        merged = sb("merged", [P, 2, W])

        xin = sb("xin", [P, 2, CHUNK, D])
        hin = sb("hin", [P, 2, CHUNK, W])
        rin = sb("rin", [P, 2, CHUNK, W])
        aT = sb("aT", [P, 2, QUAD, P])
        cT = sb("cT", [5, P * QUAD])
        cntT = sb("cntT", [5, 2, QUAD, P])
        stats = sb("stats", [P, 2, QUAD, 6])
        mv = sb("mv", [P, 2, QUAD, 2])
        sd = sb("sd", [P, 2, QUAD])
        rstd = sb("rstd", [P, 2, QUAD])
        n2 = sb("n2", [P, QUAD, D])
        n2T = sb("n2T", [P, QUAD, P])
        vout = sb("vout", [P, QUAD, D])
        xb = sb("xb", [P, QUAD, D])
        res = sb("res", [P, 2, CHUNK, D])
        dg = sb("dg", [P, 4, QUAD, 2])
        yy = sb("yy", [P, 3, QUAD, D])
        tt = sb("tt", [P, 3, QUAD, 2])

        ps = ctx.enter_context(nc.psum_tensor("ps", [P, 8, 512], F32))

        s_load = sem("s_load")
        s_edge = sem("s_edge")
        s_fill = sem("s_fill")
        s_zero = sem("s_zero")
        s_c0 = sem("s_c0")
        s_const = sem("s_const")
        s_constd = sem("s_constd")
        s_wt = sem("s_wt")
        s_wte = sem("s_wte")
        s_wd = sem("s_wd")
        s_wm = sem("s_wm")
        s_wme = sem("s_wme")
        s_wdone = sem("s_wdone")
        s_dve = sem("s_dve")

        linked = [0]

        def link(dve, ins):
            linked[0] += 1
            ins.then_inc(s_dve, 1)
            dve.wait_ge(s_dve, linked[0])

        s_waited = sem("s_waited")

        def own_wait(eng):
            eng.sem_inc(s_waited, 1)

        LOADS = 24

        def flat(v, n):
            return v.rearrange("(a n) -> a n", a=1).to_broadcast([P, n])

        class SortPass:
            def __init__(self, name):
                self.hot1 = sem(f"{name}_hot1")
                self.used1 = sem(f"{name}_used1")
                self.total = sem(f"{name}_total")
                self.based = sem(f"{name}_based")
                self.hot2 = sem(f"{name}_hot2")
                self.prefix = sem(f"{name}_prefix")
                self.ranked = sem(f"{name}_ranked")
                self.used2 = sem(f"{name}_used2")
                self.staged = sem(f"{name}_staged")
                self.sent = [sem(f"{name}_sent{h}") for h in range(2)]
                self.loaded = sem(f"{name}_loaded")
                self.chain = sem(f"{name}_chain")

        low_pass, high_pass = SortPass("low"), SortPass("high")
        s_sorted = sem("s_sorted")

        def make_hot(dve, t, h):
            for j in range(BATCH):
                ins = dve.tensor_scalar(hot[:, h, j, :], digits_b[:, :], digit_f[:, bass.ds(t + j, 1)], None,
                                        ALU.is_equal)
            return ins

        def sort_vector(dve, ph, shift, transposed):
            link(dve, dve.tensor_copy(digit_i[:, :], edges[:, :, 0]))
            if shift:
                link(dve, dve.tensor_scalar(digit_i[:, :], digit_i[:, :], shift, None, ALU.logical_shift_right))
            else:
                link(dve, dve.tensor_scalar(digit_i[:, :], digit_i[:, :], DIGIT - 1, None, ALU.bitwise_and))
            link(dve, dve.tensor_copy(digit_f[:, :], digit_i[:, :]))
            with dve.Fori(0, IT) as i:
                for h in range(2):
                    dve.wait_ge(ph.used1, i * 2 + h + 1)
                    make_hot(dve, i * (2 * BATCH) + h * BATCH, h).then_inc(ph.hot1, 1)
            dve.wait_ge(ph.total, 1)
            link(dve, dve.tensor_copy(scan[:, 0, :], ps[:, 0, 0:DIGIT]))
            link(dve, dve.tensor_copy(scan[:, 1, :], scan[:, 0, :]))
            a, b, s = 1, 2, 1
            while s < DIGIT:
                link(dve, dve.tensor_copy(scan[:, b, 0:s], scan[:, a, 0:s]))
                link(dve, dve.tensor_tensor(scan[:, b, s:], scan[:, a, s:], scan[:, a, 0:DIGIT - s], ALU.add))
                a, b, s = b, a, 2 * s
            link(dve, dve.tensor_tensor(scan[:, b, :], scan[:, a, :], scan[:, 0, :], ALU.subtract))
            link(dve, dve.tensor_copy(base_i[:, 0, :], scan[:, b, :]))
            link(dve, dve.tensor_scalar(base_i[:, 1, :], base_i[:, 0, :], P - 1, None, ALU.bitwise_and))
            link(dve, dve.tensor_copy(base_f[:, 1, :], base_i[:, 1, :]))
            link(dve, dve.tensor_tensor(base_f[:, 0, :], scan[:, b, :], base_f[:, 1, :], ALU.subtract))
            link(dve, dve.tensor_copy(base_b[:, 0, :], base_f[:, 0, :]))
            dve.tensor_copy(base_b[:, 1, :], base_f[:, 1, :]).then_inc(ph.based, 1)
            def ranks(i, first):
                for h in range(2):
                    t = i * (2 * BATCH) + h * BATCH
                    if not first:
                        dve.wait_ge(ph.used2, i * 2 + h - 1)
                    make_hot(dve, t, h).then_inc(ph.hot2, 1)
                    for j in range(BATCH):
                        dve.wait_ge(ph.prefix, i * (2 * BATCH) + h * BATCH + j + 1)
                        dve.tensor_tensor_reduce(junk[:, :], ps[:, 0, 0:DIGIT], hot[:, h, j, :], 1.0, 0.0,
                                                 ALU.mult, ALU.add, rank[:, h, j:j + 1]).then_inc(ph.ranked, 1)
                    dve.wait_ge(ph.ranked, i * (2 * BATCH) + (h + 1) * BATCH)
                    if not first:
                        dve.wait_ge(ph.sent[h], i * (16 * BATCH))
                    if transposed:
                        done = i * 4 + h * 2
                        dve.tensor_copy(rank_i[:, 0, :], rank[:, h, :]).then_inc(ph.chain, 1)
                        dve.wait_ge(ph.chain, done * 2 + 1)
                        dve.tensor_scalar(rank_i[:, 1, :], rank_i[:, 0, :], 7, None, ALU.logical_shift_right)
                        dve.tensor_scalar(rank_i[:, 2, :], rank_i[:, 0, :], P - 1, None,
                                          ALU.bitwise_and).then_inc(ph.chain, 1)
                        dve.wait_ge(ph.chain, done * 2 + 2)
                        dve.tensor_copy(rank_f[:, 0, :], rank_i[:, 1, :]).then_inc(ph.chain, 1)
                        dve.tensor_copy(rank_f[:, 1, :], rank_i[:, 2, :]).then_inc(ph.chain, 1)
                        dve.wait_ge(ph.chain, done * 2 + 4)
                    if transposed:
                        dve.scalar_tensor_tensor(out=pos[:, h, :], in0=rank_f[:, 1, :], scalar=float(T),
                                                 in1=rank_f[:, 0, :], op0=ALU.mult, op1=ALU.add)
                    else:
                        dve.tensor_copy(pos[:, h, :], rank[:, h, :])
                    dve.tensor_copy(load4[:, h, :, :], edges[:, bass.ds(t, BATCH), :]).then_inc(ph.staged, 1)
            ranks(0, True)
            with dve.Fori(1, IT) as i:
                ranks(i, False)

        def sort_tensor(pe, ph):
            tot = ps[:, 0, 0:DIGIT]
            for h in range(2):
                last = pe.matmul(tot, ones_b[:, :], zeros_b[:, :], start=(h == 0), stop=False,
                                 skip_group_check=True)
                last.then_inc(ph.used1, 1)
            with pe.Fori(0, IT) as i:
                for h in range(2):
                    pe.wait_ge(ph.hot1, i * 2 + h + 1)
                    for j in range(BATCH):
                        last = pe.matmul(tot, ones_b[:, :], hot[:, h, j, :], start=False, stop=False,
                                         skip_group_check=True)
                    last.then_inc(ph.used1, 1)
            pe.wait_ge(ph.used1, 2 * IT + 2)
            pe.matmul(tot, ones_b[:, :], zeros_b[:, :], start=False, stop=True,
                      skip_group_check=True).then_inc(ph.total, 1)
            pe.wait_ge(ph.based, 1)
            pe.matmul(tot, ident_b[:, :], base_b[:, 0, :], start=True, stop=False, skip_group_check=True)
            pe.matmul(tot, ident_b[:, :], base_b[:, 1, :], start=False, stop=False, skip_group_check=True)
            with pe.Fori(0, IT) as i:
                for h in range(2):
                    pe.wait_ge(ph.hot2, i * 2 + h + 1)
                    for j in range(BATCH):
                        pe.matmul(tot, before_b[:, :], hot[:, h, j, :], start=False, stop=False,
                                  skip_group_check=True).then_inc(ph.prefix, 1)
                        pe.wait_ge(ph.ranked, i * (2 * BATCH) + h * BATCH + j + 1)
                        last = pe.matmul(tot, notbefore_b[:, :], hot[:, h, j, :], start=False, stop=False,
                                         skip_group_check=True)
                    last.then_inc(ph.used2, 1)
            pe.matmul(tot, ones_b[:, :], zeros_b[:, :], start=False, stop=True, skip_group_check=True)

        def sort_pool(pool, ph, target):
            with pool.Fori(0, IT) as i:
                for h in range(2):
                    pool.wait_ge(ph.staged, i * 2 + h + 1)
                    own_wait(pool)
                    for j in range(BATCH):
                        pool.indirect_dma_start(
                            target, bass.IndirectOffsetOnAxis(ap=pos[:, h, j:j + 1], axis=0), load4[:, h, j, :],
                            None, bounds_check=P * T - 1, oob_is_err=False).then_inc(ph.sent[h], 16)

        def sort_load(sp, ph, target):
            for h in range(2):
                sp.wait_ge(ph.sent[h], 16 * BATCH * IT)
            sp.dma_start(edges[:, :, :], target.rearrange("(p t) c -> p t c", t=T)).then_inc(ph.loaded, 16)

        class SetPrep:
            def __init__(self, name):
                self.diag = sem(f"{name}_diag")
                self.keys = sem(f"{name}_keys")
                self.masked = sem(f"{name}_masked")
                self.count = sem(f"{name}_count")

        dst_prep, src_prep = SetPrep("dprep"), SetPrep("sprep")

        def prep_vector(dve, es, ph):
            link(dve, dve.memset(es.same[:, 0:1], 0.0))
            link(dve, dve.tensor_tensor(es.same[:, 1:T], keyf[:, 0:T - 1], keyf[:, 1:T], ALU.is_equal))
            link(dve, dve.tensor_scalar(tmp1[:, :], keyf[:, :], keyf[:, 0:1], None, ALU.is_equal))
            link(dve, dve.tensor_scalar(tmp2[:, :], keyf[:, :], -1.0, head_row[:, 0:1], ALU.mult, ALU.add))
            link(dve, dve.tensor_tensor(tmp1[:, :], tmp1[:, :], tmp2[:, :], ALU.mult))
            link(dve, dve.tensor_tensor(tmp2[:, :], keyf[:, :], tmp1[:, :], ALU.add))
            link(dve, dve.scalar_tensor_tensor(out=tmp2[:, 0:T - 1], in0=es.same[:, 1:T], scalar=float(SKIP),
                                               in1=tmp2[:, 0:T - 1], op0=ALU.mult, op1=ALU.add))
            link(dve, dve.tensor_copy(tmp2[:, T - 1:T], tail_row[:, :]))
            link(dve, dve.tensor_copy(es.sca[:, :], tmp2[:, :]))
            link(dve, dve.tensor_copy(es.hk[:, 0:1], keyf[:, 0:1]))
            link(dve, dve.tensor_copy(es.hk[:, 1:2], keyf[:, T - 1:T]))
            for b in range(2):
                dve.tensor_scalar(merge_d[:, b, :], ident[:, :], es.hk[:, b:b + 1], None,
                                  ALU.mult).then_inc(ph.diag, 1)
            dve.wait_ge(ph.keys, 1)
            for a in range(2):
                for b in range(2):
                    link(dve, dve.tensor_scalar(es.eq[:, 2 * a + b, :], ps[:, 1, b * P:(b + 1) * P],
                                                es.hk[:, a:a + 1], None, ALU.is_equal))
                    earlier = upto if (a, b) == (0, 1) else before
                    dve.tensor_tensor(merge_f[:, 2 * a + b, :], es.eq[:, 2 * a + b, :], earlier[:, :],
                                      ALU.mult).then_inc(ph.masked, 1)
            dve.wait_ge(ph.count, 1)
            link(dve, dve.tensor_scalar(merge_w[:, :], ps[:, 2, 0:2], 0.0, float(SKIP), ALU.is_gt, ALU.mult))
            link(dve, dve.tensor_tensor(es.widx[:, :], merge_w[:, :], es.hk[:, :], ALU.add))

        def prep_tensor(pe, es, ph):
            pe.wait_ge(ph.diag, 2)
            for b in range(2):
                last = pe.matmul(ps[:, 1, b * P:(b + 1) * P], ones[:, :], merge_d[:, b, :], start=True, stop=True)
            last.then_inc(ph.keys, 1)
            pe.wait_ge(ph.masked, 4)
            for b in range(2):
                for a in range(2):
                    last = pe.matmul(ps[:, 2, b:b + 1], merge_f[:, 2 * a + b, :], ones[:, 0:1],
                                     start=(a == 0), stop=(a == 1))
            last.then_inc(ph.count, 1)

        s_parts, s_joined, s_joinedc, s_stored = sem("parts"), sem("joined"), sem("joinedc"), sem("stored")

        class EdgePhase:

            def __init__(self, turn, es, table, gathers, layer):
                name = f"e{turn}"
                self.turn, self.es, self.table, self.gathers, self.layer = turn, es, table, gathers, layer
                self.n = BATCH * len(gathers)
                self.staged = sem(f"{name}_staged")
                self.gat = [sem(f"{name}_gat{h}") for h in range(2)]
                self.used = sem(f"{name}_used")
                if layer is not None:
                    self.turned = sem(f"{name}_turned")
                    self.copied = sem(f"{name}_copied")
                    self.mixed = sem(f"{name}_mixed")
                    self.added = sem(f"{name}_added")
                self.messages = sem(f"{name}_messages")
                self.chain = sem(f"{name}_chain")
                self.summed = sem(f"{name}_summed")
                self.sent = [sem(f"{name}_sent{h}") for h in range(2)]
                self.parts, self.joined, self.joinedc, self.stored = s_parts, s_joined, s_joinedc, s_stored

        def edge_pool(pool, ph):
            es = ph.es

            def gather(i, h, first):
                pool.wait_ge(ph.staged, i * 2 + h + 1)
                if not first:
                    pool.wait_ge(ph.used, i * 2 + h - 1)
                own_wait(pool)
                for g, (tab, row, c) in enumerate(ph.gathers):
                    for j in range(BATCH):
                        pool.indirect_dma_start(
                            got[:, h, g, j, 0:c], None, tab,
                            bass.IndirectOffsetOnAxis(ap=st_gat[:, h, g, j:j + 1], axis=0),
                            bounds_check=N - 1, oob_is_err=False).then_inc(ph.gat[h], 16)

            def scatter(n, h):
                pool.wait_ge(ph.summed, n + 1)
                own_wait(pool)
                for j in range(BATCH):
                    pool.indirect_dma_start(
                        ph.table, bass.IndirectOffsetOnAxis(ap=st_sca[:, h, j:j + 1], axis=0), run[:, h, j, :],
                        None, bounds_check=TR - 1, oob_is_err=False).then_inc(ph.sent[h], 16)

            gather(0, 0, True)
            gather(0, 1, True)
            scatter(0, 0)
            with pool.Fori(1, IT) as i:
                gather(i, 0, False)
                scatter(i * 2 - 1, 1)
                gather(i, 1, False)
                scatter(i * 2, 0)
            scatter(2 * IT - 1, 1)
            pool.wait_ge(ph.joinedc, ph.turn + 1)
            for b in range(2):
                pool.indirect_dma_start(
                    ph.table, bass.IndirectOffsetOnAxis(ap=es.widx[:, b:b + 1], axis=0), merged[:, b, :],
                    None, bounds_check=TR - 1, oob_is_err=False).then_inc(ph.stored, 16)

        def edge_tensor(pe, ph):
            es = ph.es

            def batch(i, h, first):
                pe.wait_ge(ph.gat[h], i * (16 * ph.n) + 16 * ph.n)
                if not first:
                    pe.wait_ge(ph.copied, i * 4 + 2 * h)
                for g in range(2):
                    for j in range(BATCH):
                        last = pe.transpose(turned[g][:, j, :], got[:, h, g, j, 0:D], ident[:, :])
                    last.then_inc(ph.turned, 1)
                pe.wait_ge(ph.turned, i * 4 + 2 * h + 2)
                pe.wait_ge(ph.copied, i * 4 + 2 * h + 2)
                if not first:
                    pe.wait_ge(ph.added, i * 2 + h)
                for j in range(BATCH):
                    for g in range(2):
                        last = pe.matmul(mixed[:, j, :], gT[:, g, j, :], ww[:, 7 * ph.layer + g, :],
                                         start=(g == 0), stop=(g == 1))
                last.then_inc(ph.mixed, 1)

            if ph.layer is not None:
                batch(0, 0, True)
                batch(0, 1, False)
                with pe.Fori(1, IT) as i:
                    batch(i, 0, False)
                    batch(i, 1, False)
            pe.wait_ge(ph.parts, 16 * (ph.turn + 1))
            for b in range(2):
                for a in range(2):
                    last = pe.matmul(ps[:, 6, b * 256:b * 256 + W], es.eq[:, 2 * a + b, :], part[:, a, :],
                                     start=(a == 0), stop=(a == 1))
            last.then_inc(ph.joined, 1)

        turned = [ps[:, 2 * g:2 * g + 2, :].rearrange("p b n -> p (b n)")[:, 0:BATCH * P]
                  .rearrange("p (j e) -> p j e", j=BATCH) for g in range(2)]
        mixed = ps[:, 4:6, :].rearrange("p b n -> p (b n)")[:, 0:BATCH * D].rearrange("p (j e) -> p j e", j=BATCH)

        def edge_scalar(act, ph):
            def batch(i, h, first):
                if ph.layer is not None:
                    for g in range(2):
                        act.wait_ge(ph.turned, i * 4 + 2 * h + g + 1)
                        if not first:
                            act.wait_ge(ph.mixed, i * 2 + h)
                        ins = act.activation(gT[:, g, :, :], turned[g], ACT.Copy).then_inc(ph.copied, 1)
                    act.wait_ge(ph.added, i * 2 + h + 1)
                    if not first:
                        act.wait_ge(ph.summed, i * 2 + h)
                    act.activation(msg[:, :, 0:D], pre[:, :, :], ACT.Relu).then_inc(ph.messages, 1)
                else:
                    act.wait_ge(ph.gat[h], i * (16 * ph.n) + 16 * ph.n)
                    if not first:
                        act.wait_ge(ph.summed, i * 2 + h)
                    for j in range(BATCH):
                        last = act.activation(msg[:, j, :], got[:, h, 0, j, :], ACT.Copy,
                                              scale=wcol[:, bass.ds(i * (2 * BATCH) + h * BATCH + j, 1)])
                    last.then_inc(ph.messages, 1)

            batch(0, 0, True)
            batch(0, 1, False)
            with act.Fori(1, IT) as i:
                batch(i, 0, False)
                batch(i, 1, False)

        def edge_vector(dve, ph):
            es = ph.es

            def stage(i, h):
                t = i * (2 * BATCH) + h * BATCH
                dve.tensor_copy(st_gat[:, h, 0:len(ph.gathers), :],
                                es.gat[:, 2 - len(ph.gathers):2, bass.ds(t, BATCH)]).then_inc(ph.staged, 1)

            def batch(i, h, first, ahead):
                t = i * (2 * BATCH) + h * BATCH
                if ph.layer is not None:
                    dve.wait_ge(ph.mixed, i * 2 + h + 1)
                    if not first:
                        dve.wait_ge(ph.messages, i * 2 + h)
                    dve.tensor_tensor(pre[:, :, :], mixed, ww[:, 7 * ph.layer + 2, :].unsqueeze(1)
                                      .to_broadcast([P, BATCH, D]), ALU.add).then_inc(ph.added, 1)
                dve.wait_ge(ph.messages, i * 2 + h + 1)
                dve.wait_ge(ph.gat[h], i * (16 * ph.n) + 16 * ph.n)
                if ph.layer is None:
                    dve.sem_inc(ph.used, 1)
                else:
                    dve.sem_inc(ph.used, 1)
                if ahead:
                    stage(i + 1, h)
                if i is not 0:
                    dve.wait_ge(ph.sent[h], i * (16 * BATCH))
                dve.tensor_copy(st_sca[:, h, :], es.sca[:, bass.ds(t, BATCH)])
                for j in range(BATCH):
                    last = run[:, 1 - h, BATCH - 1, :] if j == 0 else run[:, h, j - 1, :]
                    ins = dve.scalar_tensor_tensor(out=run[:, h, j, :], in0=last,
                                                   scalar=es.same[:, bass.ds(t + j, 1)], in1=msg[:, j, :],
                                                   op0=ALU.mult, op1=ALU.add)
                    ins.then_inc(ph.chain, 1)
                    dve.wait_ge(ph.chain, i * (2 * BATCH) + h * BATCH + j + 1)
                dve.sem_inc(ph.summed, 1)

            link(dve, dve.memset(run[:, 1, BATCH - 1, :], 0.0))
            if ph.layer is not None:
                link(dve, dve.memset(msg[:, :, D:W], 1.0))
            elif ph.gathers[0][2] == D:
                link(dve, dve.memset(got[:, :, 0, :, D:W], 1.0))
            stage(0, 0)
            stage(0, 1)
            batch(0, 0, True, True)
            batch(0, 1, False, True)
            with dve.Fori(1, IT - 1) as i:
                batch(i, 0, False, True)
                batch(i, 1, False, True)
            batch(IT - 1, 0, False, False)
            batch(IT - 1, 1, False, False)
            dve.wait_ge(ph.joined, ph.turn + 1)
            dve.tensor_copy(merged[:, :, :], ps[:, 6, :].rearrange("p (b n) -> p b n", b=2)[:, :, 0:W])\
               .then_inc(ph.joinedc, 1)

        def edge_sync(sp, ph):
            for h in range(2):
                sp.wait_ge(ph.sent[h], 16 * BATCH * IT)
            sp.dma_start(part[:, :, :], ph.table[HEAD:HEAD + 2 * P, :].rearrange("(a p) c -> p a c", a=2))\
              .then_inc(ph.parts, 16)
            sp.wait_ge(ph.stored, 32 * (ph.turn + 1))

        class DensePhase:
            def __init__(self, name, first, last, gated):
                self.turned = sem(f"{name}_turned")
                self.copied = sem(f"{name}_copied")
                self.mixed = sem(f"{name}_mixed")
                self.chunk = sem(f"{name}_chunk")
                if first:
                    self.spread = sem(f"{name}_spread")
                    self.stats = sem(f"{name}_stats")
                    self.var = sem(f"{name}_var")
                    self.std = sem(f"{name}_std")
                    self.norm = sem(f"{name}_norm")
                if last:
                    self.stats2 = sem(f"{name}_stats2")
                    self.var2 = sem(f"{name}_var2")
                    self.std2 = sem(f"{name}_std2")
                    self.a1 = sem(f"{name}_a1")
                    self.a2 = sem(f"{name}_a2")
                if first and last:
                    self.turned2 = sem(f"{name}_turned2")
                    self.copied2 = sem(f"{name}_copied2")
                    self.mixed2 = sem(f"{name}_mixed2")
                    self.added = sem(f"{name}_added")
                if gated:
                    self.gate = sem(f"{name}_gate")
                    self.act1 = sem(f"{name}_act1")
                    self.ca = sem(f"{name}_ca")
                self.loaded = [sem(f"{name}_in{b}") for b in range(2)]
                self.saved = [sem(f"{name}_out{b}") for b in range(2)]

        d1 = DensePhase("d1", True, False, False)
        d2 = DensePhase("d2", True, True, False)
        d3 = DensePhase("d3", False, True, True)

        def chunks(eng, body):
            body(0, 0, 0)
            body(0, 1, ROWS)
            with eng.Fori(1, PAIRS) as i:
                body(i, 0, i * (2 * ROWS))
                body(i, 1, i * (2 * ROWS) + ROWS)
            body(PAIRS, 0, LAST)

        def node_rows(tab, base, c):
            return tab[bass.ds(base, ROWS), 0:c].rearrange("(p j) c -> p j c", j=CHUNK)

        def dense_sync(sp, ph, ins, target):
            def load(i, b, base):
                if i is not 0:
                    sp.wait_ge(ph.chunk, i * 2 + b - 1)
                for tab, buf, c in ins:
                    sp.dma_start(buf[:, b, :, 0:c], node_rows(tab, base, c)).then_inc(ph.loaded[b], 16)

            def store(n, b, base):
                sp.wait_ge(ph.chunk, n + 1)
                sp.dma_start(node_rows(target, base, D), res[:, b, :, :]).then_inc(ph.saved[b], 16)

            load(0, 0, 0)
            load(0, 1, ROWS)
            store(0, 0, 0)
            with sp.Fori(1, PAIRS) as i:
                load(i, 0, i * (2 * ROWS))
                store(i * 2 - 1, 1, i * (2 * ROWS) - ROWS)
                load(i, 1, i * (2 * ROWS) + ROWS)
                store(i * 2, 0, i * (2 * ROWS))
            load(PAIRS, 0, LAST)
            store(2 * PAIRS - 1, 1, (2 * PAIRS - 1) * ROWS)
            sp.wait_ge(ph.saved[1], 16 * PAIRS)
            sp.wait_ge(ph.saved[0], 16 * PAIRS)
            store(2 * PAIRS, 0, LAST)
            sp.wait_ge(ph.saved[0], 16 * (PAIRS + 1))

        def turn(pe, bank, tile, q, c=None):
            for j in range(QUAD):
                last = pe.transpose(ps[:, bank, j * P:(j + 1) * P], tile[:, QUAD * q + j, 0:D], ident[:, :])
            return last

        def update_tensor(pe, ph, a_in, n_in, layer, tail):
            def body(i, b, base):
                pe.wait_ge(ph.loaded[b], i * (16 * n_in) + 16 * n_in)
                for q in range(2):
                    u = i * 4 + (2 * b + q)
                    if not (i is 0 and b == 0 and q == 0):
                        pe.wait_ge(ph.copied, u * 3)
                    turn(pe, 0, a_in[:, b], q).then_inc(ph.turned, 1)
                    turn(pe, 1, rin[:, b], q).then_inc(ph.turned, 1)
                    pe.transpose(ps[0:QUAD, 2, 0:P], rin[:, b, QUAD * q:QUAD * (q + 1), D], ident[:, :])\
                      .then_inc(ph.turned, 1)
                    pe.wait_ge(ph.copied, u * 3 + 3)
                    if not (i is 0 and b == 0 and q == 0):
                        pe.wait_ge(ph.norm, u)
                    pe.wait_ge(ph.spread, u + 1)
                    acc = ps[:, 3, :]
                    for j in range(QUAD):
                        pe.matmul(acc[:, j * P:(j + 1) * P], aT[:, 0, j, :], ww[:, 7 * layer + 3, :],
                                  start=(j == 0), stop=False, skip_group_check=True)
                        pe.matmul(acc[:, j * P:(j + 1) * P], aT[:, 1, j, :], ww[:, 7 * layer + 5, :],
                                  start=False, stop=False, skip_group_check=True)
                    pe.matmul(acc, cntT[0:5, 0, 0, :], bias5[:, layer, :, :], start=False, stop=True,
                              skip_group_check=True).then_inc(ph.mixed, 1)
                    if tail:
                        pe.wait_ge(ph.norm, u + 1)
                        turn(pe, 4, n2, 0).then_inc(ph.turned2, 1)
                        pe.wait_ge(ph.copied2, u + 1)
                        if not (i is 0 and b == 0 and q == 0):
                            pe.wait_ge(ph.added, u)
                        for j in range(QUAD):
                            last = pe.matmul(ps[:, 5, j * P:(j + 1) * P], n2T[:, j, :], ww[:, 14, :],
                                             start=True, stop=True)
                        last.then_inc(ph.mixed2, 1)
            chunks(pe, body)

        def update_scalar(act, ph, tail):
            def body(i, b, base):
                for q in range(2):
                    u = i * 4 + (2 * b + q)
                    for g in range(2):
                        act.wait_ge(ph.turned, u * 3 + g + 1)
                        if not (i is 0 and b == 0 and q == 0):
                            act.wait_ge(ph.mixed, u)
                        act.activation(aT[:, g, :, :], ps[:, g, :].rearrange("p (j e) -> p j e", j=QUAD), ACT.Copy)\
                           .then_inc(ph.copied, 1)
                    act.wait_ge(ph.turned, u * 3 + 3)
                    act.activation(cntT[0:QUAD, 0, 0, :], ps[0:QUAD, 2, 0:P], ACT.Copy).then_inc(ph.copied, 1)
                    act.wait_ge(ph.copied, u * 3 + 3)
                    act.sem_inc(ph.spread, 1)
                    act.wait_ge(ph.var, u + 1)
                    act.activation(sd[:, 0, :], mv[:, 0, :, 1], ACT.Sqrt, bias=eps[:, 0:1]).then_inc(ph.std, 1)
                    if tail:
                        act.wait_ge(ph.turned2, u + 1)
                        if not (i is 0 and b == 0 and q == 0):
                            act.wait_ge(ph.mixed2, u)
                        act.activation(n2T[:, :, :], ps[:, 4, :].rearrange("p (j e) -> p j e", j=QUAD), ACT.Copy)\
                           .then_inc(ph.copied2, 1)
                        act.wait_ge(ph.var2, u + 1)
                        act.activation(sd[:, 1, :], mv[:, 1, :, 1], ACT.Sqrt, bias=eps[:, 0:1]).then_inc(ph.std2, 1)
            chunks(act, body)

        def update_vector(dve, ph, tail):
            def norm(k, value, target, u, s_stats, s_var, s_std, s_rstd):
                for j in range(QUAD):
                    last = dve.bn_stats(stats[:, k, j, :], value(j))
                last.then_inc(s_stats, 1)
                dve.wait_ge(s_stats, u * 2 + 1)
                own_wait(dve)
                for j in range(QUAD):
                    last = dve.bn_aggr(mv[:, k, j, :], stats[:, k, j, :])
                last.then_inc(s_var, 1)
                dve.wait_ge(s_std, u + 1)
                dve.reciprocal(rstd[:, k, :], sd[:, k, :]).then_inc(s_stats, 1)
                dve.wait_ge(s_stats, u * 2 + 2)
                for j in range(QUAD):
                    last = dve.tensor_scalar(target(j), value(j), mv[:, k, j, 0:1], rstd[:, k, j:j + 1],
                                             ALU.subtract, ALU.mult)
                return last

            def body(i, b, base):
                if i is not 0:
                    dve.wait_ge(ph.saved[b], i * 16)
                for q in range(2):
                    u = i * 4 + (2 * b + q)
                    dve.wait_ge(ph.mixed, u + 1)
                    if tail:
                        if not (i is 0 and b == 0 and q == 0):
                            dve.wait_ge(ph.turned2, u)
                        norm(0, lambda j: ps[:, 3, j * P:(j + 1) * P], lambda j: n2[:, j, :], u,
                             ph.stats, ph.var, ph.std, None).then_inc(ph.norm, 1)
                        dve.wait_ge(ph.mixed2, u + 1)
                        dve.tensor_tensor(vout[:, :, :], ps[:, 5, :].rearrange("p (j e) -> p j e", j=QUAD),
                                          xin[:, b, QUAD * q:QUAD * (q + 1), :], ALU.add).then_inc(ph.a1, 1)
                        dve.wait_ge(ph.a1, u + 1)
                        dve.tensor_tensor(xb[:, :, :], vout[:, :, :],
                                          ww[:, 15, :].unsqueeze(1).to_broadcast([P, QUAD, D]),
                                          ALU.add).then_inc(ph.added, 1)
                        dve.wait_ge(ph.added, u + 1)
                        last = norm(1, lambda j: xb[:, j, :], lambda j: res[:, b, QUAD * q + j, :], u,
                                    ph.stats2, ph.var2, ph.std2, None)
                    else:
                        last = norm(0, lambda j: ps[:, 3, j * P:(j + 1) * P],
                                    lambda j: res[:, b, QUAD * q + j, :], u, ph.stats, ph.var, ph.std, None)
                        last.then_inc(ph.norm, 1)
                    if tail and q == 1:
                        last.then_inc(ph.a2, 1)
                if tail:
                    dve.wait_ge(ph.a2, i * 2 + b + 1)
                else:
                    dve.wait_ge(ph.norm, i * 4 + 2 * b + 2)
                dve.sem_inc(ph.chunk, 1)
            chunks(dve, body)

        def final_tensor(pe, ph):
            def body(i, b, base):
                pe.wait_ge(ph.loaded[b], i * 48 + 48)
                for q in range(2):
                    u = i * 4 + (2 * b + q)
                    if not (i is 0 and b == 0 and q == 0):
                        pe.wait_ge(ph.copied, u * 2)
                    turn(pe, 0, hin[:, b], q).then_inc(ph.turned, 1)
                    turn(pe, 1, rin[:, b], q).then_inc(ph.turned, 1)
                    pe.wait_ge(ph.copied, u * 2 + 2)
                    if not (i is 0 and b == 0 and q == 0):
                        pe.wait_ge(ph.a1, u)
                    for j in range(QUAD):
                        for g in range(2):
                            last = pe.matmul(ps[:, 3, j * P + 64 * g:j * P + 64 * (g + 1)], aT[:, g, j, :],
                                             gates[:, g, :], start=True, stop=True)
                    last.then_inc(ph.mixed, 1)
            chunks(pe, body)

        def final_scalar(act, ph):
            def body(i, b, base):
                for q in range(2):
                    u = i * 4 + (2 * b + q)
                    for g in range(2):
                        act.wait_ge(ph.turned, u * 2 + g + 1)
                        if not (i is 0 and b == 0 and q == 0):
                            act.wait_ge(ph.mixed, u)
                        act.activation(aT[:, g, :, :], ps[:, g, :].rearrange("p (j e) -> p j e", j=QUAD), ACT.Copy)\
                           .then_inc(ph.copied, 1)
                    act.wait_ge(ph.gate, u + 1)
                    act.activation(tt[:, 1, :, :], tt[:, 0, :, :], ACT.Sigmoid).then_inc(ph.act1, 1)
                    act.wait_ge(ph.var2, u + 1)
                    act.activation(sd[:, 1, :], mv[:, 1, :, 1], ACT.Sqrt, bias=eps[:, 0:1]).then_inc(ph.std2, 1)
            chunks(act, body)

        def final_vector(dve, ph):
            STEPS = 14

            def body(i, b, base):
                if i is not 0:
                    dve.wait_ge(ph.saved[b], i * 16)
                dve.wait_ge(ph.loaded[b], i * 48 + 48)
                for q in range(2):
                    u = i * 4 + (2 * b + q)
                    n = [0]

                    def step(ins):
                        n[0] += 1
                        ins.then_inc(ph.ca, 1)
                        dve.wait_ge(ph.ca, u * STEPS + n[0])

                    tiles = slice(QUAD * q, QUAD * (q + 1))

                    def wide(row):
                        return rows[:, row, :].unsqueeze(1).to_broadcast([P, QUAD, D])

                    def halves(t):
                        return t.rearrange("p j (g c) -> p (j g) c", g=2)

                    def each(t):
                        return t.rearrange("p j g -> p (j g)").unsqueeze(2).to_broadcast([P, 2 * QUAD, 64])

                    step(dve.tensor_copy(dg[:, 0, :, 0], hin[:, b, tiles, D]))
                    step(dve.tensor_copy(dg[:, 0, :, 1], rin[:, b, tiles, D]))
                    step(dve.tensor_scalar(dg[:, 1, :, :], dg[:, 0, :, :], 0.0, None, ALU.is_gt))
                    step(dve.tensor_tensor(dg[:, 2, :, :], dg[:, 0, :, :], dg[:, 1, :, :], ALU.mult))
                    step(dve.scalar_tensor_tensor(out=dg[:, 3, :, :], in0=dg[:, 2, :, :], scalar=1.0,
                                                  in1=dg[:, 1, :, :], op0=ALU.add, op1=ALU.subtract))
                    step(dve.reciprocal(dg[:, 0, :, :], dg[:, 3, :, :]))
                    step(dve.tensor_tensor(dg[:, 2, :, :], dg[:, 0, :, :], dg[:, 1, :, :], ALU.mult))
                    dve.wait_ge(ph.mixed, u + 1)
                    prod = ps[:, 3, :].rearrange("p (m c) -> p m c", c=64)
                    dve.tensor_tensor(halves(yy[:, 0]), prod, each(dg[:, 2]), ALU.mult).then_inc(ph.a1, 1)
                    dve.wait_ge(ph.a1, u + 1)
                    step(dve.tensor_tensor(yy[:, 1], yy[:, 0], wide(5), ALU.add))
                    step(dve.tensor_tensor(yy[:, 0], yy[:, 1], wide(6), ALU.mult))
                    step(dve.tensor_reduce(tt[:, 2, :, :].rearrange("p j g -> p (j g)"), halves(yy[:, 0]),
                                           AX.X, ALU.add))
                    dve.tensor_tensor(tt[:, 0, :, :], tt[:, 2, :, :],
                                      bfs[:, :].unsqueeze(1).to_broadcast([P, QUAD, 2]),
                                      ALU.add).then_inc(ph.gate, 1)
                    step(dve.scalar_tensor_tensor(out=yy[:, 2], in0=yy[:, 1], scalar=0.0,
                                                  in1=xin[:, b, tiles, :], op0=ALU.max, op1=ALU.add))
                    dve.wait_ge(ph.act1, u + 1)
                    step(dve.scalar_tensor_tensor(out=halves(yy[:, 0]), in0=halves(yy[:, 1]), scalar=0.0,
                                                  in1=each(tt[:, 1]), op0=ALU.min, op1=ALU.mult))
                    step(dve.tensor_tensor(vout[:, :, :], yy[:, 2], yy[:, 0], ALU.add))
                    for j in range(QUAD):
                        last = dve.bn_stats(stats[:, 1, j, :], vout[:, j, :])
                    last.then_inc(ph.stats2, 1)
                    dve.wait_ge(ph.stats2, u * 2 + 1)
                    own_wait(dve)
                    for j in range(QUAD):
                        last = dve.bn_aggr(mv[:, 1, j, :], stats[:, 1, j, :])
                    last.then_inc(ph.var2, 1)
                    dve.wait_ge(ph.std2, u + 1)
                    dve.reciprocal(rstd[:, 1, :], sd[:, 1, :]).then_inc(ph.stats2, 1)
                    dve.wait_ge(ph.stats2, u * 2 + 2)
                    for j in range(QUAD):
                        last = dve.tensor_scalar(res[:, b, QUAD * q + j, :], vout[:, j, :], mv[:, 1, j, 0:1],
                                                 rstd[:, 1, j:j + 1], ALU.subtract, ALU.mult)
                    last.then_inc(ph.a2, 1)
                    assert n[0] <= STEPS
                    while n[0] < STEPS:
                        n[0] += 1
                        dve.sem_inc(ph.ca, 1)
                dve.wait_ge(ph.a2, i * 4 + 2 * b + 2)
                dve.sem_inc(ph.chunk, 1)
            chunks(dve, body)

        zeros_b = sb("zeros_b", [P, DIGIT], BF16)

        e0 = EdgePhase(0, by_dst_set, msg_sum, [(x, 0, D), (x, 1, D)], 0)
        e1 = EdgePhase(1, by_dst_set, msg_sum, [(n1_table, 0, D), (n1_table, 1, D)], 1)
        e2 = EdgePhase(2, by_src_set, hop1, [(x1_table, 1, D)], None)
        e3 = EdgePhase(3, by_src_set, hop2, [(hop1, 1, W)], None)

        block = ctx.enter_context(nc.Block())

        @block.sync
        def _(sp):
            n = 0
            for t, s in ((nat[:, 0, :], W_enc), (nat[:, 9, :], W_out),
                         (nat[:, 10:12, :], Wm2.rearrange("l o k -> o l k")),
                         (nat[:, 1:5, :].rearrange("p (l a) k -> p l (a k)", l=2), Wm1.rearrange("l o k -> o l k")),
                         (nat[:, 5:9, :].rearrange("p (l a) k -> p l (a k)", l=2), Wu.rearrange("l o k -> o l k")),
                         (gates[:, 0, :], W0), (gates[:, 1, :], W1),
                         (cols[:, 0:1], b_enc.rearrange("(p a) -> p a", a=1)),
                         (cols[:, 1:2], gamma[0, :].rearrange("(p a) -> p a", a=1)),
                         (cols[:, 2:3], gamma[1, :].rearrange("(p a) -> p a", a=1)),
                         (cols[:, 3:4], beta[0, :].rearrange("(p a) -> p a", a=1)),
                         (cols[:, 4:5], beta[1, :].rearrange("(p a) -> p a", a=1)),
                         (cols[:, 5:6], bm2[0, :].rearrange("(p a) -> p a", a=1)),
                         (cols[:, 6:7], bm2[1, :].rearrange("(p a) -> p a", a=1)),
                         (rows[:, 0, :], flat(bm1[0, :], D)), (rows[:, 1, :], flat(bm1[1, :], D)),
                         (rows[:, 2, :], flat(bu[0, :], D)), (rows[:, 3, :], flat(bu[1, :], D)),
                         (rows[:, 4, :], flat(b_out, D)),
                         (rows[:, 5, 0:64], flat(b0, 64)), (rows[:, 5, 64:D], flat(b1, 64)),
                         (rows[:, 6, 0:64], flat(fc0.rearrange("a b -> (a b)"), 64)),
                         (rows[:, 6, 64:D], flat(fc1.rearrange("a b -> (a b)"), 64)),
                         (bfs[:, 0:1], flat(bf0, 1)), (bfs[:, 1:2], flat(bf1, 1))):
                sp.dma_start(t, s).then_inc(s_load, 16)
                n += 1
            assert n == LOADS + 1
            sp.wait_ge(s_fill, 3)
            for t, s in ((raw[:, 0, :], src), (raw[:, 1, :], dst), (raw_w[:, :], edge_weight)):
                sp.dma_start(t[0:FULL, :], s[0:FULL * T].rearrange("(p t) -> p t", t=T)).then_inc(s_edge, 16)
                sp.dma_start(t[FULL:FULL + 1, 0:REST], s[FULL * T:E].rearrange("(a t) -> a t", a=1))\
                  .then_inc(s_edge, 16)
            for tab in (msg_sum, hop1, hop2):
                v = tab.rearrange("(p a j) c -> p a (j c)", p=P, j=ZROWS)
                for a in range(TR // (P * ZROWS)):
                    sp.dma_start(v[:, a, :], zeros[:, :]).then_inc(s_zero, 16)
            sort_load(sp, low_pass, by_low)
            sort_load(sp, high_pass, by_src)
            edge_sync(sp, e0)
            dense_sync(sp, d1, [(x, xin, D), (msg_sum, rin, W)], n1_table)
            sp.sem_inc(s_sorted, 1)
            edge_sync(sp, e1)
            dense_sync(sp, d2, [(x, xin, D), (n1_table, hin, D), (msg_sum, rin, W)], x1_table)
            sp.sem_inc(s_sorted, 1)
            edge_sync(sp, e2)
            sp.sem_inc(s_sorted, 1)
            edge_sync(sp, e3)
            dense_sync(sp, d3, [(x1_table, xin, D), (hop1, hin, W), (hop2, rin, W)], out)

        @block.gpsimd
        def _(pool):
            pool.memset(ident[:, :], 0.0).then_inc(s_c0, 1)
            pool.memset(ones[:, :], 1.0).then_inc(s_c0, 1)
            pool.iota(digits_i[:, :], pattern=[[1, DIGIT]], base=0, channel_multiplier=0).then_inc(s_const, 1)
            pool.iota(part_i[:, :], pattern=[[1, 1]], base=0, channel_multiplier=1).then_inc(s_const, 1)
            pool.wait_ge(s_c0, 2)
            pool.affine_select(out=ident[:, :], in_=ident[:, :], compare_op=ALU.not_equal, fill=1.0,
                               base=0, pattern=[[-1, P]], channel_multiplier=1).then_inc(s_const, 1)
            pool.affine_select(out=before[:, :], in_=ones[:, :], compare_op=ALU.is_gt, fill=0.0,
                               base=0, pattern=[[1, P]], channel_multiplier=-1).then_inc(s_const, 1)
            pool.affine_select(out=upto[:, :], in_=ones[:, :], compare_op=ALU.is_ge, fill=0.0,
                               base=0, pattern=[[1, P]], channel_multiplier=-1).then_inc(s_const, 1)
            sort_pool(pool, low_pass, by_low)
            sort_pool(pool, high_pass, by_src)
            pool.wait_ge(s_zero, 16 * 3 * (TR // (P * ZROWS)))
            edge_pool(pool, e0)
            pool.wait_ge(s_sorted, 1)
            edge_pool(pool, e1)
            pool.wait_ge(s_sorted, 2)
            edge_pool(pool, e2)
            pool.wait_ge(s_sorted, 3)
            edge_pool(pool, e3)

        @block.scalar
        def _(act):
            act.wait_ge(s_wt, 1)
            act.activation(wT[:, :, :], ps[:, 0:3, :].rearrange("p b n -> p (b n)")[:, 0:9 * D]
                           .rearrange("p (k n) -> p k n", k=9), ACT.Copy).then_inc(s_wte, 1)
            act.wait_ge(s_wm, 1)
            act.activation(ww[:, :, :], ps[:, 4:8, :].rearrange("p b n -> p (b n)")
                           .rearrange("p (k n) -> p k n", k=16), ACT.Copy).then_inc(s_wme, 1)
            edge_scalar(act, e0)
            update_scalar(act, d1, False)
            edge_scalar(act, e1)
            update_scalar(act, d2, True)
            edge_scalar(act, e2)
            edge_scalar(act, e3)
            final_scalar(act, d3)

        @block.tensor
        def _(pe):
            pe.wait_ge(s_load, 16 * (LOADS + 1))
            pe.wait_ge(s_const, 5)
            for k in range(9):
                last = pe.transpose(ps[:, k // 4, (k % 4) * P:(k % 4 + 1) * P], nat[:, 1 + k, :], ident[:, :])
            last.then_inc(s_wt, 1)
            pe.wait_ge(s_wte, 1)
            pe.wait_ge(s_wd, 1)

            def product(k, pairs):
                for m, (a, b) in enumerate(pairs):
                    last = pe.matmul(ps[:, 4 + k // 4, (k % 4) * P:(k % 4 + 1) * P], a, b,
                                     start=(m == 0), stop=(m == len(pairs) - 1))
                return last

            for l in range(2):
                front = nat[:, 0, :] if l == 0 else scaleL[:, 0, :]
                shift = colsB[:, l, :]
                wa, wb, ua, u = wT[:, 2 * l, :], wT[:, 2 * l + 1, :], wT[:, 5 + 2 * l, :], resid[:, l, :]
                product(7 * l + 0, [(front, wa)])
                product(7 * l + 1, [(front, wb)])
                product(7 * l + 2, [(shift, wa), (shift, wb)])
                product(7 * l + 3, [(front, u)])
                product(7 * l + 4, [(shift, u)])
                product(7 * l + 5, [(nat[:, 10 + l, :], ua)])
                product(7 * l + 6, [(colsB[:, 3 + l, :], ua)])
            product(14, [(scaleL[:, 1, :], wT[:, 8, :])])
            product(15, [(colsB[:, 2, :], wT[:, 8, :])]).then_inc(s_wm, 1)
            pe.wait_ge(s_wdone, 1)
            sort_tensor(pe, low_pass)
            sort_tensor(pe, high_pass)
            prep_tensor(pe, by_dst_set, dst_prep)
            prep_tensor(pe, by_src_set, src_prep)
            edge_tensor(pe, e0)
            update_tensor(pe, d1, xin, 2, 0, False)
            edge_tensor(pe, e1)
            update_tensor(pe, d2, hin, 3, 1, True)
            edge_tensor(pe, e2)
            edge_tensor(pe, e3)
            final_tensor(pe, d3)

        @block.vector
        def _(dve):
            dve.memset(zeros[:, :], 0.0).then_inc(s_constd, 1)
            dve.memset(raw[:, 0, :], N).then_inc(s_fill, 1)
            dve.memset(raw[:, 1, :], N).then_inc(s_fill, 1)
            dve.memset(raw_w[:, :], 0.0).then_inc(s_fill, 1)
            dve.memset(eps[:, :], EPS)
            dve.memset(zeros_b[:, :], 0.0)
            dve.memset(cntT[:, :, :, :], 1.0)
            dve.wait_ge(s_const, 5)
            dve.tensor_copy(ident_b[:, :], ident[:, :])
            dve.tensor_copy(ones_b[:, :], ones[:, :])
            dve.tensor_copy(before_b[:, :], before[:, :])
            link(dve, dve.tensor_tensor(notbefore_b[:, :], ones[:, :], before[:, :], ALU.subtract))
            dve.tensor_copy(digits_b[:, :], digits_i[:, :])
            dve.tensor_scalar(head_row[:, :], part_i[:, :], float(HEAD), None, ALU.add)
            link(dve, dve.tensor_scalar(tail_row[:, :], part_i[:, :], float(TAIL), None, ALU.add))
            dve.wait_ge(s_load, 16 * (LOADS + 1))
            for k, c in enumerate((0, 3, 4, 5, 6)):
                dve.tensor_scalar(colsB[:, k, :], ones[:, :], cols[:, c:c + 1], None, ALU.mult)
            for k in range(2):
                dve.tensor_scalar(scaleL[:, k, :], ident[:, :], cols[:, 1 + k:2 + k], None, ALU.mult)
            dve.wait_ge(s_wte, 1)
            for l in range(2):
                last = dve.tensor_tensor(resid[:, l, :], ident[:, :], wT[:, 4 + 2 * l, :], ALU.add)
            last.then_inc(s_wd, 1)
            dve.wait_ge(s_wme, 1)
            for k, r in ((2, 0), (9, 1), (4, 2), (11, 3), (15, 4)):
                link(dve, dve.tensor_tensor(ww[:, k, :], ww[:, k, :], rows[:, r, :], ALU.add))
            for l in range(2):
                link(dve, dve.tensor_tensor(bias5[:, l, :, :], ident[0:5, 0:QUAD].unsqueeze(2)
                                            .to_broadcast([5, QUAD, D]),
                                            ww[0:5, 7 * l + 6, :].unsqueeze(1).to_broadcast([5, QUAD, D]), ALU.mult))
                link(dve, dve.scalar_tensor_tensor(
                    out=bias5[:, l, :, :], in0=ww[0:5, 7 * l + 4, :].unsqueeze(1).to_broadcast([5, QUAD, D]),
                    scalar=ident[0:5, QUAD:QUAD + 1], in1=bias5[:, l, :, :], op0=ALU.mult, op1=ALU.add))
            dve.sem_inc(s_wdone, 1)
            dve.wait_ge(s_edge, 16 * 6)
            link(dve, dve.memset(edges[:, :, 3], 0.0))
            link(dve, dve.tensor_copy(edges[:, :, 0], raw[:, 0, :]))
            link(dve, dve.tensor_scalar(edges[:, :, 1], raw[:, 1, :], float(N - 1), None, ALU.min))
            link(dve, dve.tensor_copy(edges[:, :, 2], raw_w[:, :]))
            for k in range(2):
                link(dve, dve.tensor_scalar(by_dst_set.gat[:, k, :], raw[:, k, :], float(N - 1), None, ALU.min))
            sort_vector(dve, low_pass, 0, True)
            dve.wait_ge(low_pass.loaded, 16)
            sort_vector(dve, high_pass, 8, False)
            link(dve, dve.tensor_copy(keyf[:, :], raw[:, 1, :]))
            prep_vector(dve, by_dst_set, dst_prep)
            dve.wait_ge(high_pass.loaded, 16)
            link(dve, dve.tensor_copy(keyf[:, :], edges[:, :, 0]))
            link(dve, dve.tensor_copy(by_src_set.gat[:, 1, :], edges[:, :, 1]))
            link(dve, dve.tensor_copy(wcol[:, :], edges[:, :, 2]))
            prep_vector(dve, by_src_set, src_prep)
            edge_vector(dve, e0)
            update_vector(dve, d1, False)
            edge_vector(dve, e1)
            update_vector(dve, d2, True)
            edge_vector(dve, e2)
            edge_vector(dve, e3)
            final_vector(dve, d3)


_INS = ["x", "src", "dst", "edge_weight", "L0_gnn_W_enc", "L0_gnn_b_enc", "L0_gnn_Wm1", "L0_gnn_bm1",
        "L0_gnn_Wm2", "L0_gnn_bm2", "L0_gnn_Wu", "L0_gnn_bu", "L0_gnn_gamma", "L0_gnn_beta", "L0_gnn_W_out",
        "L0_gnn_b_out", "L1_gnn_W0", "L1_gnn_b0", "L1_gnn_W1", "L1_gnn_b1", "L1_gnn_fc0", "L1_gnn_bf0",
        "L1_gnn_fc1", "L1_gnn_bf1"]
_OUTS = [((50000, 128), "float32")]


def kernel(**inputs):
    import numpy as _np
    import concourse.bacc as _bacc
    from concourse import mybir as _mybir
    from concourse.bass_utils import run_bass_kernel_spmd as _run

    nc = _bacc.Bacc("TRN2", target_bir_lowering=False, num_devices=1)
    arrays, args = {}, []
    for name in _INS:
        a = _np.ascontiguousarray(inputs[name])
        arrays[f"in_{name}_dram"] = a
        args.append(nc.dram_tensor(f"in_{name}_dram", a.shape, _mybir.dt.from_np(a.dtype), kind="ExternalInput").ap())
    for i, (shape, dtype) in enumerate(_OUTS):
        dt = _mybir.dt.from_np(_np.dtype(dtype))
        args.append(nc.dram_tensor(f"out_{i}_dram", shape, dt, kind="ExternalOutput").ap())
    graph_kernel(nc, *args)
    r = _run(nc, [arrays], core_ids=[0])
    got = tuple(r.results[0][f"out_{i}_dram"] for i in range(len(_OUTS)))
    return got[0]
```

```python
from contextlib import ExitStack

import concourse.bass as bass
from concourse import mybir

F32 = mybir.dt.float32
BF16 = mybir.dt.bfloat16
I32 = mybir.dt.int32
ALU = mybir.AluOpType
ACT = mybir.ActivationFunctionType
AX = mybir.AxisListType



P = 128
D = 128
W = D + 1
EPS = 1e-5
BATCH = 7
SKIP = 1 << 17
DIGIT = 256
QUAD = 4
RING = 4


def graph_kernel(nc, x, src, dst, edge_weight, W_enc, b_enc, Wm1, bm1, Wm2, bm2, Wu, bu, gamma, beta,
                 W_out, b_out, W0, b0, W1, b1, fc0, bf0, fc1, bf1, out):
    N = x.shape[0]
    E = src.shape[0]
    T = -(-E // (P * 2 * BATCH)) * 2 * BATCH
    IT = T // (2 * BATCH)
    FULL = E // T
    REST = E - FULL * T
    HEAD = N + 1
    TAIL = HEAD + P
    ZROWS = 33
    TR = -(-(TAIL + P) // (P * ZROWS)) * P * ZROWS
    ZDMAS = TR // (P * ZROWS)
    ROWS = QUAD * P
    UNITS = -(-N // ROWS)
    LAST = N - ROWS
    assert T < DIGIT and N < DIGIT * DIGIT

    with ExitStack() as ctx:
        def sb(name, shape, dt=F32):
            return ctx.enter_context(nc.sbuf_tensor(name, shape, dt))

        def sem(name):
            return ctx.enter_context(nc.semaphore(name))

        def dram(name, shape):
            return nc.dram_tensor(name, shape, F32, kind="Internal").ap()

        msg_sum = dram("msg_sum", [TR, W])
        hop1 = dram("hop1", [TR, W])
        hop2 = dram("hop2", [TR, W])
        n1_table = dram("n1_table", [N, D])
        x1_table = dram("x1_table", [N, D])
        by_low = dram("by_low", [P * T, 4])
        by_src = dram("by_src", [P * T, 4])

        ident = sb("ident", [P, P])
        ones = sb("ones", [P, P])
        before = sb("before", [P, P])
        upto = sb("upto", [P, P])
        ident_b = sb("ident_b", [P, P], BF16)
        ones_b = sb("ones_b", [P, P], BF16)
        before_b = sb("before_b", [P, P], BF16)
        notbefore_b = sb("notbefore_b", [P, P], BF16)
        digits_i = sb("digits_i", [P, DIGIT], I32)
        digits_b = sb("digits_b", [P, DIGIT], BF16)
        part_i = sb("part_i", [P, 1], I32)
        head_row = sb("head_row", [P, 1])
        tail_row = sb("tail_row", [P, 1])
        eps = sb("eps", [P, 1])
        zeros = sb("zeros", [P, ZROWS * W])

        nat = sb("nat", [P, 12, D])
        wT = sb("wT", [P, 9, D])
        gates = sb("gates", [P, 2, 64])
        cols = sb("cols", [P, 7])
        rows = sb("rows", [P, 7, D])
        bfs = sb("bfs", [P, 2])
        resid = sb("resid", [P, 2, D])
        scaleL = sb("scaleL", [P, 2, D])
        colsB = sb("colsB", [P, 5, D])
        ww = sb("ww", [P, 16, D])
        bias5 = sb("bias5", [5, 2, QUAD, D])

        raw = sb("raw", [P, 2, T], I32)
        raw_w = sb("raw_w", [P, T])
        edges = sb("edges", [P, T, 4])
        keyf = sb("keyf", [P, T])
        digit_i = sb("digit_i", [P, T], I32)
        digit_f = sb("digit_f", [P, T])
        tmp1 = sb("tmp1", [P, T])
        tmp2 = sb("tmp2", [P, T])

        class EdgeSet:
            def __init__(self, name):
                self.same = sb(f"{name}_same", [P, T])
                self.gat = sb(f"{name}_gat", [P, 2, T], I32)
                self.sca = sb(f"{name}_sca", [P, T], I32)
                self.hk = sb(f"{name}_hk", [P, 2])
                self.eq = sb(f"{name}_eq", [P, 4, P])
                self.widx = sb(f"{name}_widx", [P, 2], I32)

        by_dst_set = EdgeSet("dst")
        by_src_set = EdgeSet("src")
        wcol = sb("wcol", [P, T])
        merge_f = sb("merge_f", [P, 4, P])
        merge_d = sb("merge_d", [P, 2, P])
        merge_w = sb("merge_w", [P, 2])

        hot = sb("hot", [P, 2, BATCH, DIGIT], BF16)
        hot_next = sb("hot_next", [P, BATCH, DIGIT], BF16)
        digit_next = sb("digit_next", [P, T])
        positions = sb("positions", [P, T], I32)
        scan = sb("scan", [P, 3, DIGIT])
        base_i = sb("base_i", [P, 2, DIGIT], I32)
        base_f = sb("base_f", [P, 2, DIGIT])
        base_b = sb("base_b", [P, 2, DIGIT], BF16)
        junk = sb("junk", [P, DIGIT])
        rank = sb("rank", [P, 2, BATCH])
        rank_i = sb("rank_i", [P, 3, BATCH], I32)
        rank_f = sb("rank_f", [P, 2, BATCH])
        pos = sb("pos", [P, 2, BATCH], I32)
        load4 = sb("load4", [P, 2, BATCH, 4])

        st_gat = sb("st_gat", [P, 2, 2, BATCH], I32)
        st_sca = sb("st_sca", [P, 2, BATCH], I32)
        got = sb("got", [P, 2, 2, BATCH, W])
        gT = sb("gT", [P, 2, BATCH, P])
        pre = sb("pre", [P, BATCH, D])
        msg = sb("msg", [P, BATCH, W])
        run = sb("run", [P, 2, BATCH, W])
        part = sb("part", [P, 2, W])
        merged = sb("merged", [P, 2, W])

        xin = sb("xin", [P, RING, QUAD, D])
        hin = sb("hin", [P, RING, QUAD, W])
        rin = sb("rin", [P, RING, QUAD, W])
        res = sb("res", [P, RING, QUAD, D])
        aT = sb("aT", [P, 2, 2, QUAD, P])
        cntT = sb("cntT", [5, 2, P])
        stats = sb("stats", [P, 2, 2, QUAD, 6])
        mv = sb("mv", [P, 2, 2, QUAD, 2])
        sd = sb("sd", [P, 2, 2, QUAD])
        rstd = sb("rstd", [P, 2, 2, QUAD])
        n2 = sb("n2", [P, 2, QUAD, D])
        n2T = sb("n2T", [P, 2, QUAD, P])
        vout = sb("vout", [P, 2, QUAD, D])
        dg = sb("dg", [P, RING, 4, QUAD, 2])
        yy = sb("yy", [P, 2, 3, QUAD, D])
        tt = sb("tt", [P, 2, 3, QUAD, 2])
        b3f = sb("b3f", [1, 3, D])
        b3b = sb("b3b", [1, 3, QUAD, D], BF16)

        ps = ctx.enter_context(nc.psum_tensor("ps", [P, 8, 512], F32))

        s_load = sem("s_load")
        s_edge = sem("s_edge")
        s_fill = sem("s_fill")
        s_zero = sem("s_zero")
        s_zero2 = sem("s_zero2")
        s_c0 = sem("s_c0")
        s_const = sem("s_const")
        s_constd = sem("s_constd")
        s_wt = sem("s_wt")
        s_wte = sem("s_wte")
        s_wd = sem("s_wd")
        s_wm = sem("s_wm")
        s_wme = sem("s_wme")
        s_wdone = sem("s_wdone")
        s_dve = sem("s_dve")

        linked = [0]

        def link(dve, ins):
            linked[0] += 1
            ins.then_inc(s_dve, 1)
            dve.wait_ge(s_dve, linked[0])

        s_waited = sem("s_waited")

        def own_wait(eng):
            eng.sem_inc(s_waited, 1)

        LOADS = 24

        def flat(v, n):
            return v.rearrange("(a n) -> a n", a=1).to_broadcast([P, n])

        class SortPass:
            def __init__(self, name):
                self.hot1 = sem(f"{name}_hot1")
                self.used1 = sem(f"{name}_used1")
                self.total = sem(f"{name}_total")
                self.based = sem(f"{name}_based")
                self.hot2 = sem(f"{name}_hot2")
                self.prefix = sem(f"{name}_prefix")
                self.ranked = sem(f"{name}_ranked")
                self.used2 = sem(f"{name}_used2")
                self.placed = sem(f"{name}_placed")
                self.staged = sem(f"{name}_staged")
                self.sent = [sem(f"{name}_sent{h}") for h in range(2)]
                self.loaded = sem(f"{name}_loaded")
                self.chain = sem(f"{name}_chain")

        low_pass, high_pass = SortPass("low"), SortPass("high")
        s_whole = sem("s_whole")

        counts = ps[:, 7, 0:DIGIT]
        next_total = ps[:, 7, DIGIT:2 * DIGIT]

        def digits(dve, target, shift):
            link(dve, dve.tensor_copy(digit_i[:, :], edges[:, :, 0]))
            if shift:
                link(dve, dve.tensor_scalar(digit_i[:, :], digit_i[:, :], shift, None, ALU.logical_shift_right))
            else:
                link(dve, dve.tensor_scalar(digit_i[:, :], digit_i[:, :], DIGIT - 1, None, ALU.bitwise_and))
            link(dve, dve.tensor_copy(target[:, :], digit_i[:, :]))

        def make_hot(dve, target, digit, t):
            for j in range(BATCH):
                ins = dve.tensor_scalar(target[:, j, :], digits_b[:, :], digit[:, bass.ds(t + j, 1)], None,
                                        ALU.is_equal)
            return ins

        def totals_vector(dve, ph):
            with dve.Fori(0, IT) as i:
                for h in range(2):
                    dve.wait_ge(ph.used1, i * 2 + h + 1)
                    make_hot(dve, hot[:, h], digit_f, i * (2 * BATCH) + h * BATCH).then_inc(ph.hot1, 1)

        def totals_tensor(pe, ph):
            for h in range(2):
                pe.matmul(ps[:, 7, :], ones_b[:, :], zeros_b[:, :], start=(h == 0), stop=False,
                          skip_group_check=True).then_inc(ph.used1, 1)
            with pe.Fori(0, IT) as i:
                for h in range(2):
                    pe.wait_ge(ph.hot1, i * 2 + h + 1)
                    for j in range(BATCH):
                        last = pe.matmul(counts, ones_b[:, :], hot[:, h, j, :], start=False, stop=False,
                                         skip_group_check=True)
                    last.then_inc(ph.used1, 1)
            pe.matmul(counts, ones_b[:, :], zeros_b[:, 0:DIGIT], start=False, stop=False,
                      skip_group_check=True).then_inc(ph.total, 1)

        def bases_vector(dve, ph, total):
            dve.wait_ge(ph.total, 1)
            link(dve, dve.tensor_copy(scan[:, 0, :], total))
            link(dve, dve.tensor_copy(scan[:, 1, :], scan[:, 0, :]))
            a, b, s = 1, 2, 1
            while s < DIGIT:
                dve.tensor_copy(scan[:, b, 0:s], scan[:, a, 0:s])
                link(dve, dve.tensor_tensor(scan[:, b, s:], scan[:, a, s:], scan[:, a, 0:DIGIT - s], ALU.add))
                a, b, s = b, a, 2 * s
            link(dve, dve.tensor_tensor(scan[:, b, :], scan[:, a, :], scan[:, 0, :], ALU.subtract))
            link(dve, dve.tensor_copy(base_i[:, 0, :], scan[:, b, :]))
            link(dve, dve.tensor_scalar(base_i[:, 1, :], base_i[:, 0, :], P - 1, None, ALU.bitwise_and))
            link(dve, dve.tensor_copy(base_f[:, 1, :], base_i[:, 1, :]))
            link(dve, dve.tensor_tensor(base_f[:, 0, :], scan[:, b, :], base_f[:, 1, :], ALU.subtract))
            dve.tensor_copy(base_b[:, 0, :], base_f[:, 0, :]).then_inc(ph.based, 1)
            dve.tensor_copy(base_b[:, 1, :], base_f[:, 1, :]).then_inc(ph.based, 1)

        def bases_tensor(pe, ph):
            pe.wait_ge(ph.based, 2)
            pe.matmul(ps[:, 7, :], ones_b[:, :], zeros_b[:, :], start=True, stop=False, skip_group_check=True)
            for k in range(2):
                pe.matmul(counts, ident_b[:, :], base_b[:, k, :], start=False, stop=False, skip_group_check=True)

        def ranks_vector(dve, ph, i, h, first, low):
            t = i * (2 * BATCH) + h * BATCH
            if not first:
                dve.wait_ge(ph.used2, i * 2 + h - 1)
            make_hot(dve, hot[:, h], digit_f, t).then_inc(ph.hot2, 1)
            if low:
                if not (first and h == 0):
                    dve.wait_ge(high_pass.used1, i * 2 + h)
                make_hot(dve, hot_next, digit_next, t).then_inc(high_pass.hot1, 1)
            for j in range(BATCH):
                dve.wait_ge(ph.prefix, i * (2 * BATCH) + h * BATCH + j + 1)
                dve.tensor_tensor_reduce(junk[:, :], counts, hot[:, h, j, :], 1.0, 0.0, ALU.mult, ALU.add,
                                         rank[:, h, j:j + 1]).then_inc(ph.ranked, 1)
            dve.wait_ge(ph.ranked, i * (2 * BATCH) + (h + 1) * BATCH)
            if low:
                done = i * 8 + h * 4
                dve.tensor_copy(rank_i[:, 0, :], rank[:, h, :]).then_inc(ph.chain, 1)
                dve.wait_ge(ph.chain, done + 1)
                dve.tensor_scalar(rank_i[:, 1, :], rank_i[:, 0, :], 7, None, ALU.logical_shift_right)
                dve.tensor_scalar(rank_i[:, 2, :], rank_i[:, 0, :], P - 1, None,
                                  ALU.bitwise_and).then_inc(ph.chain, 1)
                dve.wait_ge(ph.chain, done + 2)
                dve.tensor_copy(rank_f[:, 0, :], rank_i[:, 1, :]).then_inc(ph.chain, 1)
                dve.tensor_copy(rank_f[:, 1, :], rank_i[:, 2, :]).then_inc(ph.chain, 1)
                dve.wait_ge(ph.chain, done + 4)
                dve.scalar_tensor_tensor(out=positions[:, bass.ds(t, BATCH)], in0=rank_f[:, 1, :], scalar=float(T),
                                         in1=rank_f[:, 0, :], op0=ALU.mult, op1=ALU.add).then_inc(ph.placed, 1)
            else:
                dve.tensor_copy(positions[:, bass.ds(t, BATCH)], rank[:, h, :]).then_inc(ph.placed, 1)

        def ranks_tensor(pe, ph, i, h, low):
            pe.wait_ge(ph.hot2, i * 2 + h + 1)
            for j in range(BATCH):
                pe.matmul(counts, before_b[:, :], hot[:, h, j, :], start=False, stop=False,
                          skip_group_check=True).then_inc(ph.prefix, 1)
                pe.wait_ge(ph.ranked, i * (2 * BATCH) + h * BATCH + j + 1)
                last = pe.matmul(counts, notbefore_b[:, :], hot[:, h, j, :], start=False, stop=False,
                                 skip_group_check=True)
            last.then_inc(ph.used2, 1)
            if low:
                pe.wait_ge(high_pass.hot1, i * 2 + h + 1)
                for j in range(BATCH):
                    last = pe.matmul(next_total, ones_b[:, :], hot_next[:, j, :], start=False, stop=False,
                                     skip_group_check=True)
                last.then_inc(high_pass.used1, 1)

        def sort_pool(pool, ph, target):
            pool.wait_ge(ph.placed, 2 * IT)

            def batch(i, h, first):
                t = i * (2 * BATCH) + h * BATCH
                if not first:
                    pool.wait_ge(ph.sent[h], i * (16 * BATCH))
                    own_wait(pool)
                pool.tensor_copy(pos[:, h, :], positions[:, bass.ds(t, BATCH)]).then_inc(ph.staged, 1)
                pool.tensor_copy(load4[:, h, :, :], edges[:, bass.ds(t, BATCH), :]).then_inc(ph.staged, 1)
                pool.wait_ge(ph.staged, i * 4 + 2 * h + 2)
                own_wait(pool)
                for j in range(BATCH):
                    pool.indirect_dma_start(
                        target, bass.IndirectOffsetOnAxis(ap=pos[:, h, j:j + 1], axis=0), load4[:, h, j, :],
                        None, bounds_check=P * T - 1, oob_is_err=False).then_inc(ph.sent[h], 16)

            batch(0, 0, True)
            batch(0, 1, True)
            with pool.Fori(1, IT) as i:
                batch(i, 0, False)
                batch(i, 1, False)

        def sort_load(sp, ph, target):
            for h in range(2):
                sp.wait_ge(ph.sent[h], 16 * BATCH * IT)
            sp.dma_start(edges[:, :, :], target.rearrange("(p t) c -> p t c", t=T)).then_inc(ph.loaded, 16)

        class SetPrep:
            def __init__(self, name):
                self.diag = sem(f"{name}_diag")
                self.keys = sem(f"{name}_keys")
                self.masked = sem(f"{name}_masked")
                self.count = sem(f"{name}_count")

        dst_prep, src_prep = SetPrep("dprep"), SetPrep("sprep")

        def prep_vector(dve, es, ph):
            link(dve, dve.memset(es.same[:, 0:1], 0.0))
            link(dve, dve.tensor_tensor(es.same[:, 1:T], keyf[:, 0:T - 1], keyf[:, 1:T], ALU.is_equal))
            link(dve, dve.tensor_scalar(tmp1[:, :], keyf[:, :], keyf[:, 0:1], None, ALU.is_equal))
            link(dve, dve.tensor_scalar(tmp2[:, :], keyf[:, :], -1.0, head_row[:, 0:1], ALU.mult, ALU.add))
            link(dve, dve.tensor_tensor(tmp1[:, :], tmp1[:, :], tmp2[:, :], ALU.mult))
            link(dve, dve.tensor_tensor(tmp2[:, :], keyf[:, :], tmp1[:, :], ALU.add))
            link(dve, dve.scalar_tensor_tensor(out=tmp2[:, 0:T - 1], in0=es.same[:, 1:T], scalar=float(SKIP),
                                               in1=tmp2[:, 0:T - 1], op0=ALU.mult, op1=ALU.add))
            link(dve, dve.tensor_copy(tmp2[:, T - 1:T], tail_row[:, :]))
            link(dve, dve.tensor_copy(es.sca[:, :], tmp2[:, :]))
            link(dve, dve.tensor_copy(es.hk[:, 0:1], keyf[:, 0:1]))
            link(dve, dve.tensor_copy(es.hk[:, 1:2], keyf[:, T - 1:T]))
            for b in range(2):
                dve.tensor_scalar(merge_d[:, b, :], ident[:, :], es.hk[:, b:b + 1], None,
                                  ALU.mult).then_inc(ph.diag, 1)
            dve.wait_ge(ph.keys, 1)
            for a in range(2):
                for b in range(2):
                    link(dve, dve.tensor_scalar(es.eq[:, 2 * a + b, :], ps[:, 6, b * P:(b + 1) * P],
                                                es.hk[:, a:a + 1], None, ALU.is_equal))
                    earlier = upto if (a, b) == (0, 1) else before
                    dve.tensor_tensor(merge_f[:, 2 * a + b, :], es.eq[:, 2 * a + b, :], earlier[:, :],
                                      ALU.mult).then_inc(ph.masked, 1)
            dve.wait_ge(ph.count, 1)
            link(dve, dve.tensor_scalar(merge_w[:, :], ps[:, 6, 2 * P:2 * P + 2], 0.0, float(SKIP), ALU.is_gt, ALU.mult))
            link(dve, dve.tensor_tensor(es.widx[:, :], merge_w[:, :], es.hk[:, :], ALU.add))

        def prep_tensor(pe, es, ph):
            pe.wait_ge(ph.diag, 2)
            for b in range(2):
                last = pe.matmul(ps[:, 6, b * P:(b + 1) * P], ones[:, :], merge_d[:, b, :], start=True, stop=True)
            last.then_inc(ph.keys, 1)
            pe.wait_ge(ph.masked, 4)
            for b in range(2):
                for a in range(2):
                    last = pe.matmul(ps[:, 6, 2 * P + b:2 * P + b + 1], merge_f[:, 2 * a + b, :], ones[:, 0:1],
                                     start=(a == 0), stop=(a == 1))
            last.then_inc(ph.count, 1)

        s_parts, s_joined, s_joinedc, s_stored = sem("parts"), sem("joined"), sem("joinedc"), sem("stored")

        class EdgePhase:

            def __init__(self, turn, es, table, gathers, layer, sorting):
                self.sorting = sorting
                name = f"e{turn}"
                self.turn, self.es, self.table, self.gathers, self.layer = turn, es, table, gathers, layer
                self.n = BATCH * len(gathers)
                self.staged = sem(f"{name}_staged")
                self.gat = [sem(f"{name}_gat{h}") for h in range(2)]
                self.used = sem(f"{name}_used")
                if layer is not None:
                    self.turned = sem(f"{name}_turned")
                    self.copied = sem(f"{name}_copied")
                    self.mixed = sem(f"{name}_mixed")
                    self.added = sem(f"{name}_added")
                self.messages = sem(f"{name}_messages")
                self.chain = sem(f"{name}_chain")
                self.summed = sem(f"{name}_summed")
                self.sent = [sem(f"{name}_sent{h}") for h in range(2)]
                self.parts, self.joined, self.joinedc, self.stored = s_parts, s_joined, s_joinedc, s_stored

        def edge_pool(pool, ph):
            es = ph.es

            def gather(i, h, first):
                pool.wait_ge(ph.staged, i * 2 + h + 1)
                if not first:
                    pool.wait_ge(ph.used, i * 2 + h - 1)
                own_wait(pool)
                for g, (tab, row, c) in enumerate(ph.gathers):
                    for j in range(BATCH):
                        pool.indirect_dma_start(
                            got[:, h, g, j, 0:c], None, tab,
                            bass.IndirectOffsetOnAxis(ap=st_gat[:, h, g, j:j + 1], axis=0),
                            bounds_check=N - 1, oob_is_err=False).then_inc(ph.gat[h], 16)

            def scatter(n, h):
                pool.wait_ge(ph.summed, n + 1)
                own_wait(pool)
                for j in range(BATCH):
                    pool.indirect_dma_start(
                        ph.table, bass.IndirectOffsetOnAxis(ap=st_sca[:, h, j:j + 1], axis=0), run[:, h, j, :],
                        None, bounds_check=TR - 1, oob_is_err=False).then_inc(ph.sent[h], 16)

            gather(0, 0, True)
            gather(0, 1, True)
            if ph.turn == 0:
                pool.wait_ge(s_zero, 16 * ZDMAS)
            scatter(0, 0)
            with pool.Fori(1, IT) as i:
                gather(i, 0, False)
                scatter(i * 2 - 1, 1)
                gather(i, 1, False)
                scatter(i * 2, 0)
            scatter(2 * IT - 1, 1)
            pool.wait_ge(ph.joinedc, ph.turn + 1)
            for b in range(2):
                pool.indirect_dma_start(
                    ph.table, bass.IndirectOffsetOnAxis(ap=es.widx[:, b:b + 1], axis=0), merged[:, b, :],
                    None, bounds_check=TR - 1, oob_is_err=False).then_inc(ph.stored, 16)

        def edge_tensor(pe, ph):
            es = ph.es

            def batch(i, h, first):
                pe.wait_ge(ph.gat[h], i * (16 * ph.n) + 16 * ph.n)
                if not first:
                    pe.wait_ge(ph.copied, i * 4 + 2 * h)
                for g in range(2):
                    for j in range(BATCH):
                        last = pe.transpose(turned[g][:, j, :], got[:, h, g, j, 0:D], ident[:, :])
                    last.then_inc(ph.turned, 1)
                pe.wait_ge(ph.turned, i * 4 + 2 * h + 2)
                pe.wait_ge(ph.copied, i * 4 + 2 * h + 2)
                if not first:
                    pe.wait_ge(ph.added, i * 2 + h)
                for j in range(BATCH):
                    for g in range(2):
                        last = pe.matmul(mixed[:, j, :], gT[:, g, j, :], ww[:, 7 * ph.layer + g, :],
                                         start=(g == 0), stop=(g == 1))
                last.then_inc(ph.mixed, 1)
                if ph.sorting is not None:
                    ranks_tensor(pe, ph.sorting, i, h, ph.layer == 0)

            if ph.layer is not None:
                batch(0, 0, True)
                batch(0, 1, False)
                with pe.Fori(1, IT) as i:
                    batch(i, 0, False)
                    batch(i, 1, False)
            pe.wait_ge(ph.parts, 16 * (ph.turn + 1))
            for b in range(2):
                for a in range(2):
                    last = pe.matmul(ps[:, 6, b * 256:b * 256 + W], es.eq[:, 2 * a + b, :], part[:, a, :],
                                     start=(a == 0), stop=(a == 1))
            last.then_inc(ph.joined, 1)

        turned = [ps[:, 2 * g:2 * g + 2, :].rearrange("p b n -> p (b n)")[:, 0:BATCH * P]
                  .rearrange("p (j e) -> p j e", j=BATCH) for g in range(2)]
        mixed = ps[:, 4:6, :].rearrange("p b n -> p (b n)")[:, 0:BATCH * D].rearrange("p (j e) -> p j e", j=BATCH)

        def edge_scalar(act, ph):
            def batch(i, h, first):
                if ph.layer is not None:
                    for g in range(2):
                        act.wait_ge(ph.turned, i * 4 + 2 * h + g + 1)
                        if not first:
                            act.wait_ge(ph.mixed, i * 2 + h)
                        ins = act.activation(gT[:, g, :, :], turned[g], ACT.Copy).then_inc(ph.copied, 1)
                    act.wait_ge(ph.added, i * 2 + h + 1)
                    if not first:
                        act.wait_ge(ph.summed, i * 2 + h)
                    act.activation(msg[:, :, 0:D], pre[:, :, :], ACT.Relu).then_inc(ph.messages, 1)
                else:
                    act.wait_ge(ph.gat[h], i * (16 * ph.n) + 16 * ph.n)
                    if not first:
                        act.wait_ge(ph.summed, i * 2 + h)
                    for j in range(BATCH):
                        last = act.activation(msg[:, j, :], got[:, h, 0, j, :], ACT.Copy,
                                              scale=wcol[:, bass.ds(i * (2 * BATCH) + h * BATCH + j, 1)])
                    last.then_inc(ph.messages, 1)

            batch(0, 0, True)
            batch(0, 1, False)
            with act.Fori(1, IT) as i:
                batch(i, 0, False)
                batch(i, 1, False)

        def edge_vector(dve, ph):
            es = ph.es

            def stage(i, h):
                t = i * (2 * BATCH) + h * BATCH
                dve.tensor_copy(st_gat[:, h, 0:len(ph.gathers), :],
                                es.gat[:, 2 - len(ph.gathers):2, bass.ds(t, BATCH)]).then_inc(ph.staged, 1)

            def batch(i, h, first, ahead):
                t = i * (2 * BATCH) + h * BATCH
                if ph.layer is not None:
                    dve.wait_ge(ph.mixed, i * 2 + h + 1)
                    if not first:
                        dve.wait_ge(ph.messages, i * 2 + h)
                    dve.tensor_tensor(pre[:, :, :], mixed, ww[:, 7 * ph.layer + 2, :].unsqueeze(1)
                                      .to_broadcast([P, BATCH, D]), ALU.add).then_inc(ph.added, 1)
                dve.wait_ge(ph.messages, i * 2 + h + 1)
                dve.wait_ge(ph.gat[h], i * (16 * ph.n) + 16 * ph.n)
                dve.sem_inc(ph.used, 1)
                if ahead:
                    stage(i + 1, h)
                if i is not 0:
                    dve.wait_ge(ph.sent[h], i * (16 * BATCH))
                dve.tensor_copy(st_sca[:, h, :], es.sca[:, bass.ds(t, BATCH)])
                for j in range(BATCH):
                    last = run[:, 1 - h, BATCH - 1, :] if j == 0 else run[:, h, j - 1, :]
                    ins = dve.scalar_tensor_tensor(out=run[:, h, j, :], in0=last,
                                                   scalar=es.same[:, bass.ds(t + j, 1)], in1=msg[:, j, :],
                                                   op0=ALU.mult, op1=ALU.add)
                    ins.then_inc(ph.chain, 1)
                    dve.wait_ge(ph.chain, i * (2 * BATCH) + h * BATCH + j + 1)
                dve.sem_inc(ph.summed, 1)
                if ph.sorting is not None:
                    ranks_vector(dve, ph.sorting, i, h, i is 0, ph.layer == 0)

            link(dve, dve.memset(run[:, 1, BATCH - 1, :], 0.0))
            if ph.layer is not None:
                link(dve, dve.memset(msg[:, :, D:W], 1.0))
            elif ph.gathers[0][2] == D:
                link(dve, dve.memset(got[:, :, 0, :, D:W], 1.0))
            stage(0, 0)
            stage(0, 1)
            batch(0, 0, True, True)
            batch(0, 1, False, True)
            with dve.Fori(1, IT - 1) as i:
                batch(i, 0, False, True)
                batch(i, 1, False, True)
            batch(IT - 1, 0, False, False)
            batch(IT - 1, 1, False, False)
            dve.wait_ge(ph.joined, ph.turn + 1)
            dve.tensor_copy(merged[:, :, :], ps[:, 6, :].rearrange("p (b n) -> p b n", b=2)[:, :, 0:W])\
               .then_inc(ph.joinedc, 1)

        def edge_sync(sp, ph):
            for h in range(2):
                sp.wait_ge(ph.sent[h], 16 * BATCH * IT)
            sp.dma_start(part[:, :, :], ph.table[HEAD:HEAD + 2 * P, :].rearrange("(a p) c -> p a c", a=2))\
              .then_inc(ph.parts, 16)
            sp.wait_ge(ph.stored, 32 * (ph.turn + 1))

        class Unit:

            def __init__(self, i, c):
                self.round = i + c // RING
                self.slot = c % RING
                self.par = c % 2
                self.u = self.round * RING + self.slot
                self.looped = not isinstance(i, int)
                self.base = LAST if not self.looped and self.u == UNITS - 1 else self.u * ROWS

            def after(self, n):
                return self.looped or self.u >= n

        def in_step(eng, stages):
            depth = max(offset for offset, _ in stages)
            first = -(-depth // RING) + 1
            rounds = UNITS // RING

            def straight(steps):
                for s in steps:
                    for offset, stage in stages:
                        if 0 <= s - offset < UNITS:
                            stage(Unit(0, s - offset))

            straight(range(first * RING))
            with eng.Fori(first, rounds) as i:
                for k in range(RING):
                    for offset, stage in stages:
                        stage(Unit(i, k - offset))
            straight(range(rounds * RING, UNITS + depth))

        s_ab = [sem(f"s_ab{r}") for r in range(RING)]
        s_x = [sem(f"s_x{r}") for r in range(RING)]
        s_res = [sem(f"s_res{r}") for r in range(RING)]
        USES = [len(range(r, UNITS, RING)) for r in range(RING)]

        class DensePhase:

            def __init__(self, turn, a, b, target, layer, late_x, gated):
                name = f"d{turn}"
                self.a, self.b, self.target, self.layer, self.late_x = a, b, target, layer, late_x
                self.gated = gated
                self.turn = turn
                self.ab_before = 32 * (turn - 1)
                self.x_before = 16 * max(0, turn - 2)
                self.turned = sem(f"{name}_turned")
                self.copied = sem(f"{name}_copied")
                self.mixed = sem(f"{name}_mixed")
                if not gated:
                    self.stats = sem(f"{name}_stats")
                    self.var = sem(f"{name}_var")
                    self.std = sem(f"{name}_std")
                    self.recip = sem(f"{name}_recip")
                    self.norm = sem(f"{name}_norm")
                if turn > 1:
                    self.stats2 = sem(f"{name}_stats2")
                    self.var2 = sem(f"{name}_var2")
                    self.std2 = sem(f"{name}_std2")
                    self.recip2 = sem(f"{name}_recip2")
                    self.added = sem(f"{name}_added")
                if turn == 2:
                    self.turned2 = sem(f"{name}_turned2")
                    self.copied2 = sem(f"{name}_copied2")
                    self.mixed2 = sem(f"{name}_mixed2")
                if gated:
                    self.degrees = sem(f"{name}_degrees")
                    self.scaled = sem(f"{name}_scaled")
                    self.gate = sem(f"{name}_gate")
                    self.gate_open = sem(f"{name}_gate_open")
                    self.deg_chain = sem(f"{name}_deg_chain")
                    self.joined = sem(f"{name}_joined")
                    self.summed = sem(f"{name}_summed")
                    self.ca = sem(f"{name}_ca")

                self.done = self.norm if turn == 1 else sem(f"{name}_done")

            def ab_ready(self, t):
                return (t.round + 1) * 32 + self.ab_before * USES[t.slot]

            def x_ready(self, t):
                return (t.round + 1) * 16 + self.x_before * USES[t.slot]

            def res_stored(self, t):
                return t.round * 16 + 16 * (self.turn - 1) * USES[t.slot]

        d1 = DensePhase(1, (x, xin, D), (msg_sum, rin, W), n1_table, 0, False, False)
        d2 = DensePhase(2, (n1_table, hin, D), (msg_sum, rin, W), x1_table, 1, (x, xin), False)
        d3 = DensePhase(3, (hop1, hin, W), (hop2, rin, W), out, None, (x1_table, xin), True)

        def node_rows(tab, base, c):
            return tab[bass.ds(base, ROWS), 0:c].rearrange("(p j) c -> p j c", j=QUAD)

        def dense_sync(sp, ph):
            def load(t):
                if t.after(RING):
                    sp.wait_ge(ph.turned, t.u * 2 - (RING - 1) * 2)
                    if ph.gated:
                        own_wait(sp)
                        sp.wait_ge(ph.degrees, t.u - (RING - 1))
                own_wait(sp)
                for tab, tile, c in (ph.a, ph.b):
                    sp.dma_start(tile[:, t.slot, :, 0:c], node_rows(tab, t.base, c)).then_inc(s_ab[t.slot], 16)

            def load_x(t):
                if t.after(RING):
                    sp.wait_ge(ph.added, t.u - (RING - 1))
                own_wait(sp)
                tab, tile = ph.late_x
                sp.dma_start(tile[:, t.slot, :, :], node_rows(tab, t.base, D)).then_inc(s_x[t.slot], 16)

            def store(t):
                sp.wait_ge(ph.done, t.u + 1)
                if not t.looped and t.u == UNITS - 1:
                    r = (UNITS - 2) % RING
                    sp.wait_ge(s_res[r], 16 * ph.turn * USES[r])
                own_wait(sp)
                sp.dma_start(node_rows(ph.target, t.base, D), res[:, t.slot, :, :]).then_inc(s_res[t.slot], 16)

            if ph.turn == 1:
                in_step(sp, [(0, load), (7, store)])
            elif ph.turn == 2:
                in_step(sp, [(0, load), (5, load_x), (11, store)])
            else:
                in_step(sp, [(0, load), (2, load_x), (8, store)])
            for r in range(RING):
                sp.wait_ge(s_res[r], 16 * ph.turn * USES[r])

        def quad(bank):
            return ps[:, bank, :].rearrange("p (j e) -> p j e", j=QUAD)

        def turn_quad(pe, bank, tile):
            for j in range(QUAD):
                last = pe.transpose(quad(bank)[:, j, :], tile[:, j, 0:D], ident[:, :])
            return last

        def dense_tensor(pe, ph):
            def transposes(t):
                pe.wait_ge(s_ab[t.slot], ph.ab_ready(t))
                if t.after(1):
                    pe.wait_ge(ph.copied, t.u * (2 if ph.gated else 3))
                turn_quad(pe, 0, ph.a[1][:, t.slot]).then_inc(ph.turned, 1)
                last = turn_quad(pe, 1, ph.b[1][:, t.slot])
                if not ph.gated:
                    last = pe.transpose(ps[0:QUAD, 2, 0:P], rin[:, t.slot, :, D], ident[:, :])
                last.then_inc(ph.turned, 1)

            def products(t):
                pe.wait_ge(ph.copied, t.u * 3 + 3)
                if t.after(2):
                    pe.wait_ge(ph.norm, t.u - 1)
                acc = ps[:, 3 + t.par, :]
                for j in range(QUAD):
                    pe.matmul(acc[:, j * P:(j + 1) * P], aT[:, t.par, 0, j, :], ww[:, 7 * ph.layer + 3, :],
                              start=(j == 0), stop=False, skip_group_check=True)
                    pe.matmul(acc[:, j * P:(j + 1) * P], aT[:, t.par, 1, j, :], ww[:, 7 * ph.layer + 5, :],
                              start=False, stop=False, skip_group_check=True)
                pe.matmul(acc, cntT[0:5, t.par, :], bias5[:, ph.layer, :, :], start=False, stop=True,
                          skip_group_check=True).then_inc(ph.mixed, 1)

            def gated_products(t):
                pe.wait_ge(ph.copied, t.u * 2 + 2)
                if t.after(2):
                    pe.wait_ge(ph.scaled, t.u - 1)
                for j in range(QUAD):
                    for g in range(2):
                        last = pe.matmul(ps[:, 3 + t.par, j * P + 64 * g:j * P + 64 * (g + 1)],
                                         aT[:, t.par, g, j, :], gates[:, g, :], start=True, stop=True)
                last.then_inc(ph.mixed, 1)

            def transposes2(t):
                pe.wait_ge(ph.norm, t.u + 1)
                if t.after(1):
                    pe.wait_ge(ph.copied2, t.u)
                turn_quad(pe, 5, n2[:, t.par]).then_inc(ph.turned2, 1)

            def products2(t):
                pe.wait_ge(ph.copied2, t.u + 1)
                if t.after(2):
                    pe.wait_ge(ph.added, t.u - 1)
                acc = ps[:, 6 + t.par, :]
                for k in range(3):
                    pe.matmul(acc, ones_b[0:1, :], b3b[:, k, :, :], start=(k == 0), stop=False,
                              skip_group_check=True)
                for j in range(QUAD):
                    last = pe.matmul(acc[:, j * P:(j + 1) * P], n2T[:, t.par, j, :], ww[:, 14, :],
                                     start=False, stop=(j == QUAD - 1), skip_group_check=True)
                last.then_inc(ph.mixed2, 1)

            if ph.turn == 1:
                in_step(pe, [(0, transposes), (1, products)])
            elif ph.turn == 2:
                in_step(pe, [(0, transposes), (1, products), (4, transposes2), (5, products2)])
            else:
                in_step(pe, [(0, transposes), (1, gated_products)])

        def dense_scalar(act, ph):
            def copies(t):
                for g in range(2):
                    act.wait_ge(ph.turned, t.u * 2 + g + 1)
                    if g == 0 and t.after(2):
                        act.wait_ge(ph.mixed, t.u - 1)
                    act.activation(aT[:, t.par, g, :, :], quad(g), ACT.Copy).then_inc(ph.copied, 1)
                if not ph.gated:
                    act.activation(cntT[0:QUAD, t.par, :], ps[0:QUAD, 2, 0:P], ACT.Copy).then_inc(ph.copied, 1)

            def deviation(t):
                act.wait_ge(ph.var, t.u + 1)
                act.activation(sd[:, 0, t.par, :], mv[:, 0, t.par, :, 1], ACT.Sqrt,
                               bias=eps[:, 0:1]).then_inc(ph.std, 1)

            def copies2(t):
                act.wait_ge(ph.turned2, t.u + 1)
                if t.after(2):
                    act.wait_ge(ph.mixed2, t.u - 1)
                act.activation(n2T[:, t.par, :, :], quad(5), ACT.Copy).then_inc(ph.copied2, 1)

            def gates_(t):
                act.wait_ge(ph.gate, t.u + 1)
                act.activation(tt[:, t.par, 1, :, :], tt[:, t.par, 0, :, :], ACT.Sigmoid).then_inc(ph.gate_open, 1)

            def deviation2(t):
                act.wait_ge(ph.var2, t.u + 1)
                act.activation(sd[:, 1, t.par, :], mv[:, 1, t.par, :, 1], ACT.Sqrt,
                               bias=eps[:, 0:1]).then_inc(ph.std2, 1)

            if ph.turn == 1:
                in_step(act, [(0, copies), (2, deviation)])
            elif ph.turn == 2:
                in_step(act, [(0, copies), (2, deviation), (4, copies2), (6, deviation2)])
            else:
                in_step(act, [(0, copies), (2, gates_), (3, deviation2)])

        def dense_vector(dve, ph):
            def moments(k, t, value, s_stats, s_var):
                for j in range(QUAD):
                    last = dve.bn_stats(stats[:, k, t.par, j, :], value[:, j, :])
                last.then_inc(s_stats, 1)
                dve.wait_ge(s_stats, t.u + 1)
                own_wait(dve)
                for j in range(QUAD):
                    last = dve.bn_aggr(mv[:, k, t.par, j, :], stats[:, k, t.par, j, :])
                last.then_inc(s_var, 1)

            def normalise(k, t, value, target, s_recip):
                dve.reciprocal(rstd[:, k, t.par, :], sd[:, k, t.par, :]).then_inc(s_recip, 1)
                dve.wait_ge(s_recip, t.u + 1)
                for j in range(QUAD):
                    last = dve.tensor_scalar(target[:, j, :], value[:, j, :], mv[:, k, t.par, j, 0:1],
                                             rstd[:, k, t.par, j:j + 1], ALU.subtract, ALU.mult)
                return last

            def first_moments(t):
                dve.wait_ge(ph.mixed, t.u + 1)
                moments(0, t, quad(3 + t.par), ph.stats, ph.var)

            def first_norm(t):
                if ph.turn == 1:
                    if t.after(RING):
                        dve.wait_ge(s_res[t.slot], ph.res_stored(t))
                    target = res[:, t.slot]
                else:
                    if t.after(2):
                        dve.wait_ge(ph.turned2, t.u - 1)
                    target = n2[:, t.par]
                dve.wait_ge(ph.std, t.u + 1)
                normalise(0, t, quad(3 + t.par), target, ph.recip).then_inc(ph.norm, 1)

            def residual(t):
                dve.wait_ge(s_x[t.slot], ph.x_ready(t))
                dve.wait_ge(ph.mixed2, t.u + 1)
                if t.after(2):
                    dve.wait_ge(ph.done, t.u - 1)
                dve.tensor_tensor(vout[:, t.par, :, :], quad(6 + t.par), xin[:, t.slot, :, :],
                                  ALU.add).then_inc(ph.added, 1)
                dve.wait_ge(ph.added, t.u + 1)
                moments(1, t, vout[:, t.par], ph.stats2, ph.var2)

            def last_norm(t):
                if t.after(RING):
                    dve.wait_ge(s_res[t.slot], ph.res_stored(t))
                dve.wait_ge(ph.std2, t.u + 1)
                normalise(1, t, vout[:, t.par], res[:, t.slot], ph.recip2).then_inc(ph.done, 1)

            DEGREE_STEPS, GATE_STEPS = 5, 3

            def step(t, steps, signal, n, ins):
                ins.then_inc(signal, 1)
                dve.wait_ge(signal, t.u * steps + n)

            def degrees(t):
                dve.wait_ge(s_ab[t.slot], ph.ab_ready(t))
                deg = dg[:, t.slot]
                dve.tensor_copy(deg[:, 0, :, 0], hin[:, t.slot, :, D])
                step(t, DEGREE_STEPS, ph.deg_chain, 1, dve.tensor_copy(deg[:, 0, :, 1], rin[:, t.slot, :, D]))
                step(t, DEGREE_STEPS, ph.deg_chain, 2,
                     dve.tensor_scalar(deg[:, 1], deg[:, 0], 0.0, None, ALU.is_gt))
                step(t, DEGREE_STEPS, ph.deg_chain, 3,
                     dve.tensor_tensor(deg[:, 2], deg[:, 0], deg[:, 1], ALU.mult))
                step(t, DEGREE_STEPS, ph.deg_chain, 4,
                     dve.scalar_tensor_tensor(out=deg[:, 3], in0=deg[:, 2], scalar=1.0, in1=deg[:, 1],
                                              op0=ALU.add, op1=ALU.subtract))
                step(t, DEGREE_STEPS, ph.deg_chain, 5, dve.reciprocal(deg[:, 0], deg[:, 3]))
                dve.tensor_tensor(deg[:, 2], deg[:, 0], deg[:, 1], ALU.mult).then_inc(ph.degrees, 1)

            def wide(row):
                return rows[:, row, :].unsqueeze(1).to_broadcast([P, QUAD, D])

            def halves(v):
                return v.rearrange("p j (g c) -> p (j g) c", g=2)

            def each(v):
                return v.rearrange("p j g -> p (j g)").unsqueeze(2).to_broadcast([P, 2 * QUAD, 64])

            def hops(t):
                y = yy[:, t.par]
                dve.wait_ge(ph.degrees, t.u + 1)
                dve.wait_ge(ph.mixed, t.u + 1)
                if t.after(2):
                    dve.wait_ge(ph.joined, t.u - 1)
                dve.tensor_tensor(halves(y[:, 0]), ps[:, 3 + t.par, :].rearrange("p (m c) -> p m c", c=64),
                                  each(dg[:, t.slot, 2]), ALU.mult).then_inc(ph.scaled, 1)
                dve.wait_ge(ph.scaled, t.u + 1)
                step(t, GATE_STEPS, ph.ca, 1, dve.tensor_tensor(y[:, 1], y[:, 0], wide(5), ALU.add))
                step(t, GATE_STEPS, ph.ca, 2, dve.tensor_tensor(y[:, 0], y[:, 1], wide(6), ALU.mult))
                step(t, GATE_STEPS, ph.ca, 3,
                     dve.tensor_reduce(tt[:, t.par, 2].rearrange("p j g -> p (j g)"), halves(y[:, 0]), AX.X,
                                       ALU.add))
                dve.tensor_tensor(tt[:, t.par, 0], tt[:, t.par, 2],
                                  bfs[:, :].unsqueeze(1).to_broadcast([P, QUAD, 2]), ALU.add).then_inc(ph.gate, 1)

            def join(t):
                y = yy[:, t.par]
                dve.wait_ge(s_x[t.slot], ph.x_ready(t))
                dve.scalar_tensor_tensor(out=y[:, 2], in0=y[:, 1], scalar=0.0, in1=xin[:, t.slot], op0=ALU.max,
                                         op1=ALU.add).then_inc(ph.added, 1)
                dve.wait_ge(ph.gate_open, t.u + 1)
                dve.scalar_tensor_tensor(out=halves(y[:, 0]), in0=halves(y[:, 1]), scalar=0.0,
                                         in1=each(tt[:, t.par, 1]), op0=ALU.min, op1=ALU.mult)\
                   .then_inc(ph.joined, 1)
                dve.wait_ge(ph.joined, t.u + 1)
                dve.wait_ge(ph.added, t.u + 1)
                if t.after(2):
                    dve.wait_ge(ph.done, t.u - 1)
                dve.tensor_tensor(vout[:, t.par], y[:, 2], y[:, 0], ALU.add).then_inc(ph.summed, 1)
                dve.wait_ge(ph.summed, t.u + 1)
                moments(1, t, vout[:, t.par], ph.stats2, ph.var2)

            if ph.turn == 1:
                in_step(dve, [(2, first_moments), (3, first_norm)])
            elif ph.turn == 2:
                in_step(dve, [(2, first_moments), (3, first_norm), (6, residual), (7, last_norm)])
            else:
                in_step(dve, [(0, degrees), (2, hops), (3, join), (4, last_norm)])

        zeros_b = sb("zeros_b", [P, 2 * DIGIT], BF16)

        e0 = EdgePhase(0, by_dst_set, msg_sum, [(x, 0, D), (x, 1, D)], 0, low_pass)
        e1 = EdgePhase(1, by_dst_set, msg_sum, [(n1_table, 0, D), (n1_table, 1, D)], 1, high_pass)
        e2 = EdgePhase(2, by_src_set, hop1, [(x1_table, 1, D)], None, None)
        e3 = EdgePhase(3, by_src_set, hop2, [(hop1, 1, W)], None, None)

        block = ctx.enter_context(nc.Block())

        @block.sync
        def _(sp):
            n = 0
            for t, s in ((nat[:, 0, :], W_enc), (nat[:, 9, :], W_out),
                         (nat[:, 10:12, :], Wm2.rearrange("l o k -> o l k")),
                         (nat[:, 1:5, :].rearrange("p (l a) k -> p l (a k)", l=2), Wm1.rearrange("l o k -> o l k")),
                         (nat[:, 5:9, :].rearrange("p (l a) k -> p l (a k)", l=2), Wu.rearrange("l o k -> o l k")),
                         (gates[:, 0, :], W0), (gates[:, 1, :], W1),
                         (cols[:, 0:1], b_enc.rearrange("(p a) -> p a", a=1)),
                         (cols[:, 1:2], gamma[0, :].rearrange("(p a) -> p a", a=1)),
                         (cols[:, 2:3], gamma[1, :].rearrange("(p a) -> p a", a=1)),
                         (cols[:, 3:4], beta[0, :].rearrange("(p a) -> p a", a=1)),
                         (cols[:, 4:5], beta[1, :].rearrange("(p a) -> p a", a=1)),
                         (cols[:, 5:6], bm2[0, :].rearrange("(p a) -> p a", a=1)),
                         (cols[:, 6:7], bm2[1, :].rearrange("(p a) -> p a", a=1)),
                         (rows[:, 0, :], flat(bm1[0, :], D)), (rows[:, 1, :], flat(bm1[1, :], D)),
                         (rows[:, 2, :], flat(bu[0, :], D)), (rows[:, 3, :], flat(bu[1, :], D)),
                         (rows[:, 4, :], flat(b_out, D)),
                         (rows[:, 5, 0:64], flat(b0, 64)), (rows[:, 5, 64:D], flat(b1, 64)),
                         (rows[:, 6, 0:64], flat(fc0.rearrange("a b -> (a b)"), 64)),
                         (rows[:, 6, 64:D], flat(fc1.rearrange("a b -> (a b)"), 64)),
                         (bfs[:, 0:1], flat(bf0, 1)), (bfs[:, 1:2], flat(bf1, 1))):
                sp.dma_start(t, s).then_inc(s_load, 16)
                n += 1
            assert n == LOADS + 1
            sp.wait_ge(s_fill, 3)
            for t, s in ((raw[:, 0, :], src), (raw[:, 1, :], dst), (raw_w[:, :], edge_weight)):
                sp.dma_start(t[0:FULL, :], s[0:FULL * T].rearrange("(p t) -> p t", t=T)).then_inc(s_edge, 16)
                sp.dma_start(t[FULL:FULL + 1, 0:REST], s[FULL * T:E].rearrange("(a t) -> a t", a=1))\
                  .then_inc(s_edge, 16)
            for k, tab in enumerate((msg_sum, hop1, hop2)):
                v = tab.rearrange("(p a j) c -> p a (j c)", p=P, j=ZROWS)
                for a in range(ZDMAS):
                    sp.dma_start(v[:, a, :], zeros[:, :]).then_inc(s_zero if k == 0 else s_zero2, 16)
            edge_sync(sp, e0)
            dense_sync(sp, d1)
            sp.sem_inc(s_whole, 1)
            sort_load(sp, low_pass, by_low)
            edge_sync(sp, e1)
            dense_sync(sp, d2)
            sp.sem_inc(s_whole, 1)
            sort_load(sp, high_pass, by_src)
            edge_sync(sp, e2)
            sp.sem_inc(s_whole, 1)
            edge_sync(sp, e3)
            dense_sync(sp, d3)

        @block.gpsimd
        def _(pool):
            pool.memset(ident[:, :], 0.0).then_inc(s_c0, 1)
            pool.memset(ones[:, :], 1.0).then_inc(s_c0, 1)
            pool.iota(digits_i[:, :], pattern=[[1, DIGIT]], base=0, channel_multiplier=0).then_inc(s_const, 1)
            pool.iota(part_i[:, :], pattern=[[1, 1]], base=0, channel_multiplier=1).then_inc(s_const, 1)
            pool.wait_ge(s_c0, 2)
            pool.affine_select(out=ident[:, :], in_=ident[:, :], compare_op=ALU.not_equal, fill=1.0,
                               base=0, pattern=[[-1, P]], channel_multiplier=1).then_inc(s_const, 1)
            pool.affine_select(out=before[:, :], in_=ones[:, :], compare_op=ALU.is_gt, fill=0.0,
                               base=0, pattern=[[1, P]], channel_multiplier=-1).then_inc(s_const, 1)
            pool.affine_select(out=upto[:, :], in_=ones[:, :], compare_op=ALU.is_ge, fill=0.0,
                               base=0, pattern=[[1, P]], channel_multiplier=-1).then_inc(s_const, 1)
            edge_pool(pool, e0)
            sort_pool(pool, low_pass, by_low)
            pool.wait_ge(s_whole, 1)
            edge_pool(pool, e1)
            sort_pool(pool, high_pass, by_src)
            pool.wait_ge(s_whole, 2)
            pool.wait_ge(s_zero2, 16 * 2 * ZDMAS)
            edge_pool(pool, e2)
            pool.wait_ge(s_whole, 3)
            edge_pool(pool, e3)

        @block.scalar
        def _(act):
            act.wait_ge(s_wt, 1)
            act.activation(wT[:, :, :], ps[:, 0:3, :].rearrange("p b n -> p (b n)")[:, 0:9 * D]
                           .rearrange("p (k n) -> p k n", k=9), ACT.Copy).then_inc(s_wte, 1)
            act.wait_ge(s_wm, 1)
            act.activation(ww[:, :, :], ps[:, 4:8, :].rearrange("p b n -> p (b n)")
                           .rearrange("p (k n) -> p k n", k=16), ACT.Copy).then_inc(s_wme, 1)
            edge_scalar(act, e0)
            dense_scalar(act, d1)
            edge_scalar(act, e1)
            dense_scalar(act, d2)
            edge_scalar(act, e2)
            edge_scalar(act, e3)
            dense_scalar(act, d3)

        @block.tensor
        def _(pe):
            pe.wait_ge(s_load, 16 * (LOADS + 1))
            pe.wait_ge(s_const, 5)
            for k in range(9):
                last = pe.transpose(ps[:, k // 4, (k % 4) * P:(k % 4 + 1) * P], nat[:, 1 + k, :], ident[:, :])
            last.then_inc(s_wt, 1)
            pe.wait_ge(s_wte, 1)
            pe.wait_ge(s_wd, 1)

            def product(k, pairs):
                for m, (a, b) in enumerate(pairs):
                    last = pe.matmul(ps[:, 4 + k // 4, (k % 4) * P:(k % 4 + 1) * P], a, b,
                                     start=(m == 0), stop=(m == len(pairs) - 1))
                return last

            for l in range(2):
                front = nat[:, 0, :] if l == 0 else scaleL[:, 0, :]
                shift = colsB[:, l, :]
                wa, wb, ua, u = wT[:, 2 * l, :], wT[:, 2 * l + 1, :], wT[:, 5 + 2 * l, :], resid[:, l, :]
                product(7 * l + 0, [(front, wa)])
                product(7 * l + 1, [(front, wb)])
                product(7 * l + 2, [(shift, wa), (shift, wb)])
                product(7 * l + 3, [(front, u)])
                product(7 * l + 4, [(shift, u)])
                product(7 * l + 5, [(nat[:, 10 + l, :], ua)])
                product(7 * l + 6, [(colsB[:, 3 + l, :], ua)])
            product(14, [(scaleL[:, 1, :], wT[:, 8, :])])
            product(15, [(colsB[:, 2, :], wT[:, 8, :])]).then_inc(s_wm, 1)
            pe.wait_ge(s_wdone, 1)
            prep_tensor(pe, by_dst_set, dst_prep)
            totals_tensor(pe, low_pass)
            bases_tensor(pe, low_pass)
            edge_tensor(pe, e0)
            pe.wait_ge(high_pass.used1, 2 * IT)
            pe.sem_inc(high_pass.total, 1)
            dense_tensor(pe, d1)
            bases_tensor(pe, high_pass)
            edge_tensor(pe, e1)
            dense_tensor(pe, d2)
            prep_tensor(pe, by_src_set, src_prep)
            edge_tensor(pe, e2)
            edge_tensor(pe, e3)
            dense_tensor(pe, d3)

        @block.vector
        def _(dve):
            dve.memset(zeros[:, :], 0.0).then_inc(s_constd, 1)
            dve.memset(raw[:, 0, :], N).then_inc(s_fill, 1)
            dve.memset(raw[:, 1, :], N).then_inc(s_fill, 1)
            dve.memset(raw_w[:, :], 0.0).then_inc(s_fill, 1)
            dve.memset(eps[:, :], EPS)
            dve.memset(zeros_b[:, :], 0.0)
            dve.memset(cntT[:, :, :], 1.0)
            dve.wait_ge(s_const, 5)
            dve.tensor_copy(ident_b[:, :], ident[:, :])
            dve.tensor_copy(ones_b[:, :], ones[:, :])
            dve.tensor_copy(before_b[:, :], before[:, :])
            link(dve, dve.tensor_tensor(notbefore_b[:, :], ones[:, :], before[:, :], ALU.subtract))
            dve.tensor_copy(digits_b[:, :], digits_i[:, :])
            dve.tensor_scalar(head_row[:, :], part_i[:, :], float(HEAD), None, ALU.add)
            link(dve, dve.tensor_scalar(tail_row[:, :], part_i[:, :], float(TAIL), None, ALU.add))
            dve.wait_ge(s_load, 16 * (LOADS + 1))
            for k, c in enumerate((0, 3, 4, 5, 6)):
                dve.tensor_scalar(colsB[:, k, :], ones[:, :], cols[:, c:c + 1], None, ALU.mult)
            for k in range(2):
                dve.tensor_scalar(scaleL[:, k, :], ident[:, :], cols[:, 1 + k:2 + k], None, ALU.mult)
            dve.wait_ge(s_wte, 1)
            for l in range(2):
                last = dve.tensor_tensor(resid[:, l, :], ident[:, :], wT[:, 4 + 2 * l, :], ALU.add)
            last.then_inc(s_wd, 1)
            dve.wait_ge(s_wme, 1)
            for k, r in ((2, 0), (9, 1), (4, 2), (11, 3), (15, 4)):
                link(dve, dve.tensor_tensor(ww[:, k, :], ww[:, k, :], rows[:, r, :], ALU.add))
            for l in range(2):
                link(dve, dve.tensor_tensor(bias5[:, l, :, :], ident[0:5, 0:QUAD].unsqueeze(2)
                                            .to_broadcast([5, QUAD, D]),
                                            ww[0:5, 7 * l + 6, :].unsqueeze(1).to_broadcast([5, QUAD, D]), ALU.mult))
                link(dve, dve.scalar_tensor_tensor(
                    out=bias5[:, l, :, :], in0=ww[0:5, 7 * l + 4, :].unsqueeze(1).to_broadcast([5, QUAD, D]),
                    scalar=ident[0:5, QUAD:QUAD + 1], in1=bias5[:, l, :, :], op0=ALU.mult, op1=ALU.add))
            link(dve, dve.tensor_copy(b3f[:, 0, :], ww[0:1, 15, :]))
            for k in range(3):
                link(dve, dve.tensor_copy(b3b[:, k, :, :], b3f[:, k, :].unsqueeze(1).to_broadcast([1, QUAD, D])))
                if k < 2:
                    link(dve, dve.tensor_tensor(b3f[:, k + 1, :], b3f[:, k, :], b3b[:, k, 0, :], ALU.subtract))
            dve.sem_inc(s_wdone, 1)
            dve.wait_ge(s_edge, 16 * 6)
            link(dve, dve.memset(edges[:, :, 3], 0.0))
            link(dve, dve.tensor_copy(edges[:, :, 0], raw[:, 0, :]))
            link(dve, dve.tensor_scalar(edges[:, :, 1], raw[:, 1, :], float(N - 1), None, ALU.min))
            link(dve, dve.tensor_copy(edges[:, :, 2], raw_w[:, :]))
            for k in range(2):
                link(dve, dve.tensor_scalar(by_dst_set.gat[:, k, :], raw[:, k, :], float(N - 1), None, ALU.min))
            link(dve, dve.tensor_copy(keyf[:, :], raw[:, 1, :]))
            prep_vector(dve, by_dst_set, dst_prep)
            digits(dve, digit_next, 8)
            digits(dve, digit_f, 0)
            totals_vector(dve, low_pass)
            bases_vector(dve, low_pass, counts)
            edge_vector(dve, e0)
            bases_vector(dve, high_pass, next_total)
            dense_vector(dve, d1)
            dve.wait_ge(low_pass.loaded, 16)
            digits(dve, digit_f, 8)
            edge_vector(dve, e1)
            dense_vector(dve, d2)
            dve.wait_ge(high_pass.loaded, 16)
            link(dve, dve.tensor_copy(keyf[:, :], edges[:, :, 0]))
            link(dve, dve.tensor_copy(by_src_set.gat[:, 1, :], edges[:, :, 1]))
            link(dve, dve.tensor_copy(wcol[:, :], edges[:, :, 2]))
            prep_vector(dve, by_src_set, src_prep)
            edge_vector(dve, e2)
            edge_vector(dve, e3)
            dense_vector(dve, d3)


_INS = ["x", "src", "dst", "edge_weight", "L0_gnn_W_enc", "L0_gnn_b_enc", "L0_gnn_Wm1", "L0_gnn_bm1",
        "L0_gnn_Wm2", "L0_gnn_bm2", "L0_gnn_Wu", "L0_gnn_bu", "L0_gnn_gamma", "L0_gnn_beta", "L0_gnn_W_out",
        "L0_gnn_b_out", "L1_gnn_W0", "L1_gnn_b0", "L1_gnn_W1", "L1_gnn_b1", "L1_gnn_fc0", "L1_gnn_bf0",
        "L1_gnn_fc1", "L1_gnn_bf1"]
_OUTS = [((50000, 128), "float32")]


def kernel(**inputs):
    import numpy as _np
    import concourse.bacc as _bacc
    from concourse import mybir as _mybir
    from concourse.bass_utils import run_bass_kernel_spmd as _run

    nc = _bacc.Bacc("TRN2", target_bir_lowering=False, num_devices=1)
    arrays, args = {}, []
    for name in _INS:
        a = _np.ascontiguousarray(inputs[name])
        arrays[f"in_{name}_dram"] = a
        args.append(nc.dram_tensor(f"in_{name}_dram", a.shape, _mybir.dt.from_np(a.dtype), kind="ExternalInput").ap())
    for i, (shape, dtype) in enumerate(_OUTS):
        dt = _mybir.dt.from_np(_np.dtype(dtype))
        args.append(nc.dram_tensor(f"out_{i}_dram", shape, dt, kind="ExternalOutput").ap())
    graph_kernel(nc, *args)
    r = _run(nc, [arrays], core_ids=[0])
    got = tuple(r.results[0][f"out_{i}_dram"] for i in range(len(_OUTS)))
    return got[0]
```

```python
from contextlib import ExitStack

import concourse.bass as bass
from concourse import mybir

F32 = mybir.dt.float32
BF16 = mybir.dt.bfloat16
I32 = mybir.dt.int32
ALU = mybir.AluOpType
ACT = mybir.ActivationFunctionType
AX = mybir.AxisListType



P = 128
D = 128
W = D + 1
EPS = 1e-5
BATCH = 7
SKIP = 1 << 17
DIGIT = 256
QUAD = 4
RING = 4


def graph_kernel(nc, x, src, dst, edge_weight, W_enc, b_enc, Wm1, bm1, Wm2, bm2, Wu, bu, gamma, beta,
                 W_out, b_out, W0, b0, W1, b1, fc0, bf0, fc1, bf1, out):
    N = x.shape[0]
    E = src.shape[0]
    T = -(-E // (P * 2 * BATCH)) * 2 * BATCH
    IT = T // (2 * BATCH)
    FULL = E // T
    REST = E - FULL * T
    HEAD = N + 1
    TAIL = HEAD + P
    ZROWS = 12
    TR = -(-(TAIL + P) // (P * ZROWS)) * P * ZROWS
    ZDMAS = TR // (P * ZROWS)
    ROWS = QUAD * P
    UNITS = -(-N // ROWS)
    LAST = N - ROWS
    CROWS = 2 * 3 * QUAD + 3
    assert T < DIGIT and N < DIGIT * DIGIT

    with ExitStack() as ctx:
        def sb(name, shape, dt=F32):
            return ctx.enter_context(nc.sbuf_tensor(name, shape, dt))

        def sem(name):
            return ctx.enter_context(nc.semaphore(name))

        def dram(name, shape):
            return nc.dram_tensor(name, shape, F32, kind="Internal").ap()

        msg_sum = dram("msg_sum", [TR, W])
        hop1 = dram("hop1", [TR, W])
        hop2 = dram("hop2", [TR, W])
        n1_table = dram("n1_table", [N, D])
        x1_table = dram("x1_table", [N, D])
        by_low = dram("by_low", [P * T, 4])
        by_src = dram("by_src", [P * T, 4])
        keys = dram("keys", [P * T, 1])

        ident = sb("ident", [P, P])
        ones = sb("ones", [P, P])
        before = sb("before", [P, P])
        upto = sb("upto", [P, P])
        ident_b = sb("ident_b", [P, P], BF16)
        ones_b = sb("ones_b", [P, P], BF16)
        before_b = sb("before_b", [P, P], BF16)
        notbefore_b = sb("notbefore_b", [P, P], BF16)
        digits_i = sb("digits_i", [P, DIGIT], I32)
        digits_b = sb("digits_b", [P, DIGIT], BF16)
        part_i = sb("part_i", [P, 1], I32)
        head_row = sb("head_row", [P, 1])
        tail_row = sb("tail_row", [P, 1])
        eps = sb("eps", [P, 1])
        zeros = sb("zeros", [P, ZROWS * W])

        nat = sb("nat", [P, 12, D])
        wT = sb("wT", [P, 9, D])
        gates = sb("gates", [P, 2, 65])
        cols = sb("cols", [P, 7])
        rows = sb("rows", [P, 7, D])
        bfs = sb("bfs", [P, 2])
        resid = sb("resid", [P, 2, D])
        scaleL = sb("scaleL", [P, 2, D])
        colsB = sb("colsB", [P, 5, D])
        ww = sb("ww", [P, 16, D])
        bias27 = sb("bias27", [CROWS, 2, QUAD, D], BF16)
        parts_f = sb("parts_f", [CROWS, 5, D])
        parts_b = sb("parts_b", [CROWS, 3, 5, D], BF16)
        of_part = sb("of_part", [CROWS, 6])
        of_tile = sb("of_tile", [CROWS, QUAD])

        raw = sb("raw", [P, 2, T], I32)
        raw_w = sb("raw_w", [P, T])
        edges = sb("edges", [P, T, 4])
        keyf = sb("keyf", [P, T])
        digit_i = sb("digit_i", [P, T], I32)
        digit_f = sb("digit_f", [P, T])
        tmp1 = sb("tmp1", [P, T])
        tmp2 = sb("tmp2", [P, T])

        class EdgeSet:
            def __init__(self, name):
                self.same = sb(f"{name}_same", [P, T])
                self.gat = sb(f"{name}_gat", [P, 2, T], I32)
                self.sca = sb(f"{name}_sca", [P, T], I32)
                self.hk = sb(f"{name}_hk", [P, 2])
                self.eq = sb(f"{name}_eq", [P, 4, P])
                self.widx = sb(f"{name}_widx", [P, 2], I32)

        by_dst_set = EdgeSet("dst")
        by_src_set = EdgeSet("src")
        wcol = sb("wcol", [P, T])
        merge_f = sb("merge_f", [P, 4, P])
        merge_d = sb("merge_d", [P, 2, P])
        merge_w = sb("merge_w", [P, 2])

        hot = sb("hot", [P, 2, BATCH, DIGIT], BF16)
        table = sb("table", [16, 16])
        spread = sb("spread", [16, 16, 16])
        place = sb("place", [P, T])
        positions = sb("positions", [P, T], I32)
        scan = sb("scan", [P, 3, DIGIT])
        base_i = sb("base_i", [P, 2, DIGIT], I32)
        base_f = sb("base_f", [P, 2, DIGIT])
        base_b = sb("base_b", [P, 2, DIGIT], BF16)
        junk = sb("junk", [P, DIGIT])
        rank = sb("rank", [P, 2, BATCH])
        rank_i = sb("rank_i", [P, 3, BATCH], I32)
        rank_f = sb("rank_f", [P, 2, BATCH])
        pos = sb("pos", [P, 2, BATCH], I32)
        load4 = sb("load4", [P, 2, BATCH, 4])

        st_gat = sb("st_gat", [P, 2, 2, BATCH], I32)
        st_sca = sb("st_sca", [P, 2, BATCH], I32)
        got = sb("got", [P, 2, 2, BATCH, W])
        gT = sb("gT", [P, 2, BATCH, P])
        pre = sb("pre", [P, BATCH, D])
        msg = sb("msg", [P, BATCH, W])
        run = sb("run", [P, 2, BATCH, W])
        part = sb("part", [P, 2, W])
        merged = sb("merged", [P, 2, W])

        xin = sb("xin", [P, RING, QUAD, D])
        hin = sb("hin", [P, RING, QUAD, W])
        rin = sb("rin", [P, RING, QUAD, W])
        res = sb("res", [P, RING, QUAD, D])
        aT = sb("aT", [P, 2, 2, QUAD, P])
        cnt_hi = sb("cnt_hi", [P, 2, QUAD], BF16)
        cnt_parts = sb("cnt_parts", [P, 2, 2, 3, QUAD])
        cntT = sb("cntT", [CROWS, 2, P], BF16)
        stats = sb("stats", [P, 2, RING, QUAD, 6])
        mv = sb("mv", [P, 2, RING, QUAD, 2])
        sd = sb("sd", [P, 2, RING, QUAD])
        rstd = sb("rstd", [P, 2, RING, QUAD])
        shift = sb("shift", [P, RING, QUAD])
        n2 = sb("n2", [P, 2, QUAD, D])
        n2T = sb("n2T", [P, 2, QUAD, P])
        vout = sb("vout", [P, RING, QUAD, D])
        dg = sb("dg", [P, RING, 4, QUAD, 2])
        yy = sb("yy", [P, RING, 2, QUAD, D])
        tt = sb("tt", [P, RING, 3, QUAD, 2])
        cfc = sb("cfc", [P, 2])
        b3q = sb("b3q", [3, QUAD, D], BF16)

        ps = ctx.enter_context(nc.psum_tensor("ps", [P, 8, 512], F32))

        s_load = sem("s_load")
        s_edge = sem("s_edge")
        s_fill = sem("s_fill")
        s_zero = sem("s_zero")
        s_zero2 = sem("s_zero2")
        s_const = sem("s_const")
        s_wt = sem("s_wt")
        s_wte = sem("s_wte")
        s_wd = sem("s_wd")
        s_wm = sem("s_wm")
        s_wme = sem("s_wme")
        s_wdone = sem("s_wdone")
        s_dve = sem("s_dve")

        linked = [0]

        def link(dve, ins):
            linked[0] += 1
            ins.then_inc(s_dve, 1)
            dve.wait_ge(s_dve, linked[0])

        s_late = sem("s_late")
        s_falls = sem("s_falls")
        s_fallen = sem("s_fallen")
        s_flag = sem("s_flag")
        s_counts_hi = sem("s_counts_hi")
        s_counts = sem("s_counts")
        s_waited = sem("s_waited")

        def own_wait(eng):
            eng.sem_inc(s_waited, 1)

        LOADS = 24

        def flat(v, n):
            return v.rearrange("(a n) -> a n", a=1).to_broadcast([P, n])

        class SortPass:
            def __init__(self, name):
                self.hot1 = sem(f"{name}_hot1")
                self.used1 = sem(f"{name}_used1")
                self.total = sem(f"{name}_total")
                self.based = sem(f"{name}_based")
                self.hot2 = sem(f"{name}_hot2")
                self.prefix = sem(f"{name}_prefix")
                self.ranked = sem(f"{name}_ranked")
                self.used2 = sem(f"{name}_used2")
                self.placed = sem(f"{name}_placed")
                self.staged = sem(f"{name}_staged")
                self.sent = [sem(f"{name}_sent{h}") for h in range(2)]
                self.loaded = sem(f"{name}_loaded")
                self.chain = sem(f"{name}_chain")

        low_pass, high_pass = SortPass("low"), SortPass("high")
        s_whole = sem("s_whole")

        counts = ps[:, 7, 0:DIGIT]

        def digits(dve, target, shift):
            link(dve, dve.tensor_copy(digit_i[:, :], edges[:, :, 0]))
            if shift:
                link(dve, dve.tensor_scalar(digit_i[:, :], digit_i[:, :], shift, None, ALU.logical_shift_right))
            else:
                link(dve, dve.tensor_scalar(digit_i[:, :], digit_i[:, :], DIGIT - 1, None, ALU.bitwise_and))
            link(dve, dve.tensor_copy(target[:, :], digit_i[:, :]))

        def make_hot(dve, target, digit, t):
            for j in range(BATCH):
                ins = dve.tensor_scalar(target[:, j, :], digits_b[:, :], digit[:, bass.ds(t + j, 1)], None,
                                        ALU.is_equal)
            return ins

        NIBBLE = 16
        ROUNDS = 4
        ROUND = T // ROUNDS
        nibbles = base_b[:, :, 0:T]
        hot_round = hot[:, :, :, :].rearrange("p h j d -> p h (j d)")[:, :, 0:2 * ROUND * NIBBLE]\
            .rearrange("p h (k t d) -> p h k t d", k=2, d=NIBBLE)

        def totals_vector(dve, ph, shift):
            for k in range(2):
                link(dve, dve.tensor_copy(digit_i[:, :], edges[:, :, 0]))
                link(dve, dve.tensor_scalar(digit_i[:, :], digit_i[:, :], shift + 4 * (1 - k), None,
                                            ALU.logical_shift_right))
                link(dve, dve.tensor_scalar(digit_i[:, :], digit_i[:, :], NIBBLE - 1, None, ALU.bitwise_and))
                link(dve, dve.tensor_copy(nibbles[:, k, :], digit_i[:, :]))
            for n in range(ROUNDS):
                if n >= 2:
                    dve.wait_ge(ph.used1, n - 1)
                for k in range(2):
                    dve.tensor_tensor(hot_round[:, n % 2, k], nibbles[:, k, n * ROUND:(n + 1) * ROUND].unsqueeze(2)
                                      .to_broadcast([P, ROUND, NIBBLE]),
                                      digits_b[:, 0:NIBBLE].unsqueeze(1).to_broadcast([P, ROUND, NIBBLE]),
                                      ALU.is_equal).then_inc(ph.hot1, 1)
            dve.wait_ge(ph.total, 1)
            link(dve, dve.tensor_copy(table[:, :], ps[0:NIBBLE, 7, 0:NIBBLE]))
            dve.tensor_tensor(spread[:, :, :], table[:, :].unsqueeze(1).to_broadcast([NIBBLE, NIBBLE, NIBBLE]),
                              ident[0:NIBBLE, 0:NIBBLE].unsqueeze(2).to_broadcast([NIBBLE, NIBBLE, NIBBLE]),
                              ALU.mult).then_inc(ph.hot1, 1)
            dve.wait_ge(ph.total, 2)

        def totals_tensor(pe, ph):
            for n in range(ROUNDS):
                pe.wait_ge(ph.hot1, 2 * n + 2)
                for t in range(ROUND):
                    last = pe.matmul(ps[0:NIBBLE, 7, 0:NIBBLE], hot_round[:, n % 2, 0, t, :],
                                     hot_round[:, n % 2, 1, t, :], start=(n == 0 and t == 0),
                                     stop=(n == ROUNDS - 1 and t == ROUND - 1))
                last.then_inc(ph.used1 if n < ROUNDS - 1 else ph.total, 1)
            pe.wait_ge(ph.hot1, 2 * ROUNDS + 1)
            pe.matmul(counts, ones[0:NIBBLE, :], spread[:, :, :], start=True,
                      stop=True).then_inc(ph.total, 1)

        def bases_vector(dve, ph, total):
            link(dve, dve.tensor_copy(scan[:, 0, :], total))
            link(dve, dve.tensor_copy(scan[:, 1, :], scan[:, 0, :]))
            a, b, s = 1, 2, 1
            while s < DIGIT:
                dve.tensor_copy(scan[:, b, 0:s], scan[:, a, 0:s])
                link(dve, dve.tensor_tensor(scan[:, b, s:], scan[:, a, s:], scan[:, a, 0:DIGIT - s], ALU.add))
                a, b, s = b, a, 2 * s
            link(dve, dve.tensor_tensor(scan[:, b, :], scan[:, a, :], scan[:, 0, :], ALU.subtract))
            link(dve, dve.tensor_copy(base_i[:, 0, :], scan[:, b, :]))
            link(dve, dve.tensor_scalar(base_i[:, 1, :], base_i[:, 0, :], P - 1, None, ALU.bitwise_and))
            link(dve, dve.tensor_copy(base_f[:, 1, :], base_i[:, 1, :]))
            link(dve, dve.tensor_tensor(base_f[:, 0, :], scan[:, b, :], base_f[:, 1, :], ALU.subtract))
            dve.tensor_copy(base_b[:, 0, :], base_f[:, 0, :]).then_inc(ph.based, 1)
            dve.tensor_copy(base_b[:, 1, :], base_f[:, 1, :]).then_inc(ph.based, 1)

        def bases_tensor(pe, ph):
            pe.wait_ge(ph.based, 2)
            pe.matmul(ps[:, 7, :], ones_b[:, :], zeros_b[:, :], start=True, stop=False, skip_group_check=True)
            for k in range(2):
                pe.matmul(counts, ident_b[:, :], base_b[:, k, :], start=False, stop=False, skip_group_check=True)

        def ranks_vector(dve, ph, i, h, first, low):
            t = i * (2 * BATCH) + h * BATCH
            if not first:
                dve.wait_ge(ph.used2, i * 2 + h - 1)
            make_hot(dve, hot[:, h], digit_f, t).then_inc(ph.hot2, 1)
            for j in range(BATCH):
                dve.wait_ge(ph.prefix, i * (2 * BATCH) + h * BATCH + j + 1)
                dve.tensor_tensor_reduce(junk[:, :], counts, hot[:, h, j, :], 1.0, 0.0, ALU.mult, ALU.add,
                                         rank[:, h, j:j + 1]).then_inc(ph.ranked, 1)
            dve.wait_ge(ph.ranked, i * (2 * BATCH) + (h + 1) * BATCH)
            if low:
                done = i * 8 + h * 4
                dve.tensor_copy(rank_i[:, 0, :], rank[:, h, :]).then_inc(ph.chain, 1)
                dve.wait_ge(ph.chain, done + 1)
                dve.tensor_scalar(rank_i[:, 1, :], rank_i[:, 0, :], 7, None, ALU.logical_shift_right)
                dve.tensor_scalar(rank_i[:, 2, :], rank_i[:, 0, :], P - 1, None,
                                  ALU.bitwise_and).then_inc(ph.chain, 1)
                dve.wait_ge(ph.chain, done + 2)
                dve.tensor_copy(rank_f[:, 0, :], rank_i[:, 1, :]).then_inc(ph.chain, 1)
                dve.tensor_copy(rank_f[:, 1, :], rank_i[:, 2, :]).then_inc(ph.chain, 1)
                dve.wait_ge(ph.chain, done + 4)
                dve.scalar_tensor_tensor(out=positions[:, bass.ds(t, BATCH)], in0=rank_f[:, 1, :], scalar=float(T),
                                         in1=rank_f[:, 0, :], op0=ALU.mult, op1=ALU.add).then_inc(ph.placed, 1)
            else:
                dve.tensor_copy(positions[:, bass.ds(t, BATCH)], rank[:, h, :]).then_inc(ph.placed, 1)

        def ranks_tensor(pe, ph, i, h):
            pe.wait_ge(ph.hot2, i * 2 + h + 1)
            for j in range(BATCH):
                pe.matmul(counts, before_b[:, :], hot[:, h, j, :], start=False, stop=False,
                          skip_group_check=True).then_inc(ph.prefix, 1)
                pe.wait_ge(ph.ranked, i * (2 * BATCH) + h * BATCH + j + 1)
                last = pe.matmul(counts, notbefore_b[:, :], hot[:, h, j, :], start=False, stop=False,
                                 skip_group_check=True)
            last.then_inc(ph.used2, 1)

        def sort_pool(pool, ph, target):
            pool.wait_ge(ph.placed, 2 * IT)

            def batch(i, h, first):
                t = i * (2 * BATCH) + h * BATCH
                if not first:
                    pool.wait_ge(ph.sent[h], i * (16 * BATCH))
                    own_wait(pool)
                pool.tensor_copy(pos[:, h, :], positions[:, bass.ds(t, BATCH)]).then_inc(ph.staged, 1)
                pool.tensor_copy(load4[:, h, :, :], edges[:, bass.ds(t, BATCH), :]).then_inc(ph.staged, 1)
                pool.wait_ge(ph.staged, i * 4 + 2 * h + 2)
                own_wait(pool)
                for j in range(BATCH):
                    pool.indirect_dma_start(
                        target, bass.IndirectOffsetOnAxis(ap=pos[:, h, j:j + 1], axis=0), load4[:, h, j, :],
                        None, bounds_check=P * T - 1, oob_is_err=False).then_inc(ph.sent[h], 16)

            batch(0, 0, True)
            batch(0, 1, True)
            with pool.Fori(1, IT) as i:
                batch(i, 0, False)
                batch(i, 1, False)

        def sort_load(pool, ph, target):
            for h in range(2):
                pool.wait_ge(ph.sent[h], 16 * BATCH * IT)
            pool.dma_start(edges[:, :, :], target.rearrange("(p t) c -> p t c", t=T)).then_inc(ph.loaded, 16)

        prep_diag, prep_keys, prep_masked, prep_count = (sem("prep_diag"), sem("prep_keys"), sem("prep_masked"),
                                                         sem("prep_count"))

        def prep_vector(dve, es, turn):
            link(dve, dve.memset(es.same[:, 0:1], 0.0))
            link(dve, dve.tensor_tensor(es.same[:, 1:T], keyf[:, 0:T - 1], keyf[:, 1:T], ALU.is_equal))
            link(dve, dve.tensor_scalar(tmp1[:, :], keyf[:, :], keyf[:, 0:1], None, ALU.is_equal))
            link(dve, dve.tensor_scalar(tmp2[:, :], keyf[:, :], -1.0, head_row[:, 0:1], ALU.mult, ALU.add))
            link(dve, dve.tensor_tensor(tmp1[:, :], tmp1[:, :], tmp2[:, :], ALU.mult))
            link(dve, dve.tensor_tensor(tmp2[:, :], keyf[:, :], tmp1[:, :], ALU.add))
            link(dve, dve.scalar_tensor_tensor(out=tmp2[:, 0:T - 1], in0=es.same[:, 1:T], scalar=float(SKIP),
                                               in1=tmp2[:, 0:T - 1], op0=ALU.mult, op1=ALU.add))
            link(dve, dve.tensor_copy(tmp2[:, T - 1:T], tail_row[:, :]))
            link(dve, dve.tensor_copy(es.sca[:, :], tmp2[:, :]))
            link(dve, dve.tensor_copy(es.hk[:, 0:1], keyf[:, 0:1]))
            link(dve, dve.tensor_copy(es.hk[:, 1:2], keyf[:, T - 1:T]))
            for b in range(2):
                dve.tensor_scalar(merge_d[:, b, :], ident[:, :], es.hk[:, b:b + 1], None,
                                  ALU.mult).then_inc(prep_diag, 1)
            dve.wait_ge(prep_keys, turn + 1)
            for a in range(2):
                for b in range(2):
                    link(dve, dve.tensor_scalar(es.eq[:, 2 * a + b, :], ps[:, 6, b * P:(b + 1) * P],
                                                es.hk[:, a:a + 1], None, ALU.is_equal))
                    earlier = upto if (a, b) == (0, 1) else before
                    dve.tensor_tensor(merge_f[:, 2 * a + b, :], es.eq[:, 2 * a + b, :], earlier[:, :],
                                      ALU.mult).then_inc(prep_masked, 1)
            dve.wait_ge(prep_count, turn + 1)
            link(dve, dve.tensor_scalar(merge_w[:, :], ps[:, 6, 2 * P:2 * P + 2], 0.0, float(SKIP), ALU.is_gt, ALU.mult))
            link(dve, dve.tensor_tensor(es.widx[:, :], merge_w[:, :], es.hk[:, :], ALU.add))

        def prep_tensor(pe, es, turn):
            pe.wait_ge(prep_diag, turn * 2 + 2)
            for b in range(2):
                last = pe.matmul(ps[:, 6, b * P:(b + 1) * P], ones[:, :], merge_d[:, b, :], start=True, stop=True)
            last.then_inc(prep_keys, 1)
            pe.wait_ge(prep_masked, turn * 4 + 4)
            for b in range(2):
                for a in range(2):
                    last = pe.matmul(ps[:, 6, 2 * P + b:2 * P + b + 1], merge_f[:, 2 * a + b, :], ones[:, 0:1],
                                     start=(a == 0), stop=(a == 1))
            last.then_inc(prep_count, 1)

        s_parts, s_joined, s_joinedc, s_stored = sem("parts"), sem("joined"), sem("joinedc"), sem("stored")

        class EdgePhase:

            def __init__(self, turn, es, table, gathers, layer, sorting, shares=None):
                self.sorting = sorting
                name = f"e{turn}"
                self.turn, self.es, self.table, self.gathers, self.layer = turn, es, table, gathers, layer
                self.n = BATCH * len(gathers)
                if shares is not None:
                    self.past = shares.past + IT
                    self.staged, self.gat, self.used = shares.staged, shares.gat, shares.used
                    self.messages, self.chain, self.summed = shares.messages, shares.chain, shares.summed
                    self.sent = shares.sent
                else:
                    self.past = 0
                    self.staged = sem(f"{name}_staged")
                    self.gat = [sem(f"{name}_gat{h}") for h in range(2)]
                    self.used = sem(f"{name}_used")
                    if layer is not None:
                        self.turned = sem(f"{name}_turned")
                        self.copied = sem(f"{name}_copied")
                        self.mixed = sem(f"{name}_mixed")
                        self.added = sem(f"{name}_added")
                    self.messages = sem(f"{name}_messages")
                    self.chain = sem(f"{name}_chain")
                    self.summed = sem(f"{name}_summed")
                    self.sent = [sem(f"{name}_sent{h}") for h in range(2)]
                self.parts, self.joined, self.joinedc, self.stored = s_parts, s_joined, s_joinedc, s_stored

        def edge_pool(pool, ph):
            es = ph.es

            def gather(i, h, first):
                pool.wait_ge(ph.staged, (ph.past + i) * 2 + h + 1)
                if not first:
                    pool.wait_ge(ph.used, (ph.past + i) * 2 + h - 1)
                own_wait(pool)
                for g, (tab, row, c) in enumerate(ph.gathers):
                    for j in range(BATCH):
                        pool.indirect_dma_start(
                            got[:, h, g, j, 0:c], None, tab,
                            bass.IndirectOffsetOnAxis(ap=st_gat[:, h, g, j:j + 1], axis=0),
                            bounds_check=N - 1, oob_is_err=False).then_inc(ph.gat[h], 16)

            def scatter(n, h):
                pool.wait_ge(ph.summed, ph.past * 2 + n + 1)
                own_wait(pool)
                for j in range(BATCH):
                    pool.indirect_dma_start(
                        ph.table, bass.IndirectOffsetOnAxis(ap=st_sca[:, h, j:j + 1], axis=0), run[:, h, j, :],
                        None, bounds_check=TR - 1, oob_is_err=False).then_inc(ph.sent[h], 16)

            gather(0, 0, True)
            gather(0, 1, True)
            gather(1, 0, False)
            if ph.turn == 0:
                pool.wait_ge(s_zero, 16 * ZDMAS)
            scatter(0, 0)
            gather(1, 1, False)
            scatter(1, 1)
            with pool.Fori(2, IT) as i:
                gather(i, 0, False)
                scatter(i * 2 - 2, 0)
                gather(i, 1, False)
                scatter(i * 2 - 1, 1)
            scatter(2 * IT - 2, 0)
            scatter(2 * IT - 1, 1)
            pool.wait_ge(ph.joinedc, ph.turn + 1)
            for b in range(2):
                pool.indirect_dma_start(
                    ph.table, bass.IndirectOffsetOnAxis(ap=es.widx[:, b:b + 1], axis=0), merged[:, b, :],
                    None, bounds_check=TR - 1, oob_is_err=False).then_inc(ph.stored, 16)

        def edge_tensor(pe, ph):
            es = ph.es

            def transposes(i, h, first):
                pe.wait_ge(ph.gat[h], i * (16 * ph.n) + 16 * ph.n)
                if not first:
                    pe.wait_ge(ph.copied, i * 4 + 2 * h)
                for g in range(2):
                    for j in range(BATCH):
                        last = pe.transpose(turned[g][:, j, :], got[:, h, g, j, 0:D], ident[:, :])
                    last.then_inc(ph.turned, 1)

            def products(i, h, first):
                pe.wait_ge(ph.copied, i * 4 + 2 * h + 2)
                if not first:
                    pe.wait_ge(ph.added, i * 2 + h)
                for j in range(BATCH):
                    for g in range(2):
                        last = pe.matmul(mixed[:, j, :], gT[:, g, j, :], ww[:, 7 * ph.layer + g, :],
                                         start=(g == 0), stop=(g == 1))
                last.then_inc(ph.mixed, 1)

            if ph.layer is not None:
                transposes(0, 0, True)
                products(0, 0, True)
                transposes(0, 1, False)
                products(0, 1, False)
                totals_tensor(pe, ph.sorting)
                bases_tensor(pe, ph.sorting)
                ranks_tensor(pe, ph.sorting, 0, 0)
                with pe.Fori(1, IT) as i:
                    transposes(i, 0, False)
                    ranks_tensor(pe, ph.sorting, i - 1, 1)
                    products(i, 0, False)
                    transposes(i, 1, False)
                    ranks_tensor(pe, ph.sorting, i, 0)
                    products(i, 1, False)
                ranks_tensor(pe, ph.sorting, IT - 1, 1)
            pe.wait_ge(ph.parts, 16 * (ph.turn + 1))
            for b in range(2):
                for a in range(2):
                    last = pe.matmul(ps[:, 6, b * 256:b * 256 + W], es.eq[:, 2 * a + b, :], part[:, a, :],
                                     start=(a == 0), stop=(a == 1))
            last.then_inc(ph.joined, 1)

        turned = [ps[:, 2 * g:2 * g + 2, :].rearrange("p b n -> p (b n)")[:, 0:BATCH * P]
                  .rearrange("p (j e) -> p j e", j=BATCH) for g in range(2)]
        mixed = ps[:, 4:6, :].rearrange("p b n -> p (b n)")[:, 0:BATCH * D].rearrange("p (j e) -> p j e", j=BATCH)

        def edge_scalar(act, ph):
            def batch(i, h, first):
                if ph.layer is not None:
                    for g in range(2):
                        act.wait_ge(ph.turned, i * 4 + 2 * h + g + 1)
                        if not first:
                            act.wait_ge(ph.mixed, i * 2 + h)
                        ins = act.activation(gT[:, g, :, :], turned[g], ACT.Copy).then_inc(ph.copied, 1)
                    act.wait_ge(ph.added, i * 2 + h + 1)
                    if not first:
                        act.wait_ge(ph.summed, i * 2 + h)
                    act.activation(msg[:, :, 0:D], pre[:, :, :], ACT.Relu).then_inc(ph.messages, 1)
                else:
                    act.wait_ge(ph.gat[h], (ph.past + i) * (16 * ph.n) + 16 * ph.n)
                    if not first:
                        act.wait_ge(ph.summed, (ph.past + i) * 2 + h)
                    for j in range(BATCH):
                        last = act.activation(msg[:, j, :], got[:, h, 0, j, :], ACT.Copy,
                                              scale=wcol[:, bass.ds(i * (2 * BATCH) + h * BATCH + j, 1)])
                    last.then_inc(ph.messages, 1)

            batch(0, 0, True)
            batch(0, 1, False)
            with act.Fori(1, IT) as i:
                batch(i, 0, False)
                batch(i, 1, False)

        def stage_gather(dve, ph, i, h):
            t = i * (2 * BATCH) + h * BATCH
            dve.tensor_copy(st_gat[:, h, 0:len(ph.gathers), :],
                            ph.es.gat[:, 2 - len(ph.gathers):2, bass.ds(t, BATCH)]).then_inc(ph.staged, 1)

        def stage_first(dve, ph):
            if ph.gathers[0][2] == D and ph.layer is None:
                link(dve, dve.memset(got[:, :, 0, :, D:W], 1.0))
            for h in range(2):
                stage_gather(dve, ph, 0, h)

        def edge_vector(dve, ph):
            es = ph.es

            def stage(i, h):
                stage_gather(dve, ph, i, h)

            def batch(i, h, first, ahead):
                t = i * (2 * BATCH) + h * BATCH
                if ph.layer is not None:
                    dve.wait_ge(ph.mixed, i * 2 + h + 1)
                    if not first:
                        dve.wait_ge(ph.messages, i * 2 + h)
                    dve.tensor_tensor(pre[:, :, :], mixed, ww[:, 7 * ph.layer + 2, :].unsqueeze(1)
                                      .to_broadcast([P, BATCH, D]), ALU.add).then_inc(ph.added, 1)
                dve.wait_ge(ph.messages, (ph.past + i) * 2 + h + 1)
                dve.wait_ge(ph.gat[h], (ph.past + i) * (16 * ph.n) + 16 * ph.n)
                dve.sem_inc(ph.used, 1)
                if ahead:
                    stage(i + 1, h)
                if not (isinstance(i, int) and i == 0):
                    dve.wait_ge(ph.sent[h], (ph.past + i) * (16 * BATCH))
                dve.tensor_copy(st_sca[:, h, :], es.sca[:, bass.ds(t, BATCH)])
                for j in range(BATCH):
                    last = run[:, 1 - h, BATCH - 1, :] if j == 0 else run[:, h, j - 1, :]
                    ins = dve.scalar_tensor_tensor(out=run[:, h, j, :], in0=last,
                                                   scalar=es.same[:, bass.ds(t + j, 1)], in1=msg[:, j, :],
                                                   op0=ALU.mult, op1=ALU.add)
                    ins.then_inc(ph.chain, 1)
                    dve.wait_ge(ph.chain, (ph.past + i) * (2 * BATCH) + h * BATCH + j + 1)
                dve.sem_inc(ph.summed, 1)

            def ranks(i, h):
                if ph.sorting is not None:
                    ranks_vector(dve, ph.sorting, i, h, isinstance(i, int) and i == 0, ph.layer == 0)

            link(dve, dve.memset(run[:, 1, BATCH - 1, :], 0.0))
            if ph.layer is not None:
                link(dve, dve.memset(msg[:, :, D:W], 1.0))
            batch(0, 0, True, True)
            batch(0, 1, False, True)
            if ph.sorting is not None:
                totals_vector(dve, ph.sorting, 8 * ph.turn)
                bases_vector(dve, ph.sorting, counts)
            ranks(0, 0)
            ranks(0, 1)
            with dve.Fori(1, IT - 1) as i:
                for h in range(2):
                    batch(i, h, False, True)
                    ranks(i, h)
            for h in range(2):
                batch(IT - 1, h, False, False)
                ranks(IT - 1, h)
            if ph.turn == 0:
                late_constants(dve)
            dve.wait_ge(ph.joined, ph.turn + 1)
            dve.tensor_copy(merged[:, :, :], ps[:, 6, :].rearrange("p (b n) -> p b n", b=2)[:, :, 0:W])\
               .then_inc(ph.joinedc, 1)

        def edge_sync(sp, ph):
            for h in range(2):
                sp.wait_ge(ph.sent[h], 16 * BATCH * (ph.past + IT))
            sp.dma_start(part[:, :, :], ph.table[HEAD:HEAD + 2 * P, :].rearrange("(a p) c -> p a c", a=2))\
              .then_inc(ph.parts, 16)
            sp.wait_ge(ph.stored, 32 * (ph.turn + 1))

        class Unit:

            def __init__(self, i, c):
                self.round = i + c // RING
                self.slot = c % RING
                self.par = c % 2
                self.u = self.round * RING + self.slot
                self.looped = not isinstance(i, int)
                self.base = LAST if not self.looped and self.u == UNITS - 1 else self.u * ROWS

            def after(self, n):
                return self.looped or self.u >= n

        def in_step(eng, stages):
            depth = max(offset for offset, _ in stages)
            first = -(-depth // RING) + 1
            rounds = UNITS // RING

            def straight(steps):
                for s in steps:
                    for offset, stage in stages:
                        if 0 <= s - offset < UNITS:
                            stage(Unit(0, s - offset))

            straight(range(first * RING))
            with eng.Fori(first, rounds) as i:
                for k in range(RING):
                    for offset, stage in stages:
                        stage(Unit(i, k - offset))
            straight(range(rounds * RING, UNITS + depth))

        s_ab = [sem(f"s_ab{r}") for r in range(RING)]
        s_x = [sem(f"s_x{r}") for r in range(RING)]
        s_res = [sem(f"s_res{r}") for r in range(RING)]
        USES = [len(range(r, UNITS, RING)) for r in range(RING)]

        class DensePhase:

            def __init__(self, turn, a, b, target, layer, late_x, gated):
                name = f"d{turn}"
                self.a, self.b, self.target, self.layer, self.late_x = a, b, target, layer, late_x
                self.gated = gated
                self.turn = turn
                self.ab_before = 32 * (turn - 1)
                self.x_before = 16 * max(0, turn - 2)
                self.counts_before = UNITS * (turn - 1)
                self.turned = sem(f"{name}_turned")
                self.copied = sem(f"{name}_copied")
                self.mixed = sem(f"{name}_mixed")
                if not gated:
                    self.stats = sem(f"{name}_stats")
                    self.var = sem(f"{name}_var")
                    self.std = sem(f"{name}_std")
                    self.recip = sem(f"{name}_recip")
                    self.shifted = sem(f"{name}_shifted")
                if turn > 1:
                    self.stats2 = sem(f"{name}_stats2")
                    self.var2 = sem(f"{name}_var2")
                    self.std2 = sem(f"{name}_std2")
                    self.recip2 = sem(f"{name}_recip2")
                    self.added = sem(f"{name}_added")
                if turn == 2:
                    self.turned2 = sem(f"{name}_turned2")
                    self.copied2 = sem(f"{name}_copied2")
                    self.mixed2 = sem(f"{name}_mixed2")
                if gated:
                    self.degrees = sem(f"{name}_degrees")
                    self.deg_chain = sem(f"{name}_deg_chain")
                    self.scaled = sem(f"{name}_scaled")
                    self.gate_chain = sem(f"{name}_gate_chain")
                    self.gate = sem(f"{name}_gate")
                    self.gate_open = sem(f"{name}_gate_open")
                    self.biased = sem(f"{name}_biased")
                    self.clipped = sem(f"{name}_clipped")
                    self.joined = sem(f"{name}_joined")
                    self.summed = sem(f"{name}_summed")
                else:
                    self.norm = sem(f"{name}_norm")
                self.done = self.norm if turn == 1 else sem(f"{name}_done")

            def ab_ready(self, t):
                return (t.round + 1) * 32 + self.ab_before * USES[t.slot]

            def x_ready(self, t):
                return (t.round + 1) * 16 + self.x_before * USES[t.slot]

            def res_stored(self, t):
                return t.round * 16 + 16 * (self.turn - 1) * USES[t.slot]

        d1 = DensePhase(1, (x, xin, D), (msg_sum, rin, W), n1_table, 0, False, False)
        d2 = DensePhase(2, (n1_table, hin, D), (msg_sum, rin, W), x1_table, 1, (x, xin), False)
        d3 = DensePhase(3, (hop1, hin, W), (hop2, rin, W), out, None, (x1_table, xin), True)

        def node_rows(tab, base, c):
            return tab[bass.ds(base, ROWS), 0:c].rearrange("(p j) c -> p j c", j=QUAD)

        def dense_sync(sp, ph):
            def load(t):
                if t.after(RING):
                    sp.wait_ge(ph.turned, t.u * 2 - (RING - 1) * 2)
                    if ph.gated:
                        own_wait(sp)
                        sp.wait_ge(ph.degrees, t.u - (RING - 1))
                own_wait(sp)
                for tab, tile, c in (ph.a, ph.b):
                    sp.dma_start(tile[:, t.slot, :, 0:c], node_rows(tab, t.base, c)).then_inc(s_ab[t.slot], 16)

            def load_x(t):
                if t.after(RING):
                    sp.wait_ge(ph.added, t.u - (RING - 1))
                own_wait(sp)
                tab, tile = ph.late_x
                sp.dma_start(tile[:, t.slot, :, :], node_rows(tab, t.base, D)).then_inc(s_x[t.slot], 16)

            def store(t):
                sp.wait_ge(ph.done, t.u + 1)
                if not t.looped and t.u == UNITS - 1:
                    r = (UNITS - 2) % RING
                    sp.wait_ge(s_res[r], 16 * ph.turn * USES[r])
                own_wait(sp)
                sp.dma_start(node_rows(ph.target, t.base, D), res[:, t.slot, :, :]).then_inc(s_res[t.slot], 16)

            if ph.turn == 1:
                in_step(sp, [(0, load), (8, store)])
            elif ph.turn == 2:
                in_step(sp, [(0, load), (6, load_x), (12, store)])
            else:
                in_step(sp, [(0, load), (4, load_x), (12, store)])
            for r in range(RING):
                sp.wait_ge(s_res[r], 16 * ph.turn * USES[r])

        def quad(bank):
            return ps[:, bank, :].rearrange("p (j e) -> p j e", j=QUAD)

        def turn_quad(pe, bank, tile):
            for j in range(QUAD):
                last = pe.transpose(quad(bank)[:, j, :], tile[:, j, 0:D], ident[:, :])
            return last

        def hop_bank(t, g):
            return ps[:, 2 + 2 * t.par + g, 0:65 * QUAD].rearrange("p (j c) -> p j c", j=QUAD)

        def product_bank(ph, t):
            return 3 + (t.par if ph.turn == 2 else t.slot)

        def dense_tensor(pe, ph):
            def transposes(t):
                pe.wait_ge(s_ab[t.slot], ph.ab_ready(t))
                if t.after(1):
                    pe.wait_ge(ph.copied, t.u * (2 if ph.gated else 3))
                turn_quad(pe, 0, ph.a[1][:, t.slot]).then_inc(ph.turned, 1)
                last = turn_quad(pe, 1, ph.b[1][:, t.slot])
                if not ph.gated:
                    pe.wait_ge(s_counts, ph.counts_before + t.u + 1)
                    last = pe.transpose(ps[0:CROWS - 3, 2, 0:P],
                                        cnt_parts[:, t.par].rearrange("p a k j -> p (a k j)"), ident[:, :])
                last.then_inc(ph.turned, 1)

            def products(t):
                pe.wait_ge(ph.copied, t.u * 3 + 3)
                keep = 2 if ph.turn == 2 else RING
                if t.after(keep):
                    pe.wait_ge(ph.norm, t.u - keep + 1)
                acc = ps[:, product_bank(ph, t), :]
                for j in range(QUAD):
                    pe.matmul(acc[:, j * P:(j + 1) * P], aT[:, t.par, 0, j, :], ww[:, 7 * ph.layer + 3, :],
                              start=(j == 0), stop=False, skip_group_check=True)
                    pe.matmul(acc[:, j * P:(j + 1) * P], aT[:, t.par, 1, j, :], ww[:, 7 * ph.layer + 5, :],
                              start=False, stop=False, skip_group_check=True)
                pe.matmul(acc, cntT[:, t.par, :], bias27[:, ph.layer, :, :], start=False, stop=True,
                          skip_group_check=True).then_inc(ph.mixed, 1)

            def gated_products(t):
                pe.wait_ge(ph.copied, t.u * 2 + 2)
                if t.after(2):
                    pe.wait_ge(ph.gate, t.u - 1)
                for j in range(QUAD):
                    for g in range(2):
                        last = pe.matmul(hop_bank(t, g)[:, j, :], aT[:, t.par, g, j, :], gates[:, g, :],
                                         start=True, stop=True)
                last.then_inc(ph.mixed, 1)

            def transposes2(t):
                pe.wait_ge(ph.norm, t.u + 1)
                if t.after(1):
                    pe.wait_ge(ph.copied2, t.u)
                turn_quad(pe, 5, n2[:, t.par]).then_inc(ph.turned2, 1)

            def products2(t):
                pe.wait_ge(ph.copied2, t.u + 1)
                if t.after(2):
                    pe.wait_ge(ph.added, t.u - 1)
                acc = ps[:, 6 + t.par, :]
                pe.matmul(acc, ones_b[0:3, :], b3q[:, :, :], start=True, stop=False, skip_group_check=True)
                for j in range(QUAD):
                    last = pe.matmul(acc[:, j * P:(j + 1) * P], n2T[:, t.par, j, :], ww[:, 14, :],
                                     start=False, stop=(j == QUAD - 1), skip_group_check=True)
                last.then_inc(ph.mixed2, 1)

            if ph.turn == 1:
                in_step(pe, [(1, transposes), (2, products)])
            elif ph.turn == 2:
                in_step(pe, [(1, transposes), (5, transposes2), (6, products2), (2, products)])
            else:
                in_step(pe, [(0, transposes), (1, gated_products)])

        def dense_scalar(act, ph):
            def copies(t):
                for g in range(2):
                    act.wait_ge(ph.turned, t.u * 2 + g + 1)
                    if g == 0 and t.after(2):
                        act.wait_ge(ph.mixed, t.u - 1)
                    act.activation(aT[:, t.par, g, :, :], quad(g), ACT.Copy).then_inc(ph.copied, 1)
                if not ph.gated:
                    act.activation(cntT[0:CROWS - 3, t.par, :], ps[0:CROWS - 3, 2, 0:P], ACT.Copy).then_inc(ph.copied, 1)

            def deviation(t):
                act.wait_ge(ph.var, t.u + 1)
                act.activation(sd[:, 0, t.slot, :], mv[:, 0, t.slot, :, 1], ACT.Sqrt,
                               bias=eps[:, 0:1]).then_inc(ph.std, 1)

            def copies2(t):
                act.wait_ge(ph.turned2, t.u + 1)
                if t.after(2):
                    act.wait_ge(ph.mixed2, t.u - 1)
                act.activation(n2T[:, t.par, :, :], quad(5), ACT.Copy).then_inc(ph.copied2, 1)

            def first_norm(t):
                if ph.turn == 1:
                    if t.after(RING):
                        act.wait_ge(s_res[t.slot], ph.res_stored(t))
                    target = res[:, t.slot]
                else:
                    if t.after(2):
                        act.wait_ge(ph.turned2, t.u - 1)
                    target = n2[:, t.par]
                act.wait_ge(ph.shifted, t.u + 1)
                for j in range(QUAD):
                    last = act.activation(target[:, j, :], quad(product_bank(ph, t))[:, j, :], ACT.Identity,
                                          bias=shift[:, t.slot, j:j + 1], scale=rstd[:, 0, t.slot, j:j + 1])
                last.then_inc(ph.norm, 1)

            def open_gates(t):
                if t.par == 0:
                    return
                act.wait_ge(ph.gate, t.u + 1)
                for slot in (t.slot - 1, t.slot):
                    act.activation(tt[:, slot, 1, :, :], tt[:, slot, 0, :, :], ACT.Sigmoid).then_inc(ph.gate_open, 1)

            def clip(t):
                act.wait_ge(ph.biased, t.u + 1)
                act.activation(yy[:, t.slot, 0], yy[:, t.slot, 1], ACT.Relu).then_inc(ph.clipped, 1)

            def deviation2(t):
                act.wait_ge(ph.var2, t.u + 1)
                act.activation(sd[:, 1, t.slot, :], mv[:, 1, t.slot, :, 1], ACT.Sqrt,
                               bias=eps[:, 0:1]).then_inc(ph.std2, 1)

            def deviations2(t):
                if t.par == 0:
                    return
                act.wait_ge(ph.var2, t.u + 1)
                for slot in (t.slot - 1, t.slot):
                    act.activation(sd[:, 1, slot, :], mv[:, 1, slot, :, 1], ACT.Sqrt,
                                   bias=eps[:, 0:1]).then_inc(ph.std2, 1)

            if ph.turn == 1:
                in_step(act, [(5, first_norm), (1, copies), (3, deviation)])
            elif ph.turn == 2:
                in_step(act, [(4, first_norm), (1, copies), (3, deviation), (5, copies2), (7, deviation2)])
            else:
                in_step(act, [(0, copies), (3, open_gates), (4, clip), (7, deviations2)])

        def dense_vector(dve, ph):
            def statistics(k, t, value, s_stats):
                for j in range(QUAD):
                    last = dve.bn_stats(stats[:, k, t.slot, j, :], value[:, j, :])
                last.then_inc(s_stats, 1)

            def moments(k, t, s_stats, s_var):
                dve.wait_ge(s_stats, t.u + 1)
                own_wait(dve)
                for j in range(QUAD):
                    last = dve.bn_aggr(mv[:, k, t.slot, j, :], stats[:, k, t.slot, j, :])
                last.then_inc(s_var, 1)

            def counts_high(t):
                dve.wait_ge(s_ab[t.slot], ph.ab_ready(t))
                dve.tensor_copy(cnt_hi[:, t.par, :], rin[:, t.slot, :, D]).then_inc(s_counts_hi, 1)

            def counts_parts(t):
                dve.wait_ge(s_counts_hi, ph.counts_before + t.u + 1)
                if t.after(2):
                    dve.wait_ge(ph.turned, t.u * 2 - 2)
                high = cnt_hi[:, t.par, :].unsqueeze(1).to_broadcast([P, 3, QUAD])
                dve.tensor_copy(cnt_parts[:, t.par, 0], high)
                dve.tensor_tensor(cnt_parts[:, t.par, 1], rin[:, t.slot, :, D].unsqueeze(1)
                                  .to_broadcast([P, 3, QUAD]), high, ALU.subtract).then_inc(s_counts, 1)

            def first_statistics(t):
                dve.wait_ge(ph.mixed, t.u + 1)
                statistics(0, t, quad(product_bank(ph, t)), ph.stats)

            def first_moments(t):
                moments(0, t, ph.stats, ph.var)

            def first_scale(t):
                dve.wait_ge(ph.std, t.u + 1)
                dve.reciprocal(rstd[:, 0, t.slot, :], sd[:, 0, t.slot, :]).then_inc(ph.recip, 1)

            def first_shift(t):
                dve.wait_ge(ph.recip, t.u + 1)
                dve.scalar_tensor_tensor(out=shift[:, t.slot, :], in0=mv[:, 0, t.slot, :, 0], scalar=-1.0,
                                         in1=rstd[:, 0, t.slot, :], op0=ALU.mult, op1=ALU.mult)\
                   .then_inc(ph.shifted, 1)

            def residual(t):
                dve.wait_ge(s_x[t.slot], ph.x_ready(t))
                dve.wait_ge(ph.mixed2, t.u + 1)
                if t.after(RING):
                    dve.wait_ge(ph.done, t.u - RING + 1)
                dve.tensor_tensor(vout[:, t.slot, :, :], quad(6 + t.par), xin[:, t.slot, :, :],
                                  ALU.add).then_inc(ph.added, 1)

            def last_statistics(t):
                dve.wait_ge(ph.summed if ph.gated else ph.added, t.u + 1)
                statistics(1, t, vout[:, t.slot], ph.stats2)

            def last_moments(t):
                moments(1, t, ph.stats2, ph.var2)

            def last_scale(t):
                dve.wait_ge(ph.std2, t.u + 1)
                dve.reciprocal(rstd[:, 1, t.slot, :], sd[:, 1, t.slot, :]).then_inc(ph.recip2, 1)

            def last_norm(t):
                if t.after(RING):
                    dve.wait_ge(s_res[t.slot], ph.res_stored(t))
                dve.wait_ge(ph.recip2, t.u + 1)
                for j in range(QUAD):
                    last = dve.tensor_scalar(res[:, t.slot, j, :], vout[:, t.slot, j, :], mv[:, 1, t.slot, j, 0:1],
                                             rstd[:, 1, t.slot, j:j + 1], ALU.subtract, ALU.mult)
                last.then_inc(ph.done, 1)

            TINY = 1.1754944e-38

            def degree_floor(t):
                dve.wait_ge(s_ab[t.slot], ph.ab_ready(t))
                deg = dg[:, t.slot]
                for g, tile in enumerate((hin, rin)):
                    last = dve.tensor_scalar(deg[:, 0, :, g], tile[:, t.slot, :, D], TINY, None, ALU.max)
                last.then_inc(ph.deg_chain, 1)

            def degree_inverse(t):
                deg = dg[:, t.slot]
                dve.wait_ge(ph.deg_chain, t.u * 2 + 1)
                dve.reciprocal(deg[:, 1], deg[:, 0]).then_inc(ph.deg_chain, 1)

            def degrees(t):
                deg = dg[:, t.slot]
                dve.wait_ge(ph.deg_chain, t.u * 2 + 2)
                dve.scalar_tensor_tensor(out=deg[:, 2], in0=deg[:, 0], scalar=TINY, in1=deg[:, 1], op0=ALU.is_gt,
                                         op1=ALU.mult).then_inc(ph.degrees, 1)

            def halves(v):
                return v.rearrange("p j (g c) -> p (j g) c", g=2)

            def each(v):
                return v.rearrange("p j g -> p (j g)").unsqueeze(2).to_broadcast([P, 2 * QUAD, 64])

            def hops(t):
                dve.wait_ge(ph.degrees, t.u + 1)
                dve.wait_ge(ph.mixed, t.u + 1)
                if t.after(RING):
                    dve.wait_ge(ph.summed, t.u - RING + 1)
                both = ps[:, 2 + 2 * t.par:4 + 2 * t.par, 0:65 * QUAD].rearrange("p g (j c) -> p g j c", j=QUAD)
                for g in range(2):
                    last = dve.tensor_tensor(yy[:, t.slot, 0, :, 64 * g:64 * (g + 1)], both[:, g, :, 0:64],
                                             dg[:, t.slot, 2, :, g].unsqueeze(2).to_broadcast([P, QUAD, 64]),
                                             ALU.mult)
                last.then_inc(ph.scaled, 1)
                dve.tensor_tensor(tt[:, t.slot, 2].rearrange("p j g -> p g j"), both[:, :, :, 64],
                                  dg[:, t.slot, 2].rearrange("p j g -> p g j"), ALU.mult)\
                   .then_inc(ph.gate_chain, 1)

            def gate_arguments(t):
                dve.wait_ge(ph.gate_chain, t.u + 1)
                dve.tensor_tensor(tt[:, t.slot, 0], tt[:, t.slot, 2],
                                  cfc[:, :].unsqueeze(1).to_broadcast([P, QUAD, 2]), ALU.add).then_inc(ph.gate, 1)

            def gate_negative(t):
                dve.wait_ge(ph.clipped, t.u + 1)
                dve.wait_ge(ph.gate_open, t.u + 1)
                dve.scalar_tensor_tensor(out=halves(yy[:, t.slot, 1]), in0=halves(yy[:, t.slot, 1]), scalar=0.0,
                                         in1=each(tt[:, t.slot, 1]), op0=ALU.min, op1=ALU.mult)\
                   .then_inc(ph.joined, 1)

            if ph.turn == 1:
                in_step(dve, [(0, counts_high), (4, first_scale), (0, counts_parts), (3, first_statistics),
                              (4, first_shift), (3, first_moments)])
            elif ph.turn == 2:
                in_step(dve, [(4, first_scale), (0, counts_high), (7, residual), (4, first_shift), (0, counts_parts),
                              (8, last_scale), (3, first_statistics), (7, last_statistics), (3, first_moments),
                              (8, last_norm), (7, last_moments)])
            else:
                in_step(dve, [(7, last_statistics), (0, degree_floor), (5, gate_negative), (7, last_moments),
                              (0, degree_inverse), (2, hops), (9, last_scale), (2, gate_arguments), (0, degrees),
                              (9, last_norm)])

        def dense_pool(pool, ph):
            def bias(t):
                pool.wait_ge(ph.scaled, t.u + 1)
                own_wait(pool)
                pool.tensor_tensor(yy[:, t.slot, 1], yy[:, t.slot, 0],
                                   rows[:, 5, :].unsqueeze(1).to_broadcast([P, QUAD, D]),
                                   ALU.add).then_inc(ph.biased, 1)

            def add_x(t):
                pool.wait_ge(s_x[t.slot], ph.x_ready(t))
                own_wait(pool)
                pool.wait_ge(ph.clipped, t.u + 1)
                own_wait(pool)
                pool.tensor_tensor(yy[:, t.slot, 0], yy[:, t.slot, 0], xin[:, t.slot], ALU.add)\
                    .then_inc(ph.added, 1)

            def join(t):
                pool.wait_ge(ph.joined, t.u + 1)
                own_wait(pool)
                pool.wait_ge(ph.added, t.u + 1)
                own_wait(pool)
                if t.after(RING):
                    pool.wait_ge(ph.done, t.u - RING + 1)
                    own_wait(pool)
                pool.tensor_tensor(vout[:, t.slot], yy[:, t.slot, 0], yy[:, t.slot, 1], ALU.add)\
                    .then_inc(ph.summed, 1)

            in_step(pool, [(6, join), (3, bias), (5, add_x)])

        def late_constants(dve):
            for g in range(2):
                half = slice(64 * g, 64 * (g + 1))
                link(dve, dve.tensor_tensor_reduce(junk[:, 0:64], gates[:, g, 0:64], rows[:, 6, half], 1.0, 0.0,
                                                   ALU.mult, ALU.add, gates[:, g, 64:65]))
                link(dve, dve.tensor_tensor_reduce(junk[:, 0:64], rows[:, 5, half], rows[:, 6, half], 1.0, 0.0,
                                                   ALU.mult, ALU.add, cfc[:, g:g + 1]))
            link(dve, dve.tensor_tensor(cfc[:, :], cfc[:, :], bfs[:, :], ALU.add))
            link(dve, dve.tensor_reduce(of_part[:, 0:3], ident[0:CROWS, 0:CROWS - 3]
                                        .rearrange("p (a k j) -> p k a j", a=2, k=3), AX.XY, ALU.add))
            link(dve, dve.tensor_copy(of_part[:, 3:6], ident[0:CROWS, CROWS - 3:CROWS]))
            link(dve, dve.tensor_reduce(of_tile[:, :], ident[0:CROWS, 0:CROWS - 3]
                                        .rearrange("p (m j) -> p j m", j=QUAD), AX.X, ALU.add))

            for k, row in enumerate((6, 13, 4, 11, 15)):
                last = dve.tensor_copy(parts_f[:, k, :], ww[0:CROWS, row, :])
            link(dve, last)
            for k in range(3):
                link(dve, dve.tensor_copy(parts_b[:, k, :, :], parts_f[:, :, :]))
                if k < 2:
                    link(dve, dve.tensor_tensor(parts_f[:, :, :], parts_f[:, :, :], parts_b[:, k, :, :],
                                                ALU.subtract))

            def select(out, n, rows, column):
                for k in range(3):
                    if k == 0:
                        ins = dve.tensor_scalar(out, parts_b[0:n, k, rows, :], column(k), None, ALU.mult)
                    else:
                        ins = dve.scalar_tensor_tensor(out=out, in0=parts_b[0:n, k, rows, :], scalar=column(k),
                                                       in1=out, op0=ALU.mult, op1=ALU.add)
                    link(dve, ins)

            select(parts_f[:, 0:2, :], CROWS, slice(0, 2), lambda k: of_part[:, k:k + 1])
            select(parts_f[:, 2:4, :], CROWS, slice(2, 4), lambda k: of_part[:, 3 + k:4 + k])
            for j in range(QUAD):
                last = dve.scalar_tensor_tensor(out=bias27[:, :, j, :], in0=parts_f[:, 0:2, :],
                                                scalar=of_tile[:, j:j + 1], in1=parts_f[:, 2:4, :],
                                                op0=ALU.mult, op1=ALU.add)
            link(dve, last)
            select(parts_f[0:3, 4:5, :], 3, slice(4, 5), lambda k: ident[0:3, k:k + 1])
            link(dve, dve.tensor_copy(b3q[:, :, :], parts_f[0:3, 4, :].unsqueeze(1).to_broadcast([3, QUAD, D])))
            dve.sem_inc(s_late, 1)

        sort_keys = sem("resort_keys")
        sort_row = sem("resort_row")
        sort_used = sem("resort_used")
        sort_chain = sem("resort_chain")
        sort_staged = sem("resort_staged")
        sort_sent = sem("resort_sent")
        sort_moved = sem("resort_moved")
        falls = sb("falls", [P, 1])
        falls_i = sb("falls_i", [P, 1], I32)
        GROUPS = T // BATCH
        fraction, threshold, smaller, row_key = tmp2, tmp1, digit_f, scan[:, 0, 0:T]
        compared = run[:, :, :, :].rearrange("p a b c -> p (a b c)")[:, 0:BATCH * T]\
            .rearrange("p (j t) -> p j t", j=BATCH)

        def resort_vector(dve):
            dve.tensor_copy(keyf[:, :], raw[:, 1, :]).then_inc(sort_chain, 1)
            dve.tensor_scalar(fraction[:, :], digits_i[:, 0:T], 1.0 / DIGIT, None, ALU.mult).then_inc(sort_chain, 1)
            dve.memset(place[:, :], 0.0).then_inc(sort_chain, 1)
            dve.wait_ge(sort_chain, 3)
            dve.tensor_tensor(wcol[:, :], keyf[:, :], fraction[:, :], ALU.add).then_inc(sort_keys, 1)
            with dve.Fori(0, P) as q:
                dve.wait_ge(sort_row, q * 16 + 16)
                own_wait(dve)
                start = q * (2 * GROUPS + 3) + 3
                dve.scalar_tensor_tensor(out=threshold[:, :], in0=fraction[:, :], scalar=ident[:, bass.ds(q, 1)],
                                         in1=keyf[:, :], op0=ALU.mult, op1=ALU.add).then_inc(sort_chain, 1)
                dve.wait_ge(sort_chain, start + 1)
                dve.scalar_tensor_tensor(out=threshold[:, :], in0=ones[:, 0:1].to_broadcast([P, T]),
                                         scalar=upto[:, bass.ds(q, 1)], in1=threshold[:, :], op0=ALU.subtract,
                                         op1=ALU.add).then_inc(sort_chain, 1)
                dve.wait_ge(sort_chain, start + 2)
                for g in range(GROUPS):
                    dve.tensor_tensor(compared, row_key.unsqueeze(1).to_broadcast([P, BATCH, T]),
                                      threshold[:, g * BATCH:(g + 1) * BATCH].unsqueeze(2)
                                      .to_broadcast([P, BATCH, T]), ALU.is_lt).then_inc(sort_chain, 1)
                    dve.wait_ge(sort_chain, start + 2 * g + 3)
                    dve.tensor_reduce(smaller[:, g * BATCH:(g + 1) * BATCH], compared, AX.X, ALU.add)\
                       .then_inc(sort_chain, 1)
                    dve.wait_ge(sort_chain, start + 2 * g + 4)
                dve.sem_inc(sort_used, 1)
                dve.tensor_tensor(place[:, :], place[:, :], smaller[:, :], ALU.add).then_inc(sort_chain, 1)
                dve.wait_ge(sort_chain, start + 2 * GROUPS + 3)
            dve.tensor_copy(positions[:, :], place[:, :]).then_inc(sort_keys, 1)
            dve.wait_ge(sort_moved, 32)
            dve.tensor_copy(raw[:, 0, :], edges[:, :, 0]).then_inc(sort_keys, 1)
            dve.tensor_copy(raw[:, 1, :], edges[:, :, 3]).then_inc(sort_keys, 1)
            dve.tensor_scalar(raw_w[:, :], edges[:, :, 2], 1.0, None, ALU.mult).then_inc(sort_keys, 1)
            dve.wait_ge(sort_keys, 5)

        def resort_sync(sp):
            sp.wait_ge(sort_keys, 1)
            sp.dma_start(keys.rearrange("(p t) c -> p (t c)", t=T), wcol[:, :]).then_inc(sort_moved, 16)
            sp.wait_ge(sort_moved, 16)

            def row(q):
                sp.dma_start(row_key, keys[bass.ds(q * T, T), :].rearrange("t c -> c t").to_broadcast([P, T]))\
                  .then_inc(sort_row, 16)

            row(0)
            with sp.Fori(1, P) as q:
                sp.wait_ge(sort_used, q)
                own_wait(sp)
                row(q)
            sp.wait_ge(sort_sent, 16 * T)
            sp.dma_start(edges[:, :, :], by_low.rearrange("(p t) c -> p t c", t=T)).then_inc(sort_moved, 16)

        def resort_pool(pool):
            pool.wait_ge(sort_keys, 2)

            def batch(i, first):
                if not first:
                    pool.wait_ge(sort_sent, i * (16 * BATCH))
                    own_wait(pool)
                pool.tensor_copy(pos[:, 0, :], positions[:, bass.ds(i * BATCH, BATCH)]).then_inc(sort_staged, 1)
                pool.tensor_copy(load4[:, 0, :, :], edges[:, bass.ds(i * BATCH, BATCH), :]).then_inc(sort_staged, 1)
                pool.wait_ge(sort_staged, i * 2 + 2)
                own_wait(pool)
                for j in range(BATCH):
                    pool.indirect_dma_start(
                        by_low, bass.IndirectOffsetOnAxis(ap=pos[:, 0, j:j + 1], axis=0), load4[:, 0, j, :],
                        None, bounds_check=P * T - 1, oob_is_err=False).then_inc(sort_sent, 16)

            batch(0, True)
            with pool.Fori(1, GROUPS) as i:
                batch(i, False)

        def if_unsorted(eng, resort):
            eng.wait_ge(s_flag, 1)
            with eng.If(eng.value_load(falls_i[0:1, 0:1], min_val=0, max_val=P * T) > 0):
                resort(eng)

        zeros_b = sb("zeros_b", [P, 2 * DIGIT], BF16)

        e0 = EdgePhase(0, by_dst_set, msg_sum, [(x, 0, D), (x, 1, D)], 0, low_pass)
        e1 = EdgePhase(1, by_dst_set, msg_sum, [(n1_table, 0, D), (n1_table, 1, D)], 1, high_pass)
        e2 = EdgePhase(2, by_src_set, hop1, [(x1_table, 1, D)], None, None)
        e3 = EdgePhase(3, by_src_set, hop2, [(hop1, 1, W)], None, None, e2)

        block = ctx.enter_context(nc.Block())

        @block.sync
        def _(sp):
            sp.wait_ge(s_fill, 5)
            for t, s in ((raw[:, 0, :], src), (raw[:, 1, :], dst), (raw_w[:, :], edge_weight)):
                sp.dma_start(t[0:FULL, :], s[0:FULL * T].rearrange("(p t) -> p t", t=T)).then_inc(s_edge, 16)
                sp.dma_start(t[FULL:FULL + 1, 0:REST], s[FULL * T:E].rearrange("(a t) -> a t", a=1))\
                  .then_inc(s_edge, 16)
            sp.dma_start(positions[0:FULL, :], dst[1:FULL * T + 1].rearrange("(p t) -> p t", t=T))\
              .then_inc(s_edge, 16)
            sp.dma_start(positions[FULL:FULL + 1, 0:REST - 1],
                         dst[FULL * T + 1:E].rearrange("(a t) -> a t", a=1)).then_inc(s_edge, 16)
            n = 0
            for t, s in ((nat[:, 0, :], W_enc), (nat[:, 9, :], W_out),
                         (nat[:, 10:12, :], Wm2.rearrange("l o k -> o l k")),
                         (nat[:, 1:5, :].rearrange("p (l a) k -> p l (a k)", l=2), Wm1.rearrange("l o k -> o l k")),
                         (nat[:, 5:9, :].rearrange("p (l a) k -> p l (a k)", l=2), Wu.rearrange("l o k -> o l k")),
                         (gates[:, 0, 0:64], W0), (gates[:, 1, 0:64], W1),
                         (cols[:, 0:1], b_enc.rearrange("(p a) -> p a", a=1)),
                         (cols[:, 1:2], gamma[0, :].rearrange("(p a) -> p a", a=1)),
                         (cols[:, 2:3], gamma[1, :].rearrange("(p a) -> p a", a=1)),
                         (cols[:, 3:4], beta[0, :].rearrange("(p a) -> p a", a=1)),
                         (cols[:, 4:5], beta[1, :].rearrange("(p a) -> p a", a=1)),
                         (cols[:, 5:6], bm2[0, :].rearrange("(p a) -> p a", a=1)),
                         (cols[:, 6:7], bm2[1, :].rearrange("(p a) -> p a", a=1)),
                         (rows[:, 0, :], flat(bm1[0, :], D)), (rows[:, 1, :], flat(bm1[1, :], D)),
                         (rows[:, 2, :], flat(bu[0, :], D)), (rows[:, 3, :], flat(bu[1, :], D)),
                         (rows[:, 4, :], flat(b_out, D)),
                         (rows[:, 5, 0:64], flat(b0, 64)), (rows[:, 5, 64:D], flat(b1, 64)),
                         (rows[:, 6, 0:64], flat(fc0.rearrange("a b -> (a b)"), 64)),
                         (rows[:, 6, 64:D], flat(fc1.rearrange("a b -> (a b)"), 64)),
                         (bfs[:, 0:1], flat(bf0, 1)), (bfs[:, 1:2], flat(bf1, 1))):
                sp.dma_start(t, s).then_inc(s_load, 16)
                n += 1
            assert n == LOADS + 1
            def zero(tab, a, signal):
                sp.dma_start(tab.rearrange("(p a j) c -> p a (j c)", p=P, j=ZROWS)[:, a, :], zeros[:, :])\
                  .then_inc(signal, 16)

            for a in range(ZDMAS):
                zero(msg_sum, a, s_zero)
            if_unsorted(sp, resort_sync)
            for a in range(ZDMAS):
                sp.wait_ge(e0.summed, a * (2 * IT - 6) // ZDMAS + 2)
                zero(hop1, a, s_zero2)
                zero(hop2, a, s_zero2)
            edge_sync(sp, e0)
            dense_sync(sp, d1)
            sp.sem_inc(s_whole, 1)
            edge_sync(sp, e1)
            dense_sync(sp, d2)
            sp.sem_inc(s_whole, 1)
            edge_sync(sp, e2)
            sp.sem_inc(s_whole, 1)
            edge_sync(sp, e3)
            dense_sync(sp, d3)

        @block.gpsimd
        def _(pool):
            pool.memset(ident[:, :], 0.0).then_inc(s_const, 1)
            pool.memset(ones[:, :], 1.0).then_inc(s_const, 1)
            pool.wait_ge(s_const, 2)
            pool.iota(digits_i[:, :], pattern=[[1, DIGIT]], base=0, channel_multiplier=0).then_inc(s_const, 1)
            pool.iota(part_i[:, :], pattern=[[1, 1]], base=0, channel_multiplier=1).then_inc(s_const, 1)
            pool.affine_select(out=ident[:, :], in_=ident[:, :], compare_op=ALU.not_equal, fill=1.0,
                               base=0, pattern=[[-1, P]], channel_multiplier=1).then_inc(s_const, 1)
            pool.affine_select(out=before[:, :], in_=ones[:, :], compare_op=ALU.is_gt, fill=0.0,
                               base=0, pattern=[[1, P]], channel_multiplier=-1).then_inc(s_const, 1)
            pool.affine_select(out=upto[:, :], in_=ones[:, :], compare_op=ALU.is_ge, fill=0.0,
                               base=0, pattern=[[1, P]], channel_multiplier=-1).then_inc(s_const, 1)
            if_unsorted(pool, resort_pool)
            edge_pool(pool, e0)
            sort_pool(pool, low_pass, by_low)
            sort_load(pool, low_pass, by_low)
            pool.wait_ge(s_whole, 1)
            edge_pool(pool, e1)
            sort_pool(pool, high_pass, by_src)
            sort_load(pool, high_pass, by_src)
            pool.wait_ge(s_whole, 2)
            pool.wait_ge(s_zero2, 16 * 2 * ZDMAS)
            edge_pool(pool, e2)
            pool.wait_ge(s_whole, 3)
            edge_pool(pool, e3)
            dense_pool(pool, d3)

        @block.scalar
        def _(act):
            act.wait_ge(s_wt, 1)
            act.activation(wT[:, :, :], ps[:, 0:3, :].rearrange("p b n -> p (b n)")[:, 0:9 * D]
                           .rearrange("p (k n) -> p k n", k=9), ACT.Copy).then_inc(s_wte, 1)
            act.wait_ge(s_wm, 1)
            act.activation(ww[:, :, :], ps[:, 4:8, :].rearrange("p b n -> p (b n)")
                           .rearrange("p (k n) -> p k n", k=16), ACT.Copy).then_inc(s_wme, 1)
            edge_scalar(act, e0)
            dense_scalar(act, d1)
            edge_scalar(act, e1)
            dense_scalar(act, d2)
            edge_scalar(act, e2)
            edge_scalar(act, e3)
            dense_scalar(act, d3)

        @block.tensor
        def _(pe):
            pe.wait_ge(s_const, 2)
            pe.wait_ge(s_falls, 1)
            pe.matmul(ps[:, 6, 0:1], ones[:, :], falls[:, :], start=True, stop=True).then_inc(s_fallen, 1)
            pe.wait_ge(s_load, 16 * (LOADS + 1))
            pe.wait_ge(s_const, 7)
            for k in range(9):
                last = pe.transpose(ps[:, k // 4, (k % 4) * P:(k % 4 + 1) * P], nat[:, 1 + k, :], ident[:, :])
            last.then_inc(s_wt, 1)
            pe.wait_ge(s_wte, 1)
            pe.wait_ge(s_wd, 1)

            def product(k, pairs):
                for m, (a, b) in enumerate(pairs):
                    last = pe.matmul(ps[:, 4 + k // 4, (k % 4) * P:(k % 4 + 1) * P], a, b,
                                     start=(m == 0), stop=(m == len(pairs) - 1))
                return last

            for l in range(2):
                front = nat[:, 0, :] if l == 0 else scaleL[:, 0, :]
                shift = colsB[:, l, :]
                wa, wb, ua, u = wT[:, 2 * l, :], wT[:, 2 * l + 1, :], wT[:, 5 + 2 * l, :], resid[:, l, :]
                product(7 * l + 0, [(front, wa)])
                product(7 * l + 1, [(front, wb)])
                product(7 * l + 2, [(shift, wa), (shift, wb)])
                product(7 * l + 3, [(front, u)])
                product(7 * l + 4, [(shift, u)])
                product(7 * l + 5, [(nat[:, 10 + l, :], ua)])
                product(7 * l + 6, [(colsB[:, 3 + l, :], ua)])
            product(14, [(scaleL[:, 1, :], wT[:, 8, :])])
            product(15, [(colsB[:, 2, :], wT[:, 8, :])]).then_inc(s_wm, 1)
            pe.wait_ge(s_wdone, 1)
            prep_tensor(pe, by_dst_set, 0)
            edge_tensor(pe, e0)
            pe.wait_ge(s_late, 1)
            dense_tensor(pe, d1)
            edge_tensor(pe, e1)
            dense_tensor(pe, d2)
            prep_tensor(pe, by_src_set, 1)
            edge_tensor(pe, e2)
            edge_tensor(pe, e3)
            dense_tensor(pe, d3)

        @block.vector
        def _(dve):
            dve.memset(zeros[:, :], 0.0).then_inc(s_fill, 1)
            dve.memset(raw[:, 0, :], N).then_inc(s_fill, 1)
            dve.memset(raw[:, 1, :], N).then_inc(s_fill, 1)
            dve.memset(raw_w[:, :], 0.0).then_inc(s_fill, 1)
            dve.memset(positions[:, :], N).then_inc(s_fill, 1)
            dve.wait_ge(s_edge, 16 * 8)
            link(dve, dve.tensor_tensor(tmp1[:, :], raw[:, 1, :], positions[:, :], ALU.is_gt))
            dve.tensor_reduce(falls[:, :], tmp1[:, :], AX.X, ALU.add).then_inc(s_falls, 1)
            link(dve, dve.tensor_copy(edges[:, :, 3], raw[:, 1, :]))
            link(dve, dve.tensor_copy(edges[:, :, 0], raw[:, 0, :]))
            link(dve, dve.tensor_scalar(edges[:, :, 1], raw[:, 1, :], float(N - 1), None, ALU.min))
            link(dve, dve.tensor_copy(edges[:, :, 2], raw_w[:, :]))
            dve.wait_ge(s_fallen, 1)
            dve.tensor_copy(falls_i[:, :], ps[:, 6, 0:1]).then_inc(s_flag, 1)
            dve.wait_ge(s_const, 7)
            if_unsorted(dve, resort_vector)
            link(dve, dve.tensor_scalar(edges[:, :, 1], raw[:, 1, :], float(N - 1), None, ALU.min))
            for k in range(2):
                link(dve, dve.tensor_scalar(by_dst_set.gat[:, k, :], raw[:, k, :], float(N - 1), None, ALU.min))
            stage_first(dve, e0)
            dve.memset(eps[:, :], EPS)
            dve.memset(zeros_b[:, :], 0.0)
            dve.memset(cntT[:, :, :], 1.0)
            dve.wait_ge(s_const, 7)
            dve.tensor_copy(ident_b[:, :], ident[:, :])
            dve.tensor_copy(ones_b[:, :], ones[:, :])
            dve.tensor_copy(before_b[:, :], before[:, :])
            link(dve, dve.tensor_tensor(notbefore_b[:, :], ones[:, :], before[:, :], ALU.subtract))
            dve.tensor_copy(digits_b[:, :], digits_i[:, :])
            dve.tensor_scalar(head_row[:, :], part_i[:, :], float(HEAD), None, ALU.add)
            link(dve, dve.tensor_scalar(tail_row[:, :], part_i[:, :], float(TAIL), None, ALU.add))
            dve.wait_ge(s_load, 16 * (LOADS + 1))
            for k, c in enumerate((0, 3, 4, 5, 6)):
                dve.tensor_scalar(colsB[:, k, :], ones[:, :], cols[:, c:c + 1], None, ALU.mult)
            for k in range(2):
                dve.tensor_scalar(scaleL[:, k, :], ident[:, :], cols[:, 1 + k:2 + k], None, ALU.mult)
            dve.wait_ge(s_wte, 1)
            for l in range(2):
                last = dve.tensor_tensor(resid[:, l, :], ident[:, :], wT[:, 4 + 2 * l, :], ALU.add)
            last.then_inc(s_wd, 1)
            dve.wait_ge(s_wme, 1)
            for k, r in ((2, 0), (9, 1), (4, 2), (11, 3), (15, 4)):
                link(dve, dve.tensor_tensor(ww[:, k, :], ww[:, k, :], rows[:, r, :], ALU.add))
            dve.sem_inc(s_wdone, 1)
            link(dve, dve.tensor_copy(keyf[:, :], raw[:, 1, :]))
            prep_vector(dve, by_dst_set, 0)
            digits(dve, digit_f, 0)
            edge_vector(dve, e0)
            dense_vector(dve, d1)
            stage_first(dve, e1)
            dve.wait_ge(low_pass.loaded, 16)
            digits(dve, digit_f, 8)
            edge_vector(dve, e1)
            dense_vector(dve, d2)
            dve.wait_ge(high_pass.loaded, 16)
            link(dve, dve.tensor_copy(by_src_set.gat[:, 1, :], edges[:, :, 1]))
            link(dve, dve.tensor_copy(wcol[:, :], edges[:, :, 2]))
            stage_first(dve, e2)
            link(dve, dve.tensor_copy(keyf[:, :], edges[:, :, 0]))
            prep_vector(dve, by_src_set, 1)
            edge_vector(dve, e2)
            stage_first(dve, e3)
            edge_vector(dve, e3)
            dense_vector(dve, d3)


_INS = ["x", "src", "dst", "edge_weight", "L0_gnn_W_enc", "L0_gnn_b_enc", "L0_gnn_Wm1", "L0_gnn_bm1",
        "L0_gnn_Wm2", "L0_gnn_bm2", "L0_gnn_Wu", "L0_gnn_bu", "L0_gnn_gamma", "L0_gnn_beta", "L0_gnn_W_out",
        "L0_gnn_b_out", "L1_gnn_W0", "L1_gnn_b0", "L1_gnn_W1", "L1_gnn_b1", "L1_gnn_fc0", "L1_gnn_bf0",
        "L1_gnn_fc1", "L1_gnn_bf1"]
_OUTS = [((50000, 128), "float32")]


def kernel(**inputs):
    import numpy as _np
    import concourse.bacc as _bacc
    from concourse import mybir as _mybir
    from concourse.bass_utils import run_bass_kernel_spmd as _run

    nc = _bacc.Bacc("TRN2", target_bir_lowering=False, num_devices=1)
    arrays, args = {}, []
    for name in _INS:
        a = _np.ascontiguousarray(inputs[name])
        arrays[f"in_{name}_dram"] = a
        args.append(nc.dram_tensor(f"in_{name}_dram", a.shape, _mybir.dt.from_np(a.dtype), kind="ExternalInput").ap())
    for i, (shape, dtype) in enumerate(_OUTS):
        dt = _mybir.dt.from_np(_np.dtype(dtype))
        args.append(nc.dram_tensor(f"out_{i}_dram", shape, dt, kind="ExternalOutput").ap())
    graph_kernel(nc, *args)
    r = _run(nc, [arrays], core_ids=[0])
    got = tuple(r.results[0][f"out_{i}_dram"] for i in range(len(_OUTS)))
    return got[0]
```
